# Optimizing a Trainium2 kernel written in Bass

```python
import numpy as np
import jax
import jax.numpy as jnp

def _softmax(x, axis=-1):
    return jax.nn.softmax(x, axis=axis)

def _gelu(x):
    return jax.nn.gelu(x, approximate=True)

def _silu(x):
    return jax.nn.silu(x)

def _sigmoid(x):
    return jax.nn.sigmoid(x)

def _layernorm(x, axis=-1, eps=1e-05):
    m = jnp.mean(x, axis=axis, keepdims=True)
    v = jnp.var(x, axis=axis, keepdims=True)
    return (x - m) / jnp.sqrt(v + eps)

def _scatter_add(tgt, idx, src, axis=0):
    return tgt.at[idx].add(src)

def _segment_sum(src, seg, n):
    return jax.ops.segment_sum(src, seg, n)
kernel_name = 'mk_perceiver_d2_seqx_r4_0c5ecc'

def setup_inputs(seed: int=0):
    np.random.seed(seed)
    _w = jnp.asarray

    def _rec_inputs():
        import jax
        import jax.numpy as jnp
        _rk = jax.random.key(seed)
        x = -0.000125 + 0.9999 * jax.random.normal(jax.random.fold_in(_rk, 1), (16, 64, 256), jnp.float32)
        _lenS = 64 - jax.random.randint(jax.random.fold_in(_rk, 7), (16,), 0, max(1, 64 // 4) + 1, jnp.int32)
        _lenS2 = 1601 - jax.random.randint(jax.random.fold_in(_rk, 8), (16,), 0, max(1, 1601 // 4) + 1, jnp.int32)
        _ctx_768P = jax.random.normal(jax.random.fold_in(_rk, 11), (16, 16, 192), jnp.float32)
        _ctx_768c = jax.random.dirichlet(jax.random.fold_in(_rk, 511), 0.3 * jnp.ones((16,), jnp.float32), (16, 1601))
        _ctx_768t = jnp.einsum('bsk,bkd->bsd', _ctx_768c, _ctx_768P)
        _ctx_768t = _ctx_768t * jax.lax.rsqrt(jnp.mean(jnp.square(_ctx_768t)) + 1e-12) * 0.953939
        ctx_768 = 0.00272024 + 0.999456 * (_ctx_768t + 0.3 * jax.random.normal(jax.random.fold_in(_rk, 611), (16, 1601, 192), jnp.float32))
        return (x, ctx_768)
    x, ctx_768 = _rec_inputs()

    def _L0_xattn_setup():
        import jax, jax.numpy as jnp
        import numpy as np
        N_HEADS = 16
        D_EMBED = 256
        D_CROSS = 192
        D_HEAD = D_EMBED // N_HEADS
        key = jax.random.key(seed)
        ks = jax.random.split(key, 10)
        B, SQ, SKV = (8, 1024, 77)
        s_e = 1.0 / np.sqrt(D_EMBED)
        s_c = 1.0 / np.sqrt(D_CROSS)
        return {'x': jax.random.normal(ks[0], (B, SQ, D_EMBED), jnp.float32), 'y': jax.random.normal(ks[1], (B, SKV, D_CROSS), jnp.float32), 'wq': jax.random.normal(ks[2], (D_EMBED, D_EMBED), jnp.float32) * s_e, 'bq': jnp.zeros((D_EMBED,), jnp.float32), 'wk': jax.random.normal(ks[3], (D_CROSS, D_EMBED), jnp.float32) * s_c, 'bk': jnp.zeros((D_EMBED,), jnp.float32), 'wv': jax.random.normal(ks[4], (D_CROSS, D_EMBED), jnp.float32) * s_c, 'bv': jnp.zeros((D_EMBED,), jnp.float32), 'wo': jax.random.normal(ks[5], (D_EMBED, D_EMBED), jnp.float32) * s_e, 'bo': jnp.zeros((D_EMBED,), jnp.float32)}
    _L0_xattn_all = _L0_xattn_setup()
    _L0_xattn_in = {k: v for k, v in _L0_xattn_all.items() if k in ('wq', 'bq', 'wk', 'bk', 'wv', 'bv', 'wo', 'bo')}
    del _L0_xattn_all

    def _L0_attn_setup():
        import jax, jax.numpy as jnp
        import numpy as np
        B, N, D = (2, 512, 256)
        H, QH, DH = (8, 16, 64)
        SOFTCLAMP = 50.0

        def _rmsnorm(x, w):
            eps = jnp.finfo(x.dtype).eps
            return x * jax.lax.rsqrt(jnp.mean(x * x, axis=-1, keepdims=True) + eps) * w

        def _l2norm(x):
            n = jnp.maximum(jnp.linalg.norm(x, axis=-1, keepdims=True), 1e-12)
            return x / n

        def _mh_rmsnorm(x, gamma):
            scale = (gamma + 1.0) * np.sqrt(x.shape[-1]).astype(np.float32)
            return _l2norm(x) * scale[None, :, None, :]
        key = jax.random.key(seed)
        ks = jax.random.split(key, 7)
        return {'tokens': jax.random.normal(ks[0], (B, N, D), jnp.float32), 'norm_w': jnp.ones((D,), jnp.float32) + 0.02 * jax.random.normal(ks[1], (D,), jnp.float32), 'Wq': 0.02 * jax.random.normal(ks[2], (D, QH * DH), jnp.float32), 'Wkv': 0.02 * jax.random.normal(ks[3], (D, 2 * H * DH), jnp.float32), 'Wout': 0.02 * jax.random.normal(ks[4], (H * DH, D), jnp.float32), 'q_gamma': 0.02 * jax.random.normal(ks[5], (QH, DH), jnp.float32), 'k_gamma': 0.02 * jax.random.normal(ks[6], (H, DH), jnp.float32)}
    _L0_attn_all = _L0_attn_setup()
    _L0_attn_in = {k: v for k, v in _L0_attn_all.items() if k in ('norm_w', 'Wq', 'Wkv', 'Wout', 'q_gamma', 'k_gamma')}
    del _L0_attn_all

    def _L0_ffn_setup():
        import jax, jax.numpy as jnp
        import numpy as np
        N_EMBD = 256
        N_STATE = 1024
        key = jax.random.key(seed)
        k_x, k_w1, k_b1, k_w2, k_b2 = jax.random.split(key, 5)
        x = jax.random.normal(k_x, (4, 512, N_EMBD), dtype=jnp.float32)
        w1 = jax.random.normal(k_w1, (N_EMBD, N_STATE), dtype=jnp.float32) * (1.0 / np.sqrt(N_EMBD))
        b1 = jax.random.normal(k_b1, (N_STATE,), dtype=jnp.float32) * 0.02
        w2 = jax.random.normal(k_w2, (N_STATE, N_EMBD), dtype=jnp.float32) * (1.0 / np.sqrt(N_STATE))
        b2 = jax.random.normal(k_b2, (N_EMBD,), dtype=jnp.float32) * 0.02
        return {'x': x, 'w1': w1, 'b1': b1, 'w2': w2, 'b2': b2}
    _L0_ffn_all = _L0_ffn_setup()
    _L0_ffn_in = {k: v for k, v in _L0_ffn_all.items() if k in ('w1', 'b1', 'w2', 'b2')}
    del _L0_ffn_all

    def _L1_xattn_setup():
        import jax, jax.numpy as jnp
        import numpy as np
        HEADS = 8
        DIM_HEAD = 64
        QUERY_DIM = 256
        CONTEXT_DIM = 192
        INNER = HEADS * DIM_HEAD
        key = jax.random.key(seed)
        ks = jax.random.split(key, 7)
        B, Sq, Skv = (4, 1024, 256)
        x = jax.random.normal(ks[0], (B, Sq, QUERY_DIM), dtype=jnp.float32)
        context = jax.random.normal(ks[1], (B, Skv, CONTEXT_DIM), dtype=jnp.float32)
        Wq = jax.random.normal(ks[2], (QUERY_DIM, INNER), dtype=jnp.float32) * QUERY_DIM ** (-0.5)
        Wk = jax.random.normal(ks[3], (CONTEXT_DIM, INNER), dtype=jnp.float32) * CONTEXT_DIM ** (-0.5)
        Wv = jax.random.normal(ks[4], (CONTEXT_DIM, INNER), dtype=jnp.float32) * CONTEXT_DIM ** (-0.5)
        Wo = jax.random.normal(ks[5], (INNER, QUERY_DIM), dtype=jnp.float32) * INNER ** (-0.5)
        bo = jax.random.normal(ks[6], (QUERY_DIM,), dtype=jnp.float32) * 0.01
        return {'x': x, 'context': context, 'Wq': Wq, 'Wk': Wk, 'Wv': Wv, 'Wo': Wo, 'bo': bo}
    _L1_xattn_all = _L1_xattn_setup()
    _L1_xattn_in = {k: v for k, v in _L1_xattn_all.items() if k in ('Wq', 'Wk', 'Wv', 'Wo', 'bo')}
    del _L1_xattn_all

    def _L1_attn_setup():
        import jax, jax.numpy as jnp
        import numpy as np
        T, N, D, H = (128, 64, 256, 256)
        LR = 0.001

        def _recon(params, z):
            W1, b1, W2, b2 = params
            h = jax.nn.gelu(z @ W1.T + b1, approximate=False)
            return z + h @ W2.T + b2
        key = jax.random.key(seed)
        ks = jax.random.split(key, 6)
        sd = 1.0 / np.sqrt(D)
        sh = 1.0 / np.sqrt(H)
        s4 = 1.0 / np.sqrt(H // 4)
        return {'in_seq': jax.random.normal(ks[0], (T, N, D), jnp.float32), 't_k': jax.random.normal(ks[1], (H, D), jnp.float32) * sd, 't_v': jax.random.normal(ks[2], (H, D), jnp.float32) * sd, 't_q': jax.random.normal(ks[3], (H, D), jnp.float32) * sd, 'W1': jax.random.normal(ks[4], (H // 4, H), jnp.float32) * sh, 'b1': jnp.zeros((H // 4,), jnp.float32), 'W2': jax.random.normal(ks[5], (H, H // 4), jnp.float32) * s4, 'b2': jnp.zeros((H,), jnp.float32)}
    _L1_attn_all = _L1_attn_setup()
    _L1_attn_in = {k: v for k, v in _L1_attn_all.items() if k in ('t_k', 't_v', 't_q', 'W1', 'b1', 'W2', 'b2')}
    del _L1_attn_all

    def _L1_ffn_setup():
        import jax, jax.numpy as jnp
        import numpy as np
        LN_EPS = 1e-05

        def _swiglu(h, w_gate_up, w_down):
            gu = h @ w_gate_up.T
            gate, up = jnp.split(gu, 2, axis=-1)
            return jax.nn.silu(gate) * up @ w_down.T
        key = jax.random.key(seed)
        ks = jax.random.split(key, 6)
        d_model, d_ff, E = (256, 1024, 8)
        shared_d_ff = d_ff // 4
        routed_d_ff = d_ff - shared_d_ff
        B, S = (4, 512)
        x = jax.random.normal(ks[0], (B, S, d_model), dtype=jnp.float32)
        ln_gamma = jnp.ones((d_model,), jnp.float32)
        ln_beta = jnp.zeros((d_model,), jnp.float32)
        router_w = jax.random.normal(ks[1], (E, d_model), jnp.float32) * 0.02
        gate_up_w = jax.random.normal(ks[2], (E, 2 * routed_d_ff, d_model), jnp.float32) * (1.0 / np.sqrt(d_model))
        down_w = jax.random.normal(ks[3], (E, d_model, routed_d_ff), jnp.float32) * (1.0 / np.sqrt(routed_d_ff))
        shared_gate_up_w = jax.random.normal(ks[4], (2 * shared_d_ff, d_model), jnp.float32) * (1.0 / np.sqrt(d_model))
        shared_down_w = jax.random.normal(ks[5], (d_model, shared_d_ff), jnp.float32) * (1.0 / np.sqrt(shared_d_ff))
        return dict(x=x, ln_gamma=ln_gamma, ln_beta=ln_beta, router_w=router_w, gate_up_w=gate_up_w, down_w=down_w, shared_gate_up_w=shared_gate_up_w, shared_down_w=shared_down_w)
    _L1_ffn_all = _L1_ffn_setup()
    _L1_ffn_in = {k: v for k, v in _L1_ffn_all.items() if k in ('ln_gamma', 'ln_beta', 'router_w', 'gate_up_w', 'down_w', 'shared_gate_up_w', 'shared_down_w')}
    del _L1_ffn_all
    return {'x': x, 'ctx_768': ctx_768, 'L0_xattn_wq': _L0_xattn_in['wq'], 'L0_xattn_bq': _L0_xattn_in['bq'], 'L0_xattn_wk': _L0_xattn_in['wk'], 'L0_xattn_bk': _L0_xattn_in['bk'], 'L0_xattn_wv': _L0_xattn_in['wv'], 'L0_xattn_bv': _L0_xattn_in['bv'], 'L0_xattn_wo': _L0_xattn_in['wo'], 'L0_xattn_bo': _L0_xattn_in['bo'], 'L0_attn_norm_w': _L0_attn_in['norm_w'], 'L0_attn_Wq': _L0_attn_in['Wq'], 'L0_attn_Wkv': _L0_attn_in['Wkv'], 'L0_attn_Wout': _L0_attn_in['Wout'], 'L0_attn_q_gamma': _L0_attn_in['q_gamma'], 'L0_attn_k_gamma': _L0_attn_in['k_gamma'], 'L0_ffn_w1': _L0_ffn_in['w1'], 'L0_ffn_b1': _L0_ffn_in['b1'], 'L0_ffn_w2': _L0_ffn_in['w2'], 'L0_ffn_b2': _L0_ffn_in['b2'], 'L1_xattn_Wq': _L1_xattn_in['Wq'], 'L1_xattn_Wk': _L1_xattn_in['Wk'], 'L1_xattn_Wv': _L1_xattn_in['Wv'], 'L1_xattn_Wo': _L1_xattn_in['Wo'], 'L1_xattn_bo': _L1_xattn_in['bo'], 'L1_attn_t_k': _L1_attn_in['t_k'], 'L1_attn_t_v': _L1_attn_in['t_v'], 'L1_attn_t_q': _L1_attn_in['t_q'], 'L1_attn_W1': _L1_attn_in['W1'], 'L1_attn_b1': _L1_attn_in['b1'], 'L1_attn_W2': _L1_attn_in['W2'], 'L1_attn_b2': _L1_attn_in['b2'], 'L1_ffn_ln_gamma': _L1_ffn_in['ln_gamma'], 'L1_ffn_ln_beta': _L1_ffn_in['ln_beta'], 'L1_ffn_router_w': _L1_ffn_in['router_w'], 'L1_ffn_gate_up_w': _L1_ffn_in['gate_up_w'], 'L1_ffn_down_w': _L1_ffn_in['down_w'], 'L1_ffn_shared_gate_up_w': _L1_ffn_in['shared_gate_up_w'], 'L1_ffn_shared_down_w': _L1_ffn_in['shared_down_w']}

def reference(x, ctx_768, L0_xattn_wq, L0_xattn_bq, L0_xattn_wk, L0_xattn_bk, L0_xattn_wv, L0_xattn_bv, L0_xattn_wo, L0_xattn_bo, L0_attn_norm_w, L0_attn_Wq, L0_attn_Wkv, L0_attn_Wout, L0_attn_q_gamma, L0_attn_k_gamma, L0_ffn_w1, L0_ffn_b1, L0_ffn_w2, L0_ffn_b2, L1_xattn_Wq, L1_xattn_Wk, L1_xattn_Wv, L1_xattn_Wo, L1_xattn_bo, L1_attn_t_k, L1_attn_t_v, L1_attn_t_q, L1_attn_W1, L1_attn_b1, L1_attn_W2, L1_attn_b2, L1_ffn_ln_gamma, L1_ffn_ln_beta, L1_ffn_router_w, L1_ffn_gate_up_w, L1_ffn_down_w, L1_ffn_shared_gate_up_w, L1_ffn_shared_down_w):
    import jax
    import jax.numpy as jnp

    def _L0_xattn_ref(x, y, wq, bq, wk, bk, wv, bv, wo, bo):
        import jax, jax.numpy as jnp
        import numpy as np
        N_HEADS = 16
        D_EMBED = 256
        D_CROSS = 192
        D_HEAD = D_EMBED // N_HEADS
        B, SQ, _ = x.shape
        SKV = y.shape[1]
        q = (x @ wq + bq).reshape(B, SQ, N_HEADS, D_HEAD)
        k = (y @ wk + bk).reshape(B, SKV, N_HEADS, D_HEAD)
        v = (y @ wv + bv).reshape(B, SKV, N_HEADS, D_HEAD)
        scores = jnp.einsum('bqhd,bkhd->bhqk', q, k) / jnp.sqrt(jnp.asarray(D_HEAD, x.dtype))
        attn = jax.nn.softmax(scores, axis=-1)
        out = jnp.einsum('bhqk,bkhd->bqhd', attn, v).reshape(B, SQ, D_EMBED)
        return out @ wo + bo

    def _L0_attn_ref(tokens, norm_w, Wq, Wkv, Wout, q_gamma, k_gamma):
        import jax, jax.numpy as jnp
        import numpy as np
        B, N, D = (2, 512, 256)
        H, QH, DH = (8, 16, 64)
        SOFTCLAMP = 50.0

        def _rmsnorm(x, w):
            eps = jnp.finfo(x.dtype).eps
            return x * jax.lax.rsqrt(jnp.mean(x * x, axis=-1, keepdims=True) + eps) * w

        def _l2norm(x):
            n = jnp.maximum(jnp.linalg.norm(x, axis=-1, keepdims=True), 1e-12)
            return x / n

        def _mh_rmsnorm(x, gamma):
            scale = (gamma + 1.0) * np.sqrt(x.shape[-1]).astype(np.float32)
            return _l2norm(x) * scale[None, :, None, :]
        b, n, d = tokens.shape
        x = _rmsnorm(tokens, norm_w)
        q = (x @ Wq).reshape(b, n, QH, DH).transpose(0, 2, 1, 3)
        kv = x @ Wkv
        k = kv[..., :H * DH].reshape(b, n, H, DH).transpose(0, 2, 1, 3)
        v = kv[..., H * DH:].reshape(b, n, H, DH).transpose(0, 2, 1, 3)
        q = _mh_rmsnorm(q, q_gamma)
        k = _mh_rmsnorm(k, k_gamma)
        g = QH // H
        q = q.reshape(b, H, g, n, DH)
        sim = jnp.einsum('bhgid,bhjd->bhgij', q, k)
        sim = jnp.tanh(sim / SOFTCLAMP) * SOFTCLAMP
        sim = sim * DH ** (-0.5)
        neg = -jnp.finfo(sim.dtype).max
        causal = jnp.triu(jnp.ones((n, n), dtype=bool), 1)
        sim = jnp.where(causal, neg, sim)
        attn = jax.nn.softmax(sim, axis=-1)
        out = jnp.einsum('bhgij,bhjd->bhid', attn, v)
        out = out.transpose(0, 2, 1, 3).reshape(b, n, H * DH)
        return out @ Wout

    def _L0_ffn_ref(x, w1, b1, w2, b2):
        import jax, jax.numpy as jnp
        import numpy as np
        N_EMBD = 256
        N_STATE = 1024
        h = jax.nn.gelu(jnp.einsum('bse,eh->bsh', x, w1) + b1, approximate=False)
        return jnp.einsum('bsh,he->bse', h, w2) + b2

    def _L1_xattn_ref(x, context, Wq, Wk, Wv, Wo, bo):
        import jax, jax.numpy as jnp
        import numpy as np
        HEADS = 8
        DIM_HEAD = 64
        QUERY_DIM = 256
        CONTEXT_DIM = 192
        INNER = HEADS * DIM_HEAD
        B, Sq, _ = x.shape
        h, d = (HEADS, DIM_HEAD)
        scale = d ** (-0.5)
        q = (x @ Wq).reshape(B, Sq, h, d).transpose(0, 2, 1, 3)
        k = (context @ Wk).reshape(B, -1, h, d).transpose(0, 2, 1, 3)
        v = (context @ Wv).reshape(B, -1, h, d).transpose(0, 2, 1, 3)
        scores = jnp.einsum('bhid,bhjd->bhij', q, k) * scale
        attn = jax.nn.softmax(scores, axis=-1)
        out = jnp.einsum('bhij,bhjd->bhid', attn, v)
        out = out.transpose(0, 2, 1, 3).reshape(B, Sq, h * d)
        return out @ Wo + bo

    def _L1_attn_ref(in_seq, t_k, t_v, t_q, W1, b1, W2, b2):
        import jax, jax.numpy as jnp
        import numpy as np
        T, N, D, H = (128, 64, 256, 256)
        LR = 0.001

        def _recon(params, z):
            W1, b1, W2, b2 = params
            h = jax.nn.gelu(z @ W1.T + b1, approximate=False)
            return z + h @ W2.T + b2

        def loss_fn(params, z, y):
            return jnp.mean((_recon(params, z) - y) ** 2)

        def step(params, x):
            z = x @ t_k.T
            y = x @ t_v.T
            grads = jax.grad(loss_fn)(params, z, y)
            new_params = jax.tree_util.tree_map(lambda p, g: jax.lax.stop_gradient(p - LR * g), params, grads)
            out = _recon(new_params, x @ t_q.T)
            return (new_params, out)
        _, outs = jax.lax.scan(step, (W1, b1, W2, b2), in_seq)
        return outs

    def _L1_ffn_ref(x, ln_gamma, ln_beta, router_w, gate_up_w, down_w, shared_gate_up_w, shared_down_w):
        import jax, jax.numpy as jnp
        import numpy as np
        LN_EPS = 1e-05

        def _swiglu(h, w_gate_up, w_down):
            gu = h @ w_gate_up.T
            gate, up = jnp.split(gu, 2, axis=-1)
            return jax.nn.silu(gate) * up @ w_down.T
        B, S, D = x.shape
        E = router_w.shape[0]
        top_k = 2
        xt = x.reshape(-1, D)
        mu = jnp.mean(xt, axis=-1, keepdims=True)
        var = jnp.mean(jnp.square(xt - mu), axis=-1, keepdims=True)
        normed = (xt - mu) * jax.lax.rsqrt(var + LN_EPS) * ln_gamma + ln_beta
        logits = normed.astype(jnp.float32) @ router_w.T
        probs = jax.nn.softmax(logits, axis=-1)
        top_v, top_i = jax.lax.top_k(probs, top_k)
        gates = jax.nn.softmax(top_v, axis=-1)
        comb = jnp.sum(jax.nn.one_hot(top_i, E, dtype=gates.dtype) * gates[..., None], axis=1)
        out = jnp.zeros_like(normed)
        for e in range(E):
            y = _swiglu(normed, gate_up_w[e], down_w[e])
            out = out + comb[:, e, None] * y
        out = out + _swiglu(normed, shared_gate_up_w, shared_down_w)
        return out.reshape(B, S, D)
    x = x + _L0_xattn_ref(_layernorm(x, axis=-1), ctx_768, L0_xattn_wq, L0_xattn_bq, L0_xattn_wk, L0_xattn_bk, L0_xattn_wv, L0_xattn_bv, L0_xattn_wo, L0_xattn_bo)
    x = x + _L0_attn_ref(_layernorm(x, axis=-1), L0_attn_norm_w, L0_attn_Wq, L0_attn_Wkv, L0_attn_Wout, L0_attn_q_gamma, L0_attn_k_gamma)
    x = x + _L0_ffn_ref(_layernorm(x, axis=-1), L0_ffn_w1, L0_ffn_b1, L0_ffn_w2, L0_ffn_b2)
    x = x + _L1_xattn_ref(_layernorm(x, axis=-1), ctx_768, L1_xattn_Wq, L1_xattn_Wk, L1_xattn_Wv, L1_xattn_Wo, L1_xattn_bo)
    x = x + _L1_attn_ref(_layernorm(x, axis=-1), L1_attn_t_k, L1_attn_t_v, L1_attn_t_q, L1_attn_W1, L1_attn_b1, L1_attn_W2, L1_attn_b2)
    x = x + _L1_ffn_ref(_layernorm(x, axis=-1), L1_ffn_ln_gamma, L1_ffn_ln_beta, L1_ffn_router_w, L1_ffn_gate_up_w, L1_ffn_down_w, L1_ffn_shared_gate_up_w, L1_ffn_shared_down_w)
    return x

_drawn_inputs = setup_inputs


def setup_inputs(seed=0):
    import zlib

    import numpy as np

    out = dict(_drawn_inputs(seed))
    spreads = {'L0_xattn_bq': (0.0, 0.1),
     'L0_xattn_bk': (0.0, 2.0),
     'L0_xattn_bv': (0.0, 0.1),
     'L0_xattn_bo': (0.0, 0.1),
     'L1_attn_b1': (0.0, 0.1),
     'L1_attn_b2': (0.0, 0.1),
     'L1_ffn_ln_gamma': (1.0, 0.2),
     'L1_ffn_ln_beta': (0.0, 0.1)}
    factors = {'L0_attn_norm_w': 8.0,
     'L0_attn_q_gamma': 8.0,
     'L0_attn_k_gamma': 8.0,
     'L0_ffn_b1': 2.731,
     'L1_xattn_bo': 3.911,
     'L1_attn_t_k': 8.0,
     'L1_attn_t_v': 29.827,
     'L0_ffn_b2': 2.749}
    for name, (base, spread) in spreads.items():
        noise = np.random.default_rng([zlib.crc32(name.encode()), seed]).standard_normal(out[name].shape)
        drawn = base * np.exp(spread * noise) if base else spread * noise
        out[name] = jnp.asarray(drawn.astype(out[name].dtype))
    for name, factor in factors.items():
        out[name] = (out[name] * factor).astype(out[name].dtype)
    return out
```

```python
from contextlib import ExitStack

import concourse.bass as bass
from concourse import mybir

F32 = mybir.dt.float32
ALU = mybir.AluOpType
ACT = mybir.ActivationFunctionType
AX = mybir.AxisListType

NB, NQ, D, DC, NK = 16, 64, 256, 192, 1601
NT = 8
KT = 13
KL = NK - 12 * 128


class Sem:

    def __init__(self, handle):
        self.h, self.n = handle, 0


class Queues:

    def __init__(self):
        self.q = {k: [] for k in ("pe", "dve", "act", "pool", "sp")}

    def op(self, eng, fn, *waits, sem=None, inc=1):
        self.q[eng].append((waits, fn, sem, inc))
        if sem is not None:
            sem.n += inc
            return (sem, sem.n)
        return None

    def emit(self, eng, e):
        seen = {}
        for waits, fn, sem, inc in self.q[eng]:
            for w in waits:
                if w is None:
                    continue
                s, n = w
                if seen.get(id(s), 0) < n:
                    e.wait_ge(s.h, n)
                    seen[id(s)] = n
            if fn is None:
                continue
            ins = fn(e)
            if sem is not None:
                ins.then_inc(sem.h, inc)


def program(nc, d, out, stages=6, first=1):
    ctx = ExitStack()
    with ctx:
        def sb(name, shape, dt=F32):
            return ctx.enter_context(nc.sbuf_tensor(name, shape, dt))

        sems = [0]

        def sem(name):
            sems[0] += 1
            return Sem(ctx.enter_context(nc.semaphore(f"s_{name}")))

        Q = Queues()
        op = Q.op
        ps = ctx.enter_context(nc.psum_tensor("ps", [128, 8, 512], F32))
        psf = ps[:, :, :].rearrange("p b n -> p (b n)")

        x = sb("x", [128, NT, D])
        h = sb("h", [128, NT, D])
        hT = sb("hT", [128, 2, NT * 128])
        ident = sb("ident", [128, 128])
        small = sb("small", [128, 512])
        wsb = sb("wsb", [128, 14800])
        arena = sb("arena", [128, 26000])

        class Carve:
            def __init__(self, t, off=0):
                self.t, self.off = t, off

            def __call__(self, parts, *shape):
                n = 1
                for s in shape:
                    n *= s
                v = self.t[0:parts, self.off:self.off + n]
                self.off += n
                if len(shape) == 2:
                    v = v.rearrange("p (a b) -> p a b", b=shape[1])
                elif len(shape) == 3:
                    v = v.rearrange("p (a b c) -> p a b c", b=shape[1], c=shape[2])
                assert self.off <= self.t.shape[1], (self.off, self.t.shape)
                return v

        wc = Carve(wsb)
        X0 = dict(wq=wc(128, 2, 256), wk=wc(128, 2, 193), wv1=wc(128, 16, 128), wv2=wc(65, 16, 128), wo=wc(128, 2, 256))
        endx0 = wc.off
        aWq, aWkv, aWout = wc(128, 2, 1024), wc(128, 2, 1024), wc(128, 4, 256)
        fw1, fw2 = wc(128, 2, 1024), wc(128, 8, 256)
        wc = Carve(wsb)
        X1 = dict(wq=wc(128, 2, 512), wk=wc(128, 4, 192), wv1=wc(128, 8, 128), wv2=wc(64, 8, 128), wo=wc(128, 4, 256))
        assert wc.off <= endx0
        wc = Carve(wsb, endx0)
        tk, tv, tq = wc(128, 2, 256), wc(128, 2, 256), wc(128, 2, 256)
        sgu, sdn = wc(128, 2, 512), wc(128, 2, 256)
        rw = wc(128, 2, 8)
        W1T, W2T, W2 = wc(128, 2, 64), wc(64, 256), wc(128, 2, 64)
        b2rep, b1rep = wc(64, 256), wc(64, 64)

        cc = Carve(small)
        mask0, mask1 = cc(128, 8), cc(128, 2)
        bq = cc(128, 2)
        eord = cc(128, 8)
        normw, qg, kg, b1c = cc(128, 2), cc(128, 8), cc(128, 8), cc(128, 8)
        tb1, tb2 = cc(64, 1), cc(128, 2)
        lng, lnb = cc(128, 2), cc(128, 2)
        st, mv = cc(128, NT, 6), cc(128, NT, 2)
        ve, sd, rs = cc(128, NT), cc(128, NT), cc(128, NT)
        junk = cc(128, 128)
        ss2 = cc(128, NT)

        s_c, s_x = sem("c"), sem("x")
        s_w = [sem(f"w{i}") for i in range(6)]
        s_bias = [sem(f"bias{i}") for i in range(4)]

        def load(dst, src, s, *waits):
            return op("sp", lambda e: e.dma_start(dst, src), *waits, sem=s, inc=16)

        t_x = load(x[:, :, :], d["x"].rearrange("(t b) n c -> (b n) t c", b=2), s_x)
        for dst, n in ((ident[:, :], "ident"), (mask0, "mask0"), (mask1, "mask1"), (bq, "bq"), (eord, "eord"),
                       (normw, "normw"), (qg, "qg"), (kg, "kg"), (b1c, "b1c"), (tb1, "tb1"), (tb2, "tb2"),
                       (lng, "lng"), (lnb, "lnb")):
            t_c = load(dst, d[n], s_c)
        for k in ("wq", "wk", "wv1", "wv2", "wo"):
            t_w0 = load(X0[k], d["x0_" + k], s_w[0])
        biasb = sb("biasb", [128, 256])

        eng_sems = {}

        def fresh(tag):
            old = dict(eng_sems)
            for k in ("pe", "dve", "act", "pool"):
                eng_sems[k] = sem(f"{tag}_{k}")
            if old:
                ends = [(s, s.n) for s in old.values() if s.n]
                for k in ("pe", "dve", "act", "pool"):
                    op(k, None, *ends)
                return ends
            return []

        def pe(fn, *w):
            return op("pe", fn, *w, sem=eng_sems["pe"])

        def dve(fn, *w):
            return op("dve", fn, *w, sem=eng_sems["dve"])

        def act(fn, *w):
            return op("act", fn, *w, sem=eng_sems["act"])

        def pool(fn, *w):
            return op("pool", fn, *w, sem=eng_sems["pool"])

        def mms(outap, pairs):
            def f(e):
                n = len(pairs)
                for i, (a, b) in enumerate(pairs):
                    m = e.matmul(outap, a, b, start=(i == 0), stop=(i == n - 1))
                return m
            return f

        def seq(*fns):
            def f(e):
                for g in fns:
                    m = g(e)
                return m
            return f

        def tr(outap, inap, k=128):
            return lambda e: e.transpose(outap, inap, ident[0:k, 0:k])

        def rsqrt_of(v, n_ap, r_ap, *w):
            a = act(lambda e: e.activation(n_ap, v, ACT.Sqrt), *w)
            return dve(lambda e: e.reciprocal(r_ap, n_ap), a)

        def layernorm(*w):
            for t in range(NT):
                a = dve(lambda e, t=t: e.bn_stats(st[:, t, :], x[:, t, :]), *w)
                b = dve(lambda e, t=t: e.bn_aggr(mv[:, t, :], st[:, t, :]), a)
            c = dve(lambda e: e.tensor_scalar(ve, mv[:, :, 1], 1e-5, None, ALU.add), b)
            r = rsqrt_of(ve, sd, rs, c)
            toks = []
            for t in range(NT):
                toks.append(dve(lambda e, t=t: e.tensor_scalar(h[:, t, :], x[:, t, :], mv[:, t, 0:1], rs[:, t:t + 1],
                                                               ALU.subtract, ALU.mult), r))
            return toks

        def to_hT(toks, scale=None, shift=None):
            res = {}
            n = 0
            for half in range(2):
                for k in range(2):
                    bank = n % 2
                    p = pe(seq(*[tr(ps[:, bank, 128 * i:128 * i + 128], h[:, 4 * half + i, 128 * k:128 * k + 128])
                                 for i in range(4)]), toks[4 * half + 3], t_c, res.get(n - 2))
                    o, i_ = hT[:, k, 512 * half:512 * half + 512], ps[:, bank, :]
                    if scale is None:
                        res[n] = act(lambda e, o=o, i_=i_: e.copy(o, i_), p)
                    elif shift is None:
                        res[n] = dve(lambda e, o=o, i_=i_, k=k: e.tensor_scalar(o, i_, scale[:, k:k + 1], None, ALU.mult), p)
                    else:
                        res[n] = dve(lambda e, o=o, i_=i_, k=k: e.tensor_scalar(
                            o, i_, scale[:, k:k + 1], shift[:, k:k + 1], ALU.mult, ALU.add), p)
                    n += 1
            return res[3]

        bias_tok = []

        def load_bias(i, name, *w):
            bias_tok.append(load(biasb[:, :], d[name].partition_broadcast(128), s_bias[i], *w, *bias_tok[-1:]))
            return bias_tok[-1]

        def xattn(tag, W, G, hpg, mask, kx, t_w, t_b, qbias):
            H = G * hpg
            NP = H // 2
            NH = hpg * 64
            K2 = 65 if kx else 64
            ar = Carve(arena)
            cT1 = [ar(128, NK) for _ in range(2)]
            cT2 = [ar(65, NK) for _ in range(2)]
            cN = [ar(128, KT, 193) for _ in range(2)]
            P = [ar(128, NK) for _ in range(2)]
            PT = ar(128, KT, 128)
            q1, q2 = ar(128, H * 64), ar(65, H * 64)
            qT = [ar(128, G, 128) for _ in range(2)]
            qbd = [ar(128, G * hpg, 64) for _ in range(2)]
            On = [ar(128, 193) for _ in range(2)]
            oT1, oT2 = ar(128, H, 128), ar(65, H, 128)
            aT = ar(128, G, 128)
            mx, rc = [ar(128, 1) for _ in range(2)], [ar(128, 1) for _ in range(2)]
            s_ctx = [sem(f"{tag}ctx{i}") for i in range(2)]

            toks = layernorm(t_x)
            xb = None
            if t_b is not None:
                xb = pool(lambda e: e.tensor_tensor(x[:, :, :], x[:, :, :],
                                                    biasb[:, :].unsqueeze(1).broadcast_to([128, NT, D]), ALU.add),
                          t_b, toks[-1])
            t_h = to_hT(toks)
            ones = []
            for i in range(2):
                ones.append(dve(lambda e, i=i: e.memset(cN[i][:, :, 192:193], 1.0)))
                ones.append(dve(lambda e, i=i: e.memset(cT2[i][64:65, :], 1.0)))
            t_ones = ones[-1]

            free = {}

            def load_ctx(b):
                i = b % 2
                w = (free.get(b - 2),) if b >= 2 else (t_start,)
                load(cT1[i], d["ctxT"][b, 0:128, :], s_ctx[i], *w)
                load(cT2[i][0:64, :], d["ctxT"][b, 128:192, :], s_ctx[i])
                load(cN[i][:, 0:12, 0:192], d["ctx"][b, 0:1536, :].rearrange("(t p) c -> p t c", p=128), s_ctx[i])
                return load(cN[i][0:KL, 12, 0:192], d["ctx"][b, 1536:NK, :], s_ctx[i])

            t_start = (eng_sems["dve"], toks[0][1])
            ctx_tok = {0: load_ctx(0), 1: load_ctx(1)}

            ex, smax, tfree = {}, {}, {}
            av, on, oTt = {}, {}, {}
            pt_ev = {}
            qd, qq, qTt, atile = {}, {}, {}, {}
            pairs = [(b, j) for b in range(NB) for j in range(NP)]
            evs = [None, None]
            q1free = {}

            def queries(tile):
                i = tile % 2
                p = pe(seq(*[mms(ps[:, 7, 128 * g:128 * g + 128],
                                 [(W["wq"][:, k, 128 * g:128 * g + 128], hT[:, k, 128 * tile:128 * tile + 128])
                                  for k in range(2)]) for g in range(G)]), t_h, t_w, xfree[0])
                src = ps[:, 7, 0:128 * G].rearrange("p (g n) -> p g n", n=128)
                w = (p, qd.get(2 * tile - 3))
                if qbias is None:
                    t = dve(lambda e: e.tensor_copy(qT[i], src), *w)
                else:
                    for g in range(G):
                        t = dve(lambda e, g=g: e.tensor_scalar(qT[i][:, g, :], src[:, g, :], qbias[:, g:g + 1], None, ALU.add), *w)
                qTt[tile] = t
                xfree[0] = t

            def blockdiag(b):
                i = b % 2
                s = qT[(b // 2) % 2][:, :, 64 * i:64 * i + 64]
                for g in range(G):
                    t = pool(lambda e, g=g: e.tensor_tensor(
                        qbd[i][:, g * hpg:(g + 1) * hpg, :], s[:, g, :].unsqueeze(1).broadcast_to([128, hpg, 64]),
                        mask.unsqueeze(2).broadcast_to([128, hpg, 64]), ALU.mult), qTt[b // 2], qq.get(b - 2), t_c)
                qd[b] = t

            def absorb(b, s_done):
                i = b % 2
                last = None
                for g in range(G):
                    for part in range(2):
                        m = 128 if part == 0 else K2
                        o = ps[0:m, 7, 0:NH]
                        p = pe(mms(o, [(W["wk"][:, g, 128 * part:128 * part + m],
                                        qbd[i][:, g * hpg:(g + 1) * hpg, :].rearrange("p a b -> p (a b)"))]),
                               qd[b], xfree[0])
                        dst = (q1 if part == 0 else q2)[0:m, g * NH:(g + 1) * NH]
                        xfree[0] = last = act(lambda e, dst=dst, o=o: e.copy(dst, o), p, s_done)
                qq[b] = last

            xfree = [None]

            def scores(n):
                b, j = pairs[n]
                i = b % 2
                w = [ex.get(n - 1), qq[b], ctx_tok[b], t_ones]
                fs = []
                for c in range(4):
                    k0, k1 = 512 * c, min(512 * c + 512, NK)
                    fs.append(mms(psf[:, k0:k1], [(q1[:, 128 * j:128 * j + 128], cT1[i][:, k0:k1]),
                                                  (q2[0:K2, 128 * j:128 * j + 128], cT2[i][0:K2, k0:k1])]))
                p = pe(seq(*fs), *w)
                s_tok[n] = p
                m = dve(lambda e: e.tensor_reduce(mx[n % 2], psf[:, 0:NK], AX.X, ALU.max, negate=True), p, ex.get(n - 2))
                ex[n] = act(lambda e: e.activation(P[n % 2], psf[:, 0:NK], ACT.Exp, bias=mx[n % 2]), m, tr_done.get(n - 2))

            s_tok, tr_done = {}, {}

            def values(n):
                b, j = pairs[n]
                i = b % 2
                evt = []
                for g in range(4):
                    bank = 4 + g % 2
                    ts = range(4 * g, min(4 * g + 4, KT))
                    fs = []
                    for t in ts:
                        k = 128 if t < 12 else KL
                        fs.append(tr(ps[0:k, bank, 128 * (t % 4):128 * (t % 4) + 128], P[n % 2][:, 128 * t:128 * t + k]))
                    p = pe(seq(*fs), ex[n], evs[g % 2])
                    k = 128 if g < 3 else KL
                    c = 512 if g < 3 else 128
                    dst = PT[0:k, 4 * g:4 * g + c // 128, :].rearrange("p a b -> p (a b)")
                    src = ps[0:k, bank, 0:c]
                    w = (p, av.get(n - 1))
                    if g % 2 == 0:
                        t_ = act(lambda e, dst=dst, src=src: e.copy(dst, src), *w)
                    else:
                        t_ = dve(lambda e, dst=dst, src=src: e.tensor_copy(dst, src), *w)
                    evs[g % 2] = t_
                    evt.append(t_)
                tr_done[n] = p
                o = ps[:, 6, 0:193]
                av[n] = pe(mms(o, [(PT[0:(128 if t < 12 else KL), t, :], cN[i][0:(128 if t < 12 else KL), t, :])
                                   for t in range(KT)]), *evt, on.get(n - 1), ctx_tok[b], t_ones)
                if j == NP - 1:
                    free[b] = av[n]
                r = dve(lambda e: e.reciprocal(rc[n % 2], o[:, 192:193]), av[n])
                on[n] = dve(lambda e: e.tensor_scalar(On[n % 2], o, rc[n % 2], None, ALU.mult), r, otr.get(n - 2))

            otr = {}

            def turn(n):
                b, j = pairs[n]
                o1, o2 = ps[:, 7, 0:128], ps[0:K2, 7, 128:256]
                p = pe(seq(tr(o1, On[n % 2][:, 0:128]), tr(o2, On[n % 2][:, 128:128 + K2])), on[n], xfree[0])
                otr[n] = p
                c = 64 * (b % 2)
                w = (p, atile.get(b // 2 - 1))
                dve(lambda e: e.tensor_copy(oT1[:, 2 * j:2 * j + 2, c:c + 64], o1.rearrange("p (a q) -> p a q", a=2)), *w)
                xfree[0] = oTt[n] = dve(lambda e: e.tensor_copy(oT2[0:K2, 2 * j:2 * j + 2, c:c + 64],
                                                                o2.rearrange("p (a q) -> p a q", a=2)), *w)

            def project(tile):
                last = oTt[(2 * tile + 2) * NP - 1]
                fs = []
                for g in range(G):
                    prs = []
                    for hh in range(g * hpg, (g + 1) * hpg):
                        prs += [(W["wv1"][:, hh, :], oT1[:, hh, :]), (W["wv2"][0:K2, hh, :], oT2[0:K2, hh, :])]
                    fs.append(mms(ps[:, 7, 128 * g:128 * g + 128], prs))
                p = pe(seq(*fs), last, xfree[0])
                atile[tile] = p
                c = act(lambda e: e.copy(aT.rearrange("p a b -> p (a b)"), ps[:, 7, 0:128 * G]), p, at_free[0])
                o = ps[:, 7, 0:256]
                p = pe(mms(o, [(aT[:, g, :], W["wo"][:, g, :]) for g in range(G)]), c)
                at_free[0] = p
                xfree[0] = dve(lambda e: e.tensor_tensor(x[:, tile, :], o, x[:, tile, :], ALU.add), p, xb, toks[-1])

            at_free = [None]

            N = len(pairs)

            def start_batch(b):
                if b % 2 == 0:
                    queries(b // 2)
                blockdiag(b)
                absorb(b, s_tok.get(b * NP - 1))

            for n in range(N + 1):
                if n < N:
                    b, j = pairs[n]
                    if j == 0:
                        start_batch(b)
                    scores(n)
                if n >= 1:
                    values(n - 1)
                if n >= 2:
                    turn(n - 2)
                    b2, j2 = pairs[n - 2]
                    if j2 == NP - 1 and b2 % 2 == 1:
                        project(b2 // 2)
                if n >= 1 and pairs[n - 1][1] == NP - 1 and pairs[n - 1][0] + 2 < NB:
                    bb = pairs[n - 1][0] + 2
                    ctx_tok[bb] = load_ctx(bb)
            turn(N - 1)
            project(NT - 1)

        fresh("x0")
        t_b = load_bias(0, "x0_bo")
        if first <= 1:
            xattn("x0", X0, 2, 8, mask0, True, t_w0, t_b, bq)

        for dst, n in ((aWq, "a_wq"), (aWkv, "a_wkv"), (aWout, "a_wout")):
            t_w1 = load(dst, d[n], s_w[1])
        for dst, n in ((fw1, "f_w1"), (fw2, "f_w2")):
            t_w2 = load(dst, d[n], s_w[2])

        def load_x1(*w):
            for k in ("wq", "wk", "wv1", "wv2", "wo"):
                t = load(X1[k], d["x1_" + k], s_w[3], *w)
            return t

        def load_b(*w):
            for dst, n in ((tk, "t_k"), (tv, "t_v"), (tq, "t_q"), (sgu, "m_sgu"), (sdn, "m_sdn"), (rw, "m_rw")):
                t = load(dst, d[n], s_w[4], *w)
            return t

        if first > 1:
            for k in ("pe", "dve", "act", "pool", "sp"):
                op(k, None, t_x, t_c, t_w0, t_w1, t_w2, t_b)
        if first > 2:
            tw1 = load_x1()
        if first > 3:
            tmem = load_b()
            for k in ("pe", "dve", "act", "pool", "sp"):
                op(k, None, tmem)

        def selfattn():
            ends = fresh("sa")
            tw = load_x1(*ends)
            ar = Carve(arena)
            caus = ar(128, 128)
            t_cm = load(caus, d["causal"], s_c, *ends)
            junk2 = ar(128, NT, 256)
            qn = ar(128, 16, 64)
            kn = ar(128, 8, 2, 64)
            vx = ar(128, 8, 65)
            sq = ar(128, 24, 64)
            s1, s2, s3 = ar(128, 24), ar(128, 24), ar(128, 24)
            qTs, kTs = ar(128, 8, 128), ar(128, 8, 128)
            E1, E2 = ar(128, 16, 128), ar(128, 16, 128)
            o1 = ar(128, 16, 64)
            o2 = ar(128, 8, 64)
            rr = ar(128, 16)
            oT = ar(128, 4, 128)
            g1 = dve(lambda e: e.tensor_scalar(qg, qg, 1.0, 8.0, ALU.add, ALU.mult), t_c)
            g2 = dve(lambda e: e.tensor_scalar(kg, kg, 1.0, 8.0, ALU.add, ALU.mult), t_c)
            pone = pool(lambda e: e.memset(vx[:, :, 64:65], 1.0))
            toks = layernorm()
            for t in range(NT):
                a = dve(lambda e, t=t: e.tensor_tensor_reduce(junk2[:, t, :], h[:, t, :], h[:, t, :], 1.0, 0.0, ALU.mult, ALU.add,
                                                              ss2[:, t:t + 1]), toks[-1])
            a = dve(lambda e: e.tensor_scalar(ve, ss2, 1.0 / D, 1.1920929e-07, ALU.mult, ALU.add), a)
            r = rsqrt_of(ve, sd, rs, a)
            for t in range(NT):
                toks[t] = dve(lambda e, t=t: e.tensor_scalar(h[:, t, :], h[:, t, :], rs[:, t:t + 1], None, ALU.mult), r)
            t_h = to_hT(toks, scale=normw)
            lastx = None

            def at(i):
                return 8 * (i % 2) + i // 2

            for t in range(NT):
                hs = [hT[:, k, 128 * t:128 * t + 128] for k in range(2)]
                fs = [mms(ps[:, c, :], [(hs[k], aWq[:, k, 512 * c:512 * c + 512]) for k in range(2)]) for c in range(2)]
                fs += [mms(ps[:, 2 + c, :], [(hs[k], aWkv[:, k, 512 * c:512 * c + 512]) for k in range(2)]) for c in range(2)]
                p = pe(seq(*fs), t_h, t_w1, lastx)
                qk = psf[:, 0:1536].rearrange("p (a c) -> p a c", c=64)
                a = act(lambda e: e.activation(sq, qk, ACT.Square), p)
                b = dve(lambda e: e.tensor_reduce(s1, sq, AX.X, ALU.add), a)
                c = act(lambda e: e.activation(s2, s1, ACT.Sqrt), b)
                m = dve(lambda e: e.tensor_scalar(s2, s2, 1e-12, None, ALU.max), c)
                m = dve(lambda e: e.reciprocal(s3, s2), m)
                dve(lambda e: e.tensor_tensor(qn, qk[:, 0:16, :], s3[:, 0:16].unsqueeze(2).broadcast_to([128, 16, 64]), ALU.mult), m)
                for j in range(2):
                    u = dve(lambda e, j=j: e.tensor_tensor(kn[:, :, j, :], qk[:, 16:24, :],
                                                           s3[:, 16:24].unsqueeze(2).broadcast_to([128, 8, 64]), ALU.mult), m)
                v = act(lambda e: e.copy(vx[:, :, 0:64], ps[:, 3, :].rearrange("p (a c) -> p a c", c=64)), p)
                p = pe(seq(*[tr(ps[:, 4 + i // 4, 128 * (i % 4):128 * (i % 4) + 128], qn[:, 2 * i:2 * i + 2, :].rearrange("p a c -> p (a c)"))
                             for i in range(8)]), u, lastx)
                w = dve(lambda e: e.tensor_tensor(qTs, psf[:, 2048:3072].rearrange("p (a c) -> p a c", c=128),
                                                  qg.unsqueeze(2).broadcast_to([128, 8, 128]), ALU.mult), p, g2)
                p = pe(seq(*[tr(ps[:, 6 + i // 4, 128 * (i % 4):128 * (i % 4) + 128], kn[:, i, :, :].rearrange("p a c -> p (a c)"))
                             for i in range(8)]))
                w = dve(lambda e: e.tensor_tensor(kTs, psf[:, 3072:4096].rearrange("p (a c) -> p a c", c=128),
                                                  kg.unsqueeze(2).broadcast_to([128, 8, 128]), ALU.mult), p, g2)
                p = pe(seq(*[mms(psf[:, 128 * at(i):128 * at(i) + 128],
                                 [(kTs[64 * (i % 2):64 * (i % 2) + 64, i // 2, :], qTs[64 * (i % 2):64 * (i % 2) + 64, i // 2, :])])
                             for i in range(16)]), w, v, u)
                S = psf[:, 0:2048].rearrange("p (a c) -> p a c", c=128)
                a = act(lambda e: e.activation(E1, S, ACT.Tanh, scale=1.0 / 50.0), p)
                a = act(lambda e: e.activation(E2, E1, ACT.Exp, scale=6.25), a)
                a = pool(lambda e: e.tensor_tensor(E2, E2, caus.unsqueeze(1).broadcast_to([128, 16, 128]), ALU.mult), a, t_cm)
                p = pe(seq(*[mms(psf[:, 2048 + 128 * at(i):2048 + 128 * at(i) + 65], [(E2[:, at(i), :], vx[:, i // 2, :])])
                             for i in range(16)]), a, pone, w)
                OO = psf[:, 2048:4096].rearrange("p (a c) -> p a c", c=128)
                r = dve(lambda e: e.reciprocal(rr, OO[:, :, 64]), p)
                r = dve(lambda e: e.tensor_tensor(o1, OO[:, :, 0:64], rr.unsqueeze(2).broadcast_to([128, 16, 64]), ALU.mult), r)
                r = dve(lambda e: e.tensor_tensor(o2, o1[:, 0:8, :], o1[:, 8:16, :], ALU.add), r)
                p = pe(seq(*[tr(ps[:, 0, 128 * i:128 * i + 128], o2[:, 2 * i:2 * i + 2, :].rearrange("p a c -> p (a c)"))
                             for i in range(4)]), r, a)
                c = act(lambda e: e.copy(oT.rearrange("p a c -> p (a c)"), ps[:, 0, :]), p)
                p = pe(mms(ps[:, 1, 0:256], [(oT[:, k, :], aWout[:, k, :]) for k in range(4)]), c)
                lastx = dve(lambda e, t=t: e.tensor_tensor(x[:, t, :], ps[:, 1, 0:256], x[:, t, :], ALU.add), p)
            return tw

        def ffn():
            ends = fresh("ff")
            t_b = load_bias(1, "f_b2", *ends)
            ts = s_w[4]
            load_b(*ends)
            ar = Carve(arena)
            gT = ar(128, 8, 1024)
            toks = layernorm()
            xb = pool(lambda e: e.tensor_tensor(x[:, :, :], x[:, :, :],
                                                biasb[:, :].unsqueeze(1).broadcast_to([128, NT, D]), ALU.add), t_b, toks[-1])
            t_h = to_hT(toks)
            g = {}
            n = 0
            for half in range(2):
                for f in range(8):
                    bank = 2 + n % 4
                    p = pe(mms(ps[:, bank, :], [(fw1[:, k, 128 * f:128 * f + 128], hT[:, k, 512 * half:512 * half + 512])
                                                for k in range(2)]), t_h, t_w2, g.get(n - 4))
                    g[n] = act(lambda e, f=f, half=half, bank=bank: e.activation(
                        gT[:, f, 512 * half:512 * half + 512], ps[:, bank, :], ACT.Gelu, bias=b1c[:, f:f + 1]), p)
                    n += 1
            y = {}
            for t in range(NT):
                bank = 6 + t % 2
                p = pe(mms(ps[:, bank, 0:256], [(gT[:, f, 128 * t:128 * t + 128], fw2[:, f, :]) for f in range(8)]),
                       g[7 if t < 4 else 15], y.get(t - 2))
                y[t] = dve(lambda e, t=t, bank=bank: e.tensor_tensor(x[:, t, :], ps[:, bank, 0:256], x[:, t, :], ALU.add), p, xb)
            return (ts, ts.n)

        def memory(t_w):
            ends = fresh("tt")
            for dst, n in ((W1T, "t_W1T"), (W2T, "t_W2T"), (W2, "t_W2"),
                           (b2rep, "t_b2"), (b1rep, "t_b1")):
                src = d[n].partition_broadcast(64) if n in ("t_b1", "t_b2") else d[n]
                t_p = load(dst, src, s_w[5], *ends)
            ar = Carve(arena)
            zT, eT, qT = ar(128, 2, 1024), ar(128, 2, 1024), ar(128, 2, 1024)
            z, e_, q_ = ar(64, NB, 256), ar(64, NB, 256), ar(64, NB, 256)
            wd = ar(128, 2, 256)
            ones = ar(64, 64)
            toks = layernorm()
            t_h = to_hT(toks)
            t_o = pool(lambda e: e.memset(ones, 1.0))
            t_d = dve(lambda e: e.tensor_tensor(wd, tk, tv, ALU.subtract), t_w)
            n = 0
            ev = {}
            for W, T, N in ((tk, zT, z), (wd, eT, e_), (tq, qT, q_)):
                for m in range(2):
                    for half in range(2):
                        bank = n % 4
                        p = pe(mms(ps[:, bank, :], [(W[:, k, 128 * m:128 * m + 128], hT[:, k, 512 * half:512 * half + 512])
                                                    for k in range(2)]), t_h, t_w, t_d, ev.get(n - 4))
                        o, i_ = T[:, m, 512 * half:512 * half + 512], ps[:, bank, :]
                        if n % 2:
                            ev[n] = act(lambda e, o=o, i_=i_: e.copy(o, i_), p)
                        else:
                            ev[n] = dve(lambda e, o=o, i_=i_: e.tensor_copy(o, i_), p)
                        n += 1
                for b in range(0, NB, 2):
                    bank = n % 4
                    p = pe(seq(*[mms(ps[0:64, bank, 256 * i:256 * i + 256],
                                     [(hT[:, k, 64 * (b + i):64 * (b + i) + 64], W[:, k, :]) for k in range(2)])
                                 for i in range(2)]), ev.get(n - 4))
                    o, i_ = N[:, b:b + 2, :].rearrange("p a c -> p (a c)"), ps[0:64, bank, :]
                    if n % 2:
                        ev[n] = act(lambda e, o=o, i_=i_: e.copy(o, i_), p)
                    else:
                        ev[n] = dve(lambda e, o=o, i_=i_: e.tensor_copy(o, i_), p)
                    n += 1
            t_in = [ev[n - 1], ev[n - 2]]
            hTs, hs, us, u = ar(64, 64), ar(64, 64), ar(64, 64), ar(64, 64)
            m1, sqv, th, nu, de, ph, gp, da = [ar(64, 64) for _ in range(8)]
            dr, eb = ar(64, 256), [ar(64, 256) for _ in range(2)]
            drT = ar(128, 2, 64)
            gq = ar(64, 64)
            o64 = [ar(64, 256) for _ in range(2)]
            C = 0.001 * 2.0 / (NQ * D)
            C0 = 0.3989422804014327
            up1, up2, upb1, upb2 = None, None, None, None
            oq = None
            s_o = [sem("o64_0"), sem("o64_1")]
            dst_tok = {}
            prev = None
            last_q = None
            ov_prev = None
            upd = [t_p]
            oall = h
            for t in range(NB):
                tt = slice(64 * t, 64 * t + 64)
                w0 = [*t_in, *upd, t_o]
                pa = pe(seq(mms(ps[0:64, 0, 0:64], [(W1T[:, k, :], zT[:, k, tt]) for k in range(2)]),
                            mms(ps[0:64, 1, 0:64], [(zT[:, k, tt], W1T[:, k, :]) for k in range(2)])), *w0)
                ah = act(lambda e: e.activation(hTs, ps[0:64, 0, 0:64], ACT.Gelu, bias=tb1), pa, t_c)
                a = dve(lambda e: e.tensor_tensor(u, ps[0:64, 1, 0:64], b1rep, ALU.add), pa, *w0)
                sq_ = dve(lambda e: e.tensor_tensor(sqv, u, u, ALU.mult), a)
                m_ = dve(lambda e: e.tensor_scalar(m1, sqv, 1e-24, 2e-12, ALU.is_lt, ALU.mult), sq_)
                us_ = dve(lambda e: e.tensor_tensor(us, u, m1, ALU.add), m_)
                a2 = act(lambda e: e.activation(hs, us, ACT.Gelu), us_)
                at = act(lambda e: e.activation(th, sqv, ACT.Tanh, scale=-0.25), sq_)
                pb = pe(seq(*[mms(ps[:, 2, 64 * m:64 * m + 64], [(W2T[:, 128 * m:128 * m + 128], hTs)]) for m in range(2)]), ah)
                for m in range(2):
                    dT = dve(lambda e, m=m, tt=tt: e.scalar_tensor_tensor(drT[:, m, :], ps[:, 2, 64 * m:64 * m + 64], tb2[:, m:m + 1],
                                                                          eT[:, m, tt], ALU.add, ALU.add), pb, *w0)
                pc = pe(mms(ps[0:64, 3, 0:256], [(hTs, W2T)]), ov_prev)
                eb_ = pool(lambda e, t=t: e.tensor_tensor(eb[t % 2], e_[:, t, :], b2rep, ALU.add), *w0)
                pd = pe(mms(ps[0:64, 4, 0:64], [(drT[:, m, :], W2[:, m, :]) for m in range(2)]), dT)
                d_ = dve(lambda e, t=t: e.tensor_tensor(dr, ps[0:64, 3, 0:256], eb[t % 2], ALU.add), pc, eb_)
                r = dve(lambda e: e.tensor_scalar(nu, th, C0, C0, ALU.mult, ALU.add), at)
                r = dve(lambda e: e.tensor_scalar(de, th, -1.0, 1.0, ALU.mult, ALU.add), at)
                r = dve(lambda e: e.reciprocal(de, de), r)
                r = dve(lambda e: e.tensor_tensor(ph, nu, de, ALU.mult), r)
                r = dve(lambda e: e.tensor_tensor(ph, ph, u, ALU.mult), r)
                r = dve(lambda e: e.reciprocal(gp, us), us_, r)
                r = dve(lambda e: e.tensor_tensor(gp, gp, hs, ALU.mult), r, a2)
                r = dve(lambda e: e.tensor_tensor(gp, gp, ph, ALU.add), r)
                da_ = dve(lambda e: e.tensor_tensor(da, ps[0:64, 4, 0:64], gp, ALU.mult), pd, r)
                p1 = pe(seq(*[mms(ps[:, 5, 64 * k:64 * k + 64], [(z[:, t, 128 * k:128 * k + 128], da)]) for k in range(2)]), da_)
                p2 = pe(seq(mms(ps[0:64, 6, 0:64], [(ones, da)]), mms(ps[0:64, 6, 64:66], [(da, ones[:, 0:2])])))
                p3 = pe(seq(mms(ps[0:64, 7, 0:256], [(hs, dr)]),
                            mms(ps[0:64, 7, 256:512], [(ones, dr)])), d_, a2)
                p4 = pe(seq(*[mms(ps[:, 4, 64 + 64 * m:128 + 64 * m], [(dr[:, 128 * m:128 * m + 128], hs)]) for m in range(2)],
                            *[mms(ps[:, 4, 256 + 64 * m:258 + 64 * m], [(dr[:, 128 * m:128 * m + 128], ones[:, 0:2])]) for m in range(2)]), da_)

                def update(dst, src, *w):
                    return dve(lambda e: e.scalar_tensor_tensor(dst, src, -C, dst, ALU.mult, ALU.add), *w)
                rd = [last_q]
                u1 = update(W1T.rearrange("p a b -> p (a b)"), ps[:, 5, 0:128], p1, last_q)
                u2 = update(b1rep, ps[0:64, 6, 0:64], p2)
                u3 = update(tb1, ps[0:64, 6, 64:65], p2, last_q)
                u4 = update(W2T, ps[0:64, 7, 0:256], p3)
                u5 = update(b2rep, ps[0:64, 7, 256:512], p3, eb_)
                for m in range(2):
                    u6 = update(W2[:, m, :], ps[:, 4, 64 + 64 * m:128 + 64 * m], p4)
                    u7 = update(tb2[:, m:m + 1], ps[:, 4, 256 + 64 * m:257 + 64 * m], p4)
                upd = [u7]
                pq = pe(mms(ps[0:64, 0, 128:192], [(W1T[:, k, :], qT[:, k, tt]) for k in range(2)]), u7)
                gq_ = act(lambda e: e.activation(gq, ps[0:64, 0, 128:192], ACT.Gelu, bias=tb1), pq, u3)
                qb = pool(lambda e, t=t: e.tensor_tensor(o64[t % 2], q_[:, t, :], b2rep, ALU.add), u5, dst_tok.get(t - 2), *t_in)
                po = pe(mms(ps[0:64, 3, 256:512], [(gq, W2T)]), gq_)
                ov = dve(lambda e, t=t: e.tensor_tensor(o64[t % 2], ps[0:64, 3, 256:512], o64[t % 2], ALU.add), po, qb)
                last_q = po
                ov_prev = ov
                upd.append(gq_)
                upd.append(po)
                dst_tok[t] = load(oall[64 * (t % 2):64 * (t % 2) + 64, t // 2, :], o64[t % 2], s_o[t % 2], ov)
            dve(lambda e: e.tensor_tensor(x[:, :, :], x[:, :, :], oall[:, :, :], ALU.add), dst_tok[NB - 1], dst_tok[NB - 2])

        def moe():
            ends = fresh("mo")
            ar = Carve(arena)
            wg = [ar(128, 2, 1536) for _ in range(2)]
            wdn = [ar(128, 6, 256) for _ in range(2)]
            aT = [ar(128, 6, 512) for _ in range(2)]
            sg = [ar(128, 512) for _ in range(2)]
            lg, pr, oh1, oh2, tmp = [ar(128, NT, 8) for _ in range(5)]
            comb = ar(128, NT, 8)
            v1, v2, f_, g1, g2 = [ar(128, NT) for _ in range(5)]
            s_e = [sem("e0"), sem("e1")]
            efree = {}

            def load_e(i):
                w = ends if i < 2 else [efree[i - 2]]
                load(wg[i % 2], d["m_gu"][i], s_e[i % 2], *w)
                return load(wdn[i % 2], d["m_dn"][i], s_e[i % 2])

            et = {0: load_e(0), 1: load_e(1)}
            toks = layernorm()
            t_h = to_hT(toks, scale=lng, shift=lnb)
            p = pe(seq(*[mms(ps[:, 0, 8 * t:8 * t + 8], [(hT[:, k, 128 * t:128 * t + 128], rw[:, k, :]) for k in range(2)])
                         for t in range(NT)]), t_h)

            def b3(v):
                return v.unsqueeze(2).broadcast_to([128, NT, 8])

            L = ps[:, 0, 0:64].rearrange("p (t e) -> p t e", e=8)
            a = dve(lambda e: e.tensor_reduce(v1, L, AX.X, ALU.max), p)
            a = dve(lambda e: e.tensor_tensor(lg, L, b3(v1), ALU.subtract), a)
            a = act(lambda e: e.activation(pr, lg, ACT.Exp), a)
            a = dve(lambda e: e.tensor_reduce(v1, pr, AX.X, ALU.add), a)
            a = dve(lambda e: e.reciprocal(v1, v1), a)
            a = dve(lambda e: e.tensor_tensor(pr, pr, b3(v1), ALU.mult), a)

            def top(oh, v, a):
                a = dve(lambda e: e.tensor_reduce(v, pr, AX.X, ALU.max), a)
                a = dve(lambda e: e.tensor_tensor(tmp, pr, b3(v), ALU.is_equal), a)
                a = dve(lambda e: e.tensor_tensor(tmp, tmp, eord.unsqueeze(1).broadcast_to([128, NT, 8]), ALU.mult), a, t_c)
                a = dve(lambda e: e.tensor_reduce(f_, tmp, AX.X, ALU.max), a)
                return dve(lambda e: e.tensor_tensor(oh, tmp, b3(f_), ALU.is_equal), a)

            a = top(oh1, v1, a)
            a = dve(lambda e: e.scalar_tensor_tensor(pr, oh1, -2.0, pr, ALU.mult, ALU.add), a)
            a = top(oh2, v2, a)
            a = dve(lambda e: e.tensor_tensor(v2, v2, v1, ALU.subtract), a)
            a = act(lambda e: e.activation(g2, v2, ACT.Exp), a)
            a = dve(lambda e: e.tensor_scalar(g1, g2, 1.0, None, ALU.add), a)
            a = dve(lambda e: e.reciprocal(g1, g1), a)
            a = dve(lambda e: e.tensor_tensor(g2, g2, g1, ALU.mult), a)
            a = dve(lambda e: e.tensor_tensor(oh1, oh1, b3(g1), ALU.mult), a)
            a = dve(lambda e: e.tensor_tensor(oh2, oh2, b3(g2), ALU.mult), a)
            t_comb = dve(lambda e: e.tensor_tensor(comb, oh1, oh2, ALU.add), a)

            up, sgt, adone, ydone = {}, {}, {}, {}
            n = m = c = 0
            for i in range(9):
                gu, dn, F = (wg[i % 2], wdn[i % 2], 6) if i < 8 else (sgu, sdn, 2)
                for half in range(2):
                    A = aT[c % 2]
                    hh = [hT[:, k, 512 * half:512 * half + 512] for k in range(2)]
                    for f in range(F):
                        b = 2 * (n % 3)
                        p = pe(seq(*[mms(ps[:, b + j, :], [(gu[:, k, 128 * (f + F * j):128 * (f + F * j) + 128], hh[k]) for k in range(2)])
                                     for j in range(2)]), t_h, et.get(i), up.get(n - 3), t_comb)
                        s = act(lambda e, n=n, b=b: e.activation(sg[n % 2], ps[:, b, :], ACT.Silu), p, up.get(n - 2))
                        up[n] = dve(lambda e, n=n, b=b, A=A, f=f: e.tensor_tensor(A[:, f, :], ps[:, b + 1, :], sg[n % 2], ALU.mult),
                                    s, adone.get(c - 2))
                        n += 1
                    for t in range(4):
                        bank = 6 + m % 2
                        p = pe(mms(ps[:, bank, 0:256], [(A[:, f, 128 * t:128 * t + 128], dn[:, f, :]) for f in range(F)]),
                               up[n - 1], ydone.get(m - 2))
                        tt = 4 * half + t
                        if i < 8:
                            ydone[m] = dve(lambda e, tt=tt, i=i, bank=bank: e.scalar_tensor_tensor(
                                x[:, tt, :], ps[:, bank, 0:256], comb[:, tt, i:i + 1], x[:, tt, :], ALU.mult, ALU.add), p, *toks[-1:])
                        else:
                            ydone[m] = dve(lambda e, tt=tt, bank=bank: e.tensor_tensor(
                                x[:, tt, :], ps[:, bank, 0:256], x[:, tt, :], ALU.add), p)
                        m += 1
                    adone[c] = p
                    c += 1
                efree[i] = p
                if i + 2 < 8:
                    et[i + 2] = load_e(i + 2)

        if stages > 1 and first <= 2:
            tw1 = selfattn()
        if stages > 2 and first <= 3:
            tmem = ffn()
        if stages > 3 and first <= 4:
            t_b = load_bias(2, "x1_bo", *fresh("x1"))
            xattn("x1", X1, 4, 2, mask1, False, tw1, t_b, None)
        if stages > 4 and first <= 5:
            memory(tmem)
        if stages > 5 and first <= 6:
            moe()
        ends = [(s, s.n) for s in eng_sems.values() if s.n]
        s_out = sem("out")
        t_o = op("sp", lambda e: e.dma_start(out.rearrange("(t b) n c -> (b n) t c", b=2), x[:, :, :]), *ends, sem=s_out, inc=16)
        op("sp", None, t_o)

        block = ctx.enter_context(nc.Block())

        @block.tensor
        def _(e):
            Q.emit("pe", e)

        @block.vector
        def _(e):
            Q.emit("dve", e)

        @block.scalar
        def _(e):
            Q.emit("act", e)

        @block.gpsimd
        def _(e):
            Q.emit("pool", e)

        @block.sync
        def _(e):
            Q.emit("sp", e)


def layout(np, i):
    a = {k: np.asarray(v) for k, v in i.items()}
    C = np.ascontiguousarray
    r = {}
    r["x"] = a["x"]
    r["ctx"] = a["ctx_768"]
    r["ctxT"] = C(a["ctx_768"].transpose(0, 2, 1))
    f = np.float32
    r["ident"] = np.eye(128, dtype=f)
    p = np.arange(128)
    r["mask0"] = ((p[:, None] // 16 == np.arange(8)[None]) * 0.25).astype(f)
    r["mask1"] = ((p[:, None] // 64 == np.arange(2)[None]) * 0.125).astype(f)
    r["eord"] = np.tile(8.0 - np.arange(8), (128, 1)).astype(f)
    r["causal"] = ((p[:, None] // 64 == p[None] // 64) & (p[:, None] <= p[None])).astype(f)

    def col(v, n):
        return C(v.reshape(n, 128).T)

    def rows(w, n):
        return C(w.reshape(n, 128, w.shape[1]).transpose(1, 0, 2))

    r["bq"] = col(a["L0_xattn_bq"], 2)
    r["normw"] = col(a["L0_attn_norm_w"], 2)
    r["qg"] = col(a["L0_attn_q_gamma"].reshape(-1), 8)
    r["kg"] = C(np.concatenate([a["L0_attn_k_gamma"].T] * 2, 0))
    r["b1c"] = col(a["L0_ffn_b1"], 8)
    r["tb1"] = C(a["L1_attn_b1"].reshape(64, 1))
    r["tb2"] = col(a["L1_attn_b2"], 2)
    r["lng"] = col(a["L1_ffn_ln_gamma"], 2)
    r["lnb"] = col(a["L1_ffn_ln_beta"], 2)
    r["x0_bo"], r["f_b2"], r["x1_bo"] = a["L0_xattn_bo"], a["L0_ffn_b2"], a["L1_xattn_bo"]
    r["x0_wq"] = rows(a["L0_xattn_wq"], 2)
    r["x0_wk"] = rows(C(np.concatenate([a["L0_xattn_wk"], a["L0_xattn_bk"][None]], 0).T), 2)
    wv = np.concatenate([a["L0_xattn_wv"], a["L0_xattn_bv"][None]], 0)

    def place(wv, H, dh, hpg):
        o = np.zeros((wv.shape[0], H, 128), f)
        for hh in range(H):
            o[:, hh, dh * (hh % hpg):dh * (hh % hpg) + dh] = wv[:, hh * dh:(hh + 1) * dh]
        return o

    wv = place(wv, 16, 16, 8)
    r["x0_wv1"], r["x0_wv2"] = C(wv[:128]), C(wv[128:])
    r["x0_wo"] = rows(a["L0_xattn_wo"], 2)
    r["a_wq"], r["a_wkv"], r["a_wout"] = rows(a["L0_attn_Wq"], 2), rows(a["L0_attn_Wkv"], 2), rows(a["L0_attn_Wout"], 4)
    r["f_w1"], r["f_w2"] = rows(a["L0_ffn_w1"], 2), rows(a["L0_ffn_w2"], 8)
    r["x1_wq"] = rows(a["L1_xattn_Wq"], 2)
    r["x1_wk"] = rows(C(a["L1_xattn_Wk"].T), 4)
    wv = place(a["L1_xattn_Wv"], 8, 64, 2)
    r["x1_wv1"], r["x1_wv2"] = C(wv[:128]), C(wv[128:])
    r["x1_wo"] = rows(a["L1_xattn_Wo"], 4)
    for k in "kvq":
        r["t_" + k] = rows(C(a["L1_attn_t_" + k].T), 2)
    r["t_W1T"] = rows(C(a["L1_attn_W1"].T), 2)
    r["t_W2T"] = C(a["L1_attn_W2"].T)
    r["t_W2"] = rows(a["L1_attn_W2"], 2)
    r["t_b1"], r["t_b2"] = a["L1_attn_b1"], a["L1_attn_b2"]
    r["m_rw"] = rows(C(a["L1_ffn_router_w"].T), 2)
    r["m_gu"] = C(a["L1_ffn_gate_up_w"].transpose(0, 2, 1).reshape(8, 2, 128, 1536).transpose(0, 2, 1, 3))
    r["m_dn"] = C(a["L1_ffn_down_w"].transpose(0, 2, 1).reshape(8, 6, 128, 256).transpose(0, 2, 1, 3))
    r["m_sgu"] = rows(C(a["L1_ffn_shared_gate_up_w"].T), 2)
    r["m_sdn"] = rows(C(a["L1_ffn_shared_down_w"].T), 2)
    return r


def kernel(**inputs):
    import numpy as np
    import concourse.bacc as bacc
    from concourse.bass_utils import run_bass_kernel_spmd

    nc = bacc.Bacc("TRN2", target_bir_lowering=False, num_devices=1)
    arrays = layout(np, inputs)
    d = {n: nc.dram_tensor("in_" + n, v.shape, mybir.dt.from_np(v.dtype), kind="ExternalInput").ap() for n, v in arrays.items()}
    out = nc.dram_tensor("out_x", (16, 64, 256), F32, kind="ExternalOutput").ap()
    program(nc, d, out)
    r = run_bass_kernel_spmd(nc, [{"in_" + n: v for n, v in arrays.items()}], core_ids=[0])
    return r.results[0]["out_x"]
```

```python
from contextlib import ExitStack

import concourse.bass as bass
from concourse import mybir

F32 = mybir.dt.float32
F32R = mybir.dt.float32r
ALU = mybir.AluOpType
ACT = mybir.ActivationFunctionType
AX = mybir.AxisListType

NB, NQ, D, DC, NK = 16, 64, 256, 192, 1601
NT = 8
KT = 13
NS = 23
KL = NK - 12 * 128


class Sem:

    def __init__(self, handle):
        self.h, self.n = handle, 0


class Queues:

    def __init__(self):
        self.q = {k: [] for k in ("pe", "dve", "act", "pool", "sp")}

    def op(self, eng, fn, *waits, sem=None, inc=1):
        self.q[eng].append((waits, fn, sem, inc))
        if sem is not None:
            sem.n += inc
            return (sem, sem.n)
        return None

    def emit(self, eng, e):
        seen = {}
        for waits, fn, sem, inc in self.q[eng]:
            for w in waits:
                if w is None:
                    continue
                s, n = w
                if seen.get(id(s), 0) < n:
                    e.wait_ge(s.h, n)
                    seen[id(s)] = n
            if fn is None:
                continue
            ins = fn(e)
            if sem is not None:
                ins.then_inc(sem.h, inc)


def program(nc, d, out, stages=6, first=1):
    ctx = ExitStack()
    with ctx:
        def sb(name, shape, dt=F32):
            return ctx.enter_context(nc.sbuf_tensor(name, shape, dt))

        sems = [0]

        def sem(name):
            sems[0] += 1
            return Sem(ctx.enter_context(nc.semaphore(f"s_{name}")))

        Q = Queues()
        op = Q.op
        ps = ctx.enter_context(nc.psum_tensor("ps", [128, 8, 512], F32))
        psf = ps[:, :, :].rearrange("p b n -> p (b n)")

        x = sb("x", [128, NT, D])
        h = sb("h", [128, NT, D])
        hT = sb("hT", [128, 2, NT * 128])
        ident = sb("ident", [128, 128])
        small = sb("small", [128, 512])
        biasb, zeros = sb("biasb", [128, 256]), sb("zeros", [128, 256])
        first_ctx = ExitStack()
        ctx.callback(first_ctx.close)
        arenaR0 = first_ctx.enter_context(nc.sbuf_tensor("arenaR0", [128, 36000], F32R))
        arena0 = first_ctx.enter_context(nc.sbuf_tensor("arena0", [128, 9100], F32))

        class Carve:
            def __init__(self, t, off=0):
                self.t, self.off = t, off

            def __call__(self, parts, *shape):
                n = 1
                for s in shape:
                    n *= s
                v = self.t[0:parts, self.off:self.off + n]
                self.off += n
                if len(shape) == 2:
                    v = v.rearrange("p (a b) -> p a b", b=shape[1])
                elif len(shape) == 3:
                    v = v.rearrange("p (a b c) -> p a b c", b=shape[1], c=shape[2])
                assert self.off <= self.t.shape[1], (self.off, self.t.shape)
                return v

        ar0 = Carve(arena0)
        X0 = {k: ar0(128, 2, 256) for k in ("wq", "wk", "wv", "wo")}

        cc = Carve(small)
        mask0, mask1 = cc(128, 8), cc(128, 2)
        fold, own = cc(128, 64), cc(128, 32)
        bq, bkc, bvc = cc(128, 2), cc(128, 2), cc(128, 2)
        eord = cc(128, 8)
        normw, qg, kg, b1c = cc(128, 2), cc(128, 8), cc(128, 8), cc(128, 8)
        tb1, tb2 = cc(128, 1)[0:64], cc(128, 2)
        lng, lnb = cc(128, 2), cc(128, 2)
        n_const = cc.off
        st, mv = cc(128, NT, 6), cc(128, NT, 2)
        ve, sd, rs = cc(128, NT), cc(128, NT), cc(128, NT)
        ss2 = cc(128, NT)

        s_c, s_x = sem("c"), sem("x")
        xs_d = nc.dram_tensor("xs_rows", (128 * NS, D), F32, kind="Internal").ap()
        ys_d = nc.dram_tensor("ys_rows", (128 * NS, D), F32, kind="Internal").ap()
        s_w = [sem(f"w{i}") for i in range(6)]
        s_bias = [sem(f"bias{i}") for i in range(4)]

        def load(dst, src, s, *waits):
            return op("sp", lambda e: e.dma_start(dst, src), *waits, sem=s, inc=16)

        t_x = load(x[:, :, :], d["x"].rearrange("(t b) n c -> (b n) t c", b=2), s_x)
        load(ident[:, :], d["ident"], s_c)
        t_c = load(small[:, 0:n_const], d["small"], s_c)
        for k in ("wk", "wv"):
            t_w0 = load(X0[k], d["x0_" + k], s_w[0])

        eng_sems = {}

        def fresh(tag):
            old = dict(eng_sems)
            for k in ("pe", "dve", "act", "pool"):
                eng_sems[k] = sem(f"{tag}_{k}")
            if old:
                ends = [(s, s.n) for s in old.values() if s.n]
                for k in ("pe", "dve", "act", "pool"):
                    op(k, None, *ends)
                return ends
            return []

        def pe(fn, *w):
            return op("pe", fn, *w, sem=eng_sems["pe"])

        def dve(fn, *w):
            return op("dve", fn, *w, sem=eng_sems["dve"])

        def act(fn, *w):
            return op("act", fn, *w, sem=eng_sems["act"])

        def pool(fn, *w):
            return op("pool", fn, *w, sem=eng_sems["pool"])

        def mms(outap, pairs, first=True, last=True):
            def f(e):
                n = len(pairs)
                for i, (a, b) in enumerate(pairs):
                    m = e.matmul(outap, a, b, start=(first and i == 0), stop=(last and i == n - 1))
                return m
            return f

        def seq(*fns):
            def f(e):
                for g in fns:
                    m = g(e)
                return m
            return f

        def tr(outap, inap, k=128):
            return lambda e: e.transpose(outap, inap, ident[0:k, 0:k])

        def rsqrt_of(v, n_ap, r_ap, *w):
            a = act(lambda e: e.activation(n_ap, v, ACT.Sqrt), *w)
            return dve(lambda e: e.reciprocal(r_ap, n_ap), a)

        known = {}

        def moments(t, *w):
            a = dve(lambda e: e.bn_stats(st[:, t, :], x[:, t, :]), *w)
            known[t] = dve(lambda e: e.bn_aggr(mv[:, t, :], st[:, t, :]), a)

        def layernorm(*w):
            for t in range(NT):
                if t not in known:
                    moments(t, *w)
            b = known[NT - 1]
            known.clear()
            c = dve(lambda e: e.tensor_scalar(ve, mv[:, :, 1], 1e-5, None, ALU.add), b)
            r = rsqrt_of(ve, sd, rs, c)
            toks = []
            for t in range(NT):
                toks.append(dve(lambda e, t=t: e.tensor_scalar(h[:, t, :], x[:, t, :], mv[:, t, 0:1], rs[:, t:t + 1],
                                                               ALU.subtract, ALU.mult), r))
            return toks

        def to_hT(toks, scale=None, shift=None):
            res = {}
            n = 0
            for half in range(2):
                for k in range(2):
                    bank = n % 2
                    p = pe(seq(*[tr(ps[:, bank, 128 * i:128 * i + 128], h[:, 4 * half + i, 128 * k:128 * k + 128])
                                 for i in range(4)]), toks[4 * half + 3], t_c, res.get(n - 2))
                    o, i_ = hT[:, k, 512 * half:512 * half + 512], ps[:, bank, :]
                    if scale is None:
                        res[n] = act(lambda e, o=o, i_=i_: e.copy(o, i_), p)
                    elif shift is None:
                        res[n] = dve(lambda e, o=o, i_=i_, k=k: e.tensor_scalar(o, i_, scale[:, k:k + 1], None, ALU.mult), p)
                    else:
                        res[n] = dve(lambda e, o=o, i_=i_, k=k: e.tensor_scalar(
                            o, i_, scale[:, k:k + 1], shift[:, k:k + 1], ALU.mult, ALU.add), p)
                    n += 1
            return res[3]

        bias_tok = []

        def load_bias(i, name, *w):
            bias_tok.append(load(biasb[:, :], d[name].partition_broadcast(128), s_bias[i], *w, *bias_tok[-1:]))
            return bias_tok[-1]

        def latents(t_w):
            W = X0
            ar, arr = ar0, Carve(arenaR0)
            raw2, P = ar(128, NK), ar(128, NK)
            c1h, c1l, c2 = [arr(128, KT * 128) for _ in range(3)]
            wh, wl = [{k: arr(128, 2, 256) for k in ("wk", "wv")} for _ in range(2)]
            PTh, PTl = arr(128, KT, 256), arr(128, KT, 256)
            Vh, Vl = [[arr(128, KT, 256) for _ in range(2)] for _ in range(2)]
            vs = [ar(128, 512) for _ in range(4)]
            oS = ar(128, 256)
            O = [ar(128, 8, 32) for _ in range(2)]
            aT = ar(128, 2, 128)
            mx4, mx, sums, rc = [[ar(128, k) for _ in range(2)] for k in (4, 1, 2, 1)]
            Kh, Kl = [[arr(128, NK + 1) for _ in range(2)] for _ in range(2)]
            qh, ql = [[arr(128, 8, 64) for _ in range(2)] for _ in range(2)]
            qTh, qTl = arr(128, 2, 128), arr(128, 2, 128)
            s_raw, s_wq = sem("x0raw"), sem("x0wq")
            for c in (c1h, c1l, c2):
                t_ones = dve(lambda e, c=c: e.memset(c[:, NK:KT * 128].bitcast(F32), 0.0))
            for k in ("wk", "wv"):
                a = act(lambda e, k=k: e.copy(wh[k], W[k]), t_w)
                t_wl = pool(lambda e, k=k: e.tensor_tensor(wl[k], W[k], wh[k], ALU.subtract), a)

            pairs = [(b, j) for b in range(NB) for j in range(8)]
            N = len(pairs)
            raw_tok, split_tok, cread, kt, vt, qt, qTt, bd = {}, {}, {}, {}, {}, {}, {}, {}
            exa, exb, s_tok, tr_done, av, on, turned, aTt, proj, oSt, oSr, rct = {}, {}, {}, {}, {}, {}, {}, {}, {}, {}, {}, {}
            free, vread, ptt = {}, {}, {}

            def raw1(b):
                return P if b == 0 else h[:, :, :].rearrange("p a b -> p (a b)")[:, 0:NK]

            def load_raw(b, *w):
                if b:
                    w += tuple(t for c in range(4) for t in split_tok[b - 1, c])
                load(raw1(b), d["ctxT"][b, 0:128, :], s_raw, *w)
                load(raw2[0:64, :], d["ctxT"][b, 128:192, :], s_raw, *w)
                raw_tok[b] = load(raw2[64:128, :], d["ctxT"][b, 128:192, :], s_raw)

            def split(b, c):
                w = (raw_tok[b], cread.get(b - 1), t_ones)
                k = slice(400 * c, 400 * c + 400 + (c == 3))
                a1 = act(lambda e: e.copy(c1h[:, k], raw1(b)[:, k]), *w)
                a2 = (act if c > 1 else pool)(lambda e: (e.copy if c > 1 else e.tensor_copy)(c2[:, k], raw2[:, k]), *w)
                p1 = pool(lambda e: e.tensor_tensor(c1l[:, k], raw1(b)[:, k], c1h[:, k], ALU.subtract), a1)
                p2 = pool(lambda e: e.tensor_tensor(c2[64:128, k], raw2[64:128, k], c2[64:128, k], ALU.subtract), a2, p1)
                op("pool", None, p2)
                split_tok[b, c] = [a1, p2]

            def keys(b, g, c, bank, early=False):
                k0, n = 400 * c, 400 + 2 * (c == 3)
                k, f = slice(k0, k0 + n), slice(128 * g, 128 * g + 128)
                H, L = wh["wk"], wl["wk"]
                o = ps[:, bank, 0:n]
                p = pe(mms(o, [(H[:, 0, f], c1h[:, k]), (H[:, 0, f], c1l[:, k]), (L[:, 0, f], c1h[:, k]),
                               (H[:, 1, f], c2[:, k]), (L[:, 1, f], c2[:, k])]), *split_tok[b, c], t_wl, free.get(bank))
                cread[b] = p
                w = (p, t_c, s_tok.get(8 * b - 5 + 4 * g))
                if early:
                    a = dve(lambda e: e.tensor_scalar(Kh[g][:, k], o, bkc[:, g:g + 1], None, ALU.add), *w)
                else:
                    a = act(lambda e: e.activation(Kh[g][:, k], o, ACT.Identity, bias=bkc[:, g:g + 1]), *w)
                free[bank] = kt[b, g] = dve(lambda e: e.scalar_tensor_tensor(
                    Kl[g][:, k], o, bkc[:, g:g + 1], Kh[g][:, k], ALU.add, ALU.subtract), a)

            def vals(b, q, bank, early=False):
                H, L = wh["wv"], wl["wv"]
                ts = range(2 * q, min(2 * q + 2, KT))
                fs = []
                for t in ts:
                    k = slice(128 * t, 128 * t + 128)
                    fs.append(mms(ps[:, bank, 256 * (t % 2):256 * (t % 2) + 256],
                                  [(c1h[:, k], H[:, 0, :]), (c1l[:, k], H[:, 0, :]), (c1h[:, k], L[:, 0, :]),
                                   (c2[:, k], H[:, 1, :]), (c2[:, k], L[:, 1, :])]))
                p = pe(seq(*fs), *split_tok[b, min(256 * q // 400, 3)], *split_tok[b, min((256 * q + 255) // 400, 3)], t_wl, free.get(bank))
                cread[b] = p
                r, w, v = (128, 512, vs[q % 4]) if q < 6 else (KL, 256, vs[q % 4])
                o = ps[0:r, bank, 0:w]
                w_ = (p, vread.get(q % 4))
                if early:
                    free[bank] = a = dve(lambda e: e.tensor_copy(v[0:r, 0:w], o), *w_)
                else:
                    free[bank] = a = act(lambda e: e.copy(v[0:r, 0:w], o), *w_)
                H, L = [x_[b % 2][0:r, ts[0]:ts[-1] + 1, :].rearrange("p a c -> p (a c)") for x_ in (Vh, Vl)]
                h_ = pool(lambda e: e.tensor_copy(H, v[0:r, 0:w]), a, av.get(4 * b - 5))
                vt[b] = vread[q % 4] = pool(lambda e: e.tensor_tensor(L, v[0:r, 0:w], H, ALU.subtract), h_)

            def queries(tile, bank=6):
                p = pe(seq(*[mms(ps[:, bank, 128 * g:128 * g + 128],
                                 [(W["wq"][:, k, 128 * g:128 * g + 128], hT[:, k, 128 * tile:128 * tile + 128])
                                  for k in range(2)]) for g in range(2)]), t_h, t_w, free.get(bank))
                w = (p, t_c, bd.get((2 * tile - 1, 1)))
                for g in range(2):
                    o = ps[:, bank, 128 * g:128 * g + 128]
                    a = act(lambda e, g=g, o=o: e.activation(qTh[:, g, :], o, ACT.Identity, bias=bq[:, g:g + 1]), *w)
                for g in range(2):
                    o = ps[:, bank, 128 * g:128 * g + 128]
                    a = dve(lambda e, g=g, o=o: e.scalar_tensor_tensor(qTl[:, g, :], o, bq[:, g:g + 1], qTh[:, g, :],
                                                                       ALU.add, ALU.subtract), a)
                qTt[tile] = free[bank] = a

            def blockdiag(b, g):
                c = slice(64 * (b % 2), 64 * (b % 2) + 64)
                for q, s in ((qh, qTh), (ql, qTl)):
                    bd[b, g] = pool(lambda e, q=q, s=s: e.tensor_tensor(
                        q[g], s[:, g, c].unsqueeze(1).broadcast_to([128, 8, 64]),
                        mask0.unsqueeze(2).broadcast_to([128, 8, 64]), ALU.mult), qTt[b // 2], t_c, s_tok.get(8 * b - 5 + 4 * g))

            def turn_p(n, g):
                bank = 4 + g % 2
                fs = []
                for t in range(4 * g, min(4 * g + 4, KT)):
                    k = 128 if t < 12 else KL
                    fs.append(tr(ps[0:k, bank, 128 * (t % 4):128 * (t % 4) + 128], P[:, 128 * t:128 * t + k]))
                tr_done[n] = p = pe(seq(*fs), exa[n], exb[n], free.get(bank))
                k, c = (128, 512) if g < 3 else (KL, 128)
                H, L = [x_[0:k, 4 * g:4 * g + c // 128, 128 * (n % 2):128 * (n % 2) + 128] for x_ in (PTh, PTl)]
                src = ps[0:k, bank, 0:c].rearrange("p (a c) -> p a c", c=128)
                a = act(lambda e: e.copy(H, src), p, av.get(n // 2 - 1))
                free[bank] = ptt[n, g] = dve(lambda e: e.tensor_tensor(L, src, H, ALU.subtract), a)

            def scores(n, c):
                b, j = pairs[n]
                g = j // 4
                w = 400 + 2 * (c == 3)
                k = slice(400 * c, 400 * c + w)
                m = slice(2 * (j % 4), 2 * (j % 4) + 2)
                H, L = [q[g][:, m, :].rearrange("p a b -> p (a b)") for q in (qh, ql)]
                s_tok[n] = pe(mms(ps[:, c, 0:w], [(H, Kh[g][:, k]), (H, Kl[g][:, k]), (L, Kh[g][:, k])]),
                              (exa if c < 3 else exb).get(n - 1, free.get(c)), bd[b, g], kt[b, g])
                dve(lambda e: e.tensor_reduce(mx4[n % 2][:, c:c + 1], ps[:, c, 0:400 + (c == 3)], AX.X, ALU.max),
                    s_tok[n], exb.get(n - 2))

            def softmax(n):
                m = dve(lambda e: e.tensor_reduce(mx[n % 2], mx4[n % 2], AX.X, ALU.max, negate=True), (eng_sems["dve"], eng_sems["dve"].n))
                exa[n] = act(lambda e: e.activation(P[:, 0:1200].rearrange("p (a b) -> p a b", b=400), ps[:, 0:3, 0:400], ACT.Exp,
                                                    bias=mx[n % 2], accum_out=sums[n % 2][:, 0:1]),
                             m, tr_done.get(n - 1), *(split_tok[0, 3] if n == 0 else ()))
                exb[n] = act(lambda e: e.activation(P[:, 1200:NK], ps[:, 3, 0:401], ACT.Exp, bias=mx[n % 2],
                                                    accum_out=sums[n % 2][:, 1:2]), m)

            def values(m):
                b, g = m // 4, (m // 2) % 2
                o = ps[:, 7, 0:256]
                f = slice(128 * g, 128 * g + 128)
                for t in range(KT):
                    r = 128 if t < 12 else KL
                    H, L = Vh[b % 2][0:r, t, f], Vl[b % 2][0:r, t, f]
                    av[m] = pe(mms(o, [(H, PTh[0:r, t, :]), (H, PTl[0:r, t, :]), (L, PTh[0:r, t, :])], t == 0, t == KT - 1),
                               ptt[2 * m + 1, t // 4], free.get(7), vt[b])
                free[7] = oSt[m] = dve(lambda e: e.tensor_copy(oS, o), av[m], oSr.get(m - 1))

            def normalise(m):
                b = m // 4
                o = ps[:, 7, 0:256]
                oSr[m] = p = pe(seq(*[tr(o[:, 128 * i:128 * i + 128], oS[:, 128 * i:128 * i + 128]) for i in range(2)]), oSt[m], free[7])
                for i in range(2):
                    n = 2 * m + i
                    j = n % 8
                    free[7] = on[n] = dve(lambda e, i=i, j=j: e.scalar_tensor_tensor(
                        O[b % 2][:, j, :], o[:, 128 * i + 32 * (j % 4):128 * i + 32 * (j % 4) + 32], rc[i], own, ALU.mult, ALU.mult),
                        p, rct[n], t_c, turned.get((b - 2, 1)))

            def total(n):
                s_, r = sums[n % 2], rc[n % 2]
                a = dve(lambda e: e.tensor_tensor(r, s_[:, 0:1], s_[:, 1:2], ALU.add), exb[n], on.get(n - 2))
                rct[n] = dve(lambda e: e.reciprocal(r, r), a)

            def turn(b, g):
                o = ps[:, 6, 0:64]
                turned[b, g] = p = pe(mms(o, [(O[b % 2][:, 4 * g:4 * g + 4, :].rearrange("p a c -> p (a c)"), fold)]),
                                      on[8 * b + 4 * g + 3], free[6], t_c)
                free[6] = aTt[b, g] = dve(lambda e: e.tensor_scalar(aT[:, g, 64 * (b % 2):64 * (b % 2) + 64], o, bvc[:, g:g + 1], None, ALU.add),
                                          p, t_c, proj.get(b // 2 - 1))

            def project(tile):
                o = ps[:, 6, 0:256]
                proj[tile] = p = pe(mms(o, [(aT[:, g, :], W["wo"][:, g, :]) for g in range(2)]), free[6])
                free[6] = dve(lambda e: e.tensor_tensor(x[:, tile, :], o, x[:, tile, :], ALU.add), p, xb, toks[-1])
                moments(tile, free[6])

            load_raw(0)
            for k in ("wq", "wo"):
                t_w = load(W[k], d["x0_" + k], s_wq)
            t_b = load_bias(0, "x0_bo")
            t_zero = load(xs_d.rearrange("(i p) c -> p i c", p=128), zeros[:, :].unsqueeze(1).broadcast_to([128, NS, D]), s_zero, t_z)
            for c in range(4):
                split(0, c)
            toks = layernorm(t_x)
            for c in range(4):
                keys(0, 0, c, 2 + c)
            for q in range(2):
                vals(0, q, 6 + q)
            t_h = to_hT(toks)
            xb = pool(lambda e: e.tensor_tensor(x[:, :, :], x[:, :, :],
                                                biasb[:, :].unsqueeze(1).broadcast_to([128, NT, D]), ALU.add), t_b, toks[-1])
            queries(0)
            blockdiag(0, 0)
            load_raw(1, t_h)
            for q in range(2, 7):
                vals(0, q, 2 + q % 4)

            for n in range(N + 1):
                b, j = pairs[n] if n < N else (NB, 0)
                jobs = []
                if b < NB and j == 1:
                    jobs = [lambda c=c: keys(b, 1, c, 4 + c, c < 2) for c in range(4)]
                elif b + 1 < NB and j == 3:
                    jobs = [lambda q=q: vals(b + 1, q, 4 + q, q < 4) for q in range(4)]
                elif b + 1 < NB and j == 5:
                    jobs = [lambda c=c: keys(b + 1, 0, c, 4 + c, c < 2) for c in range(4)]
                elif b + 1 < NB and j == 7:
                    jobs = [lambda q=q: vals(b + 1, q, q, q < 5) for q in range(4, 7)]
                if j == 0 and b < NB:
                    blockdiag(b, 1)
                if j == 4 and b + 1 < NB:
                    blockdiag(b + 1, 0)
                if n >= 1:
                    turn_p(n - 1, 0)
                    turn_p(n - 1, 1)
                if n < N:
                    scores(n, 0)
                    scores(n, 1)
                if n >= 3 and n % 2 == 1:
                    normalise((n - 3) // 2)
                if n >= 4 and n % 4 == 2:
                    b2, j2 = pairs[n - 3]
                    turn(b2, j2 // 4)
                if n >= 1:
                    turn_p(n - 1, 2)
                if n < N:
                    scores(n, 2)
                if j == 3:
                    if b + 2 < NB:
                        load_raw(b + 2)
                if n >= 1:
                    turn_p(n - 1, 3)
                if n < N:
                    scores(n, 3)
                    softmax(n)
                if j == 2 and b + 1 < NB:
                    for c in range(4):
                        split(b + 1, c)
                for f in jobs:
                    f()
                if n >= 1:
                    total(n - 1)
                if n >= 3 and b % 2 == 0 and j == 2:
                    project(b // 2 - 1)
                if j == 2 and b % 2 == 1 and b + 1 < NB:
                    queries((b + 1) // 2)
                if n >= 1 and n % 2 == 0:
                    values(n // 2 - 1)
            normalise(N // 2 - 1)
            turn(NB - 1, 1)
            project(NT - 1)
            return t_b, t_zero, [cread[NB - 1]]

        def xattn(tag, W, G, hpg, mask, t_w, t_b):
            H = G * hpg
            NP = H // 2
            PPG = hpg // 2
            NH = hpg * 64
            aw, ar, arr = Carve(wsb[:, 0:9216]), Carve(arena), Carve(arenaR)
            raw1 = h[:, :, :].rearrange("p a b -> p (a b)")[:, 0:NK]
            raw2, P, rawn = aw(128, NK), aw(128, NK), aw(128, KT, 192)
            qT = [aw(128, G, 128) for _ in range(2)]
            qbd = [aw(128, H, 64) for _ in range(2)]
            oT1, oT2 = aw(128, H, 128), ar(64, H, 128)
            On = [ar(128, 192) for _ in range(2)]
            Ol = ar(128, 192)
            aT = ar(128, G, 128)
            mx4, mx = [ar(128, 4) for _ in range(2)], [ar(128, 1) for _ in range(2)]
            rc = [ar(128, 1) for _ in range(2)]
            c1h, c1l, c2 = [[arr(128, NK + 1) for _ in range(2)] for _ in range(3)]
            cN = [arr(128, KT, 386) for _ in range(2)]
            PTh, PTl = [arr(128, KT, 128) for _ in range(2)]
            qh, ql = [arr(128, 2, H * 64) for _ in range(2)]
            s_raw = sem(f"{tag}raw")
            s_cn = sem(f"{tag}cn")

            toks = layernorm(t_x)
            xb = pool(lambda e: e.tensor_tensor(x[:, :, :], x[:, :, :],
                                                biasb[:, :].unsqueeze(1).broadcast_to([128, NT, D]), ALU.add), t_b, toks[-1])
            t_h = to_hT(toks)
            for i in range(2):
                for col, v in ((192, 1.0), (193, 0.0)):
                    dve(lambda e, i=i, col=col, v=v: e.memset(cN[i][:, :, col:col + 1].bitcast(F32), v))
                for c in (c1h, c1l, c2):
                    t_ones = dve(lambda e, i=i, c=c: e.memset(c[i][:, NK:NK + 1].bitcast(F32), 0.0))

            pairs = [(b, j) for b in range(NB) for j in range(NP)]
            N = len(pairs)
            raw_tok, cn_tok, split_tok, part_tok = {}, {}, {}, {}
            exa, exb, s_tok, tr_done, av, on, otr, oTt = {}, {}, {}, {}, {}, {}, {}, {}
            qTt, qd, qq, atile = {}, {}, {}, {}
            qread = {}
            evs = [None, None]
            xfree = [None]
            at_free = [None]

            def load_raw(b):
                w = [t for c in range(4) for t in split_tok[b - 1, c]] if b else (t_h,)
                load(raw1, d["ctxT"][b, 0:128, :], s_raw, *w)
                load(raw2[0:64, :], d["ctxT"][b, 128:192, :], s_raw, *w)
                raw_tok[b] = load(raw2[64:128, :], d["ctxT"][b, 128:192, :], s_raw)

            def load_cn(b):
                w = part_tok.get(b - 1, t_ones)
                load(rawn[:, 0:12, :], d["ctx"][b, 0:1536, :].rearrange("(t p) c -> p t c", p=128), s_cn, w)
                cn_tok[b] = load(rawn[0:KL, 12, :], d["ctx"][b, 1536:NK, :], s_cn)

            def split_keys(b, c):
                o = cN[b % 2]
                w = (cn_tok[b], av.get((b - 1) * NP - 1))
                t0, t1 = (0, 4, 7, 10)[c], (4, 7, 10, 12)[c]
                for k, t in [(128, slice(t0, t1))] + ([(KL, slice(12, 13))] if c == 3 else []):
                    p = pool(lambda e, k=k, t=t: e.tensor_copy(o[0:k, t, 0:192], rawn[0:k, t, :]), *w)
                    part_tok[b] = pool(lambda e, k=k, t=t: e.tensor_tensor(o[0:k, t, 194:386], rawn[0:k, t, :],
                                                                           o[0:k, t, 0:192], ALU.subtract), p)

            def split(b, c):
                i = b % 2
                k = slice(400 * c, 400 * c + 400 + (c == 3))
                w = (raw_tok[b], s_tok.get((b - 1) * NP - 1), t_ones)
                a1 = act(lambda e: e.copy(c1h[i][:, k], raw1[:, k]), *w)
                a2 = act(lambda e: e.copy(c2[i][:, k], raw2[:, k]), *w)
                p1 = pool(lambda e: e.tensor_tensor(c1l[i][:, k], raw1[:, k], c1h[i][:, k], ALU.subtract), a1)
                split_tok[b, c] = [a1, p1, a2]

            def split_low(b, c):
                i = b % 2
                k = slice(400 * c, 400 * c + 400 + (c == 3))
                t = split_tok[b, c]
                t[2] = dve(lambda e: e.tensor_tensor(c2[i][64:128, k], raw2[64:128, k], c2[i][64:128, k], ALU.subtract), t[2])

            def queries(tile):
                i = tile % 2
                p = pe(seq(*[mms(ps[:, 7, 128 * g:128 * g + 128],
                                 [(W["wq"][:, k, 128 * g:128 * g + 128], hT[:, k, 128 * tile:128 * tile + 128])
                                  for k in range(2)]) for g in range(G)]), t_h, t_w, xfree[0])
                src = ps[:, 7, 0:128 * G].rearrange("p (g n) -> p g n", n=128)
                w = (p, qd.get(2 * tile - 3))
                t = dve(lambda e: e.tensor_copy(qT[i], src), *w)
                qTt[tile] = xfree[0] = t

            def blockdiag(b):
                i = b % 2
                s = qT[(b // 2) % 2][:, :, 64 * i:64 * i + 64]
                for g in range(G):
                    t = pool(lambda e, g=g: e.tensor_tensor(
                        qbd[i][:, g * hpg:(g + 1) * hpg, :], s[:, g, :].unsqueeze(1).broadcast_to([128, hpg, 64]),
                        mask.unsqueeze(2).broadcast_to([128, hpg, 64]), ALU.mult), qTt[b // 2], qread.get(b - 2), t_c)
                qd[b] = t

            def absorb(b, g):
                i = b % 2
                qs = qbd[i][:, g * hpg:(g + 1) * hpg, :].rearrange("p a b -> p (a b)")
                sl = slice(g * NH, (g + 1) * NH)
                w = s_tok.get((b - 1) * NP + (g + 1) * PPG - 1) if b else None
                p = pe(seq(*[mms(ps[:, 7, NH * part:NH * part + NH], [(W["wk"][:, g, 128 * part:128 * part + 128], qs)])
                             for part in range(2)]), qd[b], xfree[0], t_w)
                o = ps[:, 7, 0:2 * NH].rearrange("p (a c) -> p a c", c=NH)
                a = act(lambda e: e.copy(qh[:, :, sl], o), p, w)
                xfree[0] = dve(lambda e: e.tensor_tensor(ql[:, :, sl], o, qh[:, :, sl], ALU.subtract), a)
                qread[b] = p
                qq[b, g] = xfree[0]

            def turn_p(n, g):
                bank = 4 + g % 2
                fs = []
                for t in range(4 * g, min(4 * g + 4, KT)):
                    k = 128 if t < 12 else KL
                    fs.append(tr(ps[0:k, bank, 128 * (t % 4):128 * (t % 4) + 128], P[:, 128 * t:128 * t + k]))
                p = pe(seq(*fs), exa[n], exb[n], evs[g % 2])
                k, c = (128, 512) if g < 3 else (KL, 128)
                hi, lo = [v[0:k, 4 * g:4 * g + c // 128, :].rearrange("p a b -> p (a b)") for v in (PTh, PTl)]
                src = ps[0:k, bank, 0:c]
                a = act(lambda e: e.copy(hi, src), p, av.get(n - 1))
                evs[g % 2] = dve(lambda e: e.tensor_tensor(lo, src, hi, ALU.subtract), a)
                tr_done[n] = p

            def scores(n, c):
                b, j = pairs[n]
                i = b % 2
                g = j // PPG
                k0, k1 = 400 * c, 400 * c + (400 if c < 3 else 402)
                m = slice(128 * j, 128 * j + 128)
                k = slice(k0, k1)
                s_tok[n] = pe(mms(ps[:, c, 0:k1 - k0], [(qh[:, 0, m], c1h[i][:, k]), (qh[:, 0, m], c1l[i][:, k]), (ql[:, 0, m], c1h[i][:, k]),
                                                        (qh[:, 1, m], c2[i][:, k]), (ql[:, 1, m], c2[i][:, k])]),
                              exa.get(n - 1) if c < 3 else exb.get(n - 1), qq[b, g], *split_tok[b, c], t_ones)
                dve(lambda e: e.tensor_reduce(mx4[n % 2][:, c:c + 1], ps[:, c, 0:400 + (c == 3)], AX.X, ALU.max),
                    s_tok[n], exb.get(n - 2))

            def softmax(n):
                m = dve(lambda e: e.tensor_reduce(mx[n % 2], mx4[n % 2], AX.X, ALU.max, negate=True), (eng_sems["dve"], eng_sems["dve"].n))
                bias = mx[n % 2]
                exa[n] = act(lambda e: e.activation(P[:, 0:1200].rearrange("p (a b) -> p a b", b=400), ps[:, 0:3, 0:400], ACT.Exp, bias=bias),
                             m, tr_done.get(n - 1))
                exb[n] = act(lambda e: e.activation(P[:, 1200:NK], ps[:, 3, 0:401], ACT.Exp, bias=bias), m)

            def values(n):
                b, j = pairs[n]
                o, c = ps[:, 6, 0:386], cN[b % 2]

                def f(e):
                    for t in range(KT):
                        k = 128 if t < 12 else KL
                        two = [(o, PTh, 386), (o[:, 0:256], PTl, 256)]
                        for i, (ot, pt, w) in enumerate(two if t < 12 else two[::-1]):
                            m = e.matmul(ot, pt[0:k, t, :], c[0:k, t, 0:w], start=(t + i == 0), stop=(t + i == 13))
                    return m
                av[n] = pe(f, evs[0], evs[1], on.get(n - 1), part_tok[b], t_ones)
                r = dve(lambda e: e.reciprocal(rc[n % 2], o[:, 192:193]), av[n])
                r = dve(lambda e: e.tensor_scalar(Ol, o[:, 194:386], rc[n % 2], None, ALU.mult), r)
                on[n] = dve(lambda e: e.scalar_tensor_tensor(On[n % 2], o[:, 0:192], rc[n % 2], Ol, ALU.mult, ALU.add), r, otr.get(n - 2))

            def turn(n):
                b, j = pairs[n]
                o1, o2 = ps[:, 7, 0:128], ps[0:64, 7, 128:256]
                p = pe(seq(tr(o1, On[n % 2][:, 0:128]), tr(o2, On[n % 2][:, 128:128 + 64])), on[n], xfree[0])
                otr[n] = p
                c = 64 * (b % 2)
                w = (p, atile.get(b // 2 - 1))
                dve(lambda e: e.tensor_copy(oT1[:, 2 * j:2 * j + 2, c:c + 64], o1.rearrange("p (a q) -> p a q", a=2)), *w)
                xfree[0] = oTt[n] = dve(lambda e: e.tensor_copy(oT2[0:64, 2 * j:2 * j + 2, c:c + 64],
                                                                o2.rearrange("p (a q) -> p a q", a=2)), *w)

            def project(tile):
                last = oTt[(2 * tile + 2) * NP - 1]
                fs = []
                for g in range(G):
                    prs = []
                    for hh in range(g * hpg, (g + 1) * hpg):
                        prs += [(W["wv1"][:, hh, :], oT1[:, hh, :]), (W["wv2"][0:64, hh, :], oT2[0:64, hh, :])]
                    fs.append(mms(ps[:, 7, 128 * g:128 * g + 128], prs))
                p = pe(seq(*fs), last, xfree[0])
                atile[tile] = p
                c = act(lambda e: e.copy(aT.rearrange("p a b -> p (a b)"), ps[:, 7, 0:128 * G]), p, at_free[0])
                o = ps[:, 7, 0:256]
                p = pe(mms(o, [(aT[:, g, :], W["wo"][:, g, :]) for g in range(G)]), c)
                at_free[0] = p
                xfree[0] = dve(lambda e: e.tensor_tensor(x[:, tile, :], o, x[:, tile, :], ALU.add), p, xb, toks[-1])
                moments(tile, xfree[0])

            load_raw(0)
            load_cn(0)
            for c in range(4):
                split(0, c)
            for c in range(4):
                split_low(0, c)
            load_raw(1)
            queries(0)
            blockdiag(0)
            for g in range(G):
                absorb(0, g)
            for c in range(4):
                split_keys(0, c)
            load_cn(1)

            for n in range(N + 1):
                if n < N:
                    b, j = pairs[n]
                    if j == 0 and b + 1 < NB:
                        if (b + 1) % 2 == 0:
                            queries((b + 1) // 2)
                        blockdiag(b + 1)
                if n >= 1:
                    turn_p(n - 1, 0)
                    turn_p(n - 1, 1)
                if n < N:
                    scores(n, 0)
                    scores(n, 1)
                if n >= 1:
                    turn_p(n - 1, 2)
                    turn_p(n - 1, 3)
                if n < N:
                    scores(n, 2)
                    scores(n, 3)
                    softmax(n)
                    if b + 1 < NB:
                        split(b + 1, j)
                if n >= 2:
                    turn(n - 2)
                    b2, j2 = pairs[n - 2]
                    if j2 == NP - 1 and b2 % 2 == 1:
                        project(b2 // 2)
                if n < N and b + 1 < NB:
                    split_low(b + 1, j)
                if n >= 1:
                    values(n - 1)
                if n < N and b + 1 < NB:
                    split_keys(b + 1, j)
                    if j == 3 and b + 2 < NB:
                        load_raw(b + 2)
                        load_cn(b + 2)
                    absorb(b + 1, j)
            turn(N - 1)
            project(NT - 1)

        fresh("x0")
        s_zero = sem("zero")
        t_z = pool(lambda e: e.memset(zeros[:, :], 0.0))
        if first <= 1:
            t_b, t_zero, t_early = latents(t_w0)
        else:
            t_zero = load(xs_d.rearrange("(i p) c -> p i c", p=128), zeros[:, :].unsqueeze(1).broadcast_to([128, NS, D]), s_zero, t_z)
            t_b, t_early = load_bias(0, "x0_bo"), []

        t_end = fresh("x0e")
        first_ctx.close()
        second_ctx = ExitStack()
        ctx.callback(second_ctx.close)
        wsb = second_ctx.enter_context(nc.sbuf_tensor("wsb", [128, 14400], F32))
        wc = Carve(wsb)
        aWq, aWkv, aWout = wc(128, 2, 1024), wc(128, 2, 1024), wc(128, 4, 256)
        fw1, fw2 = wc(128, 2, 1024), wc(128, 8, 256)
        X1 = dict(wq=wc(128, 2, 512), wk=wc(128, 4, 256), wv1=wc(128, 8, 128), wv2=wc(64, 8, 128), wo=wc(128, 4, 256))

        for dst, n in ((aWq, "a_wq"), (aWkv, "a_wkv"), (aWout, "a_wout")):
            t_w1 = load(dst, d[n], s_w[1], *t_early)
        for dst, n in ((fw1, "f_w1"), (fw2, "f_w2")):
            t_w2 = load(dst, d[n], s_w[2], *t_end)

        def load_x1(*w):
            for k in ("wq", "wk", "wv1", "wv2", "wo"):
                t = load(X1[k], d["x1_" + k], s_w[3], *w)
            return t

        if first > 1:
            for k in ("pe", "dve", "act", "pool", "sp"):
                op(k, None, t_x, t_c, t_w0, t_w1, t_w2, t_b)
        if first == 4:
            tw1 = load_x1()

        def selfattn(arena):
            ends = fresh("sa")
            ar, ah = Carve(arena), Carve(h[:, :, :].rearrange("p a b -> p (a b)"))
            caus = ar(128, 128)
            t_cm = load(caus, d["causal"], s_cm, *ends)
            qk = ar(128, NT, 24, 64)
            vx = ar(128, NT, 8, 65)
            s1, s2, s3 = ar(128, NT, 24), ar(128, NT, 24), ar(128, NT, 24)
            kn = [ar(128, 8, 2, 64) for _ in range(2)]
            qTs, kTs = [ar(128, 8, 128) for _ in range(2)], [ar(128, 8, 128) for _ in range(2)]
            E = [ar(128, 16, 128) for _ in range(2)]
            rr = [ar(128, 16) for _ in range(2)]
            sq = [ar(128, 24, 64) for _ in range(2)]
            junk = ar(128, 2, 256)
            o1, o2, oT = ah(128, 16, 64), ah(128, 8, 64), ah(128, 4, 128)
            g1 = dve(lambda e: e.tensor_scalar(qg, qg, 1.0, 8.0, ALU.add, ALU.mult), t_c)
            g2 = dve(lambda e: e.tensor_scalar(kg, kg, 1.0, 8.0, ALU.add, ALU.mult), t_c)
            g2 = dve(lambda e: e.tensor_tensor(qg, qg, kg, ALU.mult), g1, g2)
            pone = pool(lambda e: e.memset(vx[:, :, :, 64:65], 1.0))
            toks = layernorm()
            a = None
            for t in range(NT):
                a = dve(lambda e, t=t: e.tensor_tensor_reduce(junk[:, t % 2, :], h[:, t, :], h[:, t, :], 1.0, 0.0, ALU.mult, ALU.add,
                                                              ss2[:, t:t + 1]), toks[-1], a if t > 1 else None)
            a = dve(lambda e: e.tensor_scalar(ve, ss2, 1.0 / D, 1.1920929e-07, ALU.mult, ALU.add), a)
            r = rsqrt_of(ve, sd, rs, a)
            for t in range(NT):
                toks[t] = dve(lambda e, t=t: e.tensor_scalar(h[:, t, :], h[:, t, :], rs[:, t:t + 1], None, ALU.mult), r)
            t_h = to_hT(toks, scale=normw)
            free = {b: t_h for b in range(8)}
            sqread, sqsum, vt, qn, knt, knr, ev, st_, ex, ms, on, oread = {}, {}, {}, {}, {}, {}, {}, {}, {}, {}, {}, {}

            def at(i):
                return 8 * (i % 2) + i // 2

            def bank(t, i):
                return 4 * (t % 2) + i

            def place(t, i, n=128):
                return psf[:, 2048 * (t % 2) + 128 * i:2048 * (t % 2) + 128 * i + n]

            def project(t):
                b0 = bank(t, 0)
                hs = [hT[:, k, 128 * t:128 * t + 128] for k in range(2)]
                fs = [mms(ps[:, b0 + c, :], [(hs[k], aWq[:, k, 512 * c:512 * c + 512]) for k in range(2)]) for c in range(2)]
                fs += [mms(ps[:, b0 + 2 + c, :], [(hs[k], aWkv[:, k, 512 * c:512 * c + 512]) for k in range(2)]) for c in range(2)]
                p = pe(seq(*fs), t_h, t_w1, *[free[b0 + i] for i in range(4)])
                src = psf[:, 512 * b0:512 * b0 + 1536].rearrange("p (a c) -> p a c", c=64)
                c = dve(lambda e: e.tensor_copy(qk[:, t, :, :], src), p)
                a = act(lambda e: e.activation(sq[t % 2], src, ACT.Square), p, sqsum.get(t - 2), c)
                vt[t] = act(lambda e: e.copy(vx[:, t, :, 0:64], ps[:, b0 + 3, :].rearrange("p (a c) -> p a c", c=64)), p)
                for i in range(4):
                    free[b0 + i] = vt[t]
                sqsum[t] = dve(lambda e: e.tensor_reduce(s1[:, t, :], sq[t % 2], AX.X, ALU.add), a)

            def norms(half):
                u = slice(4 * half, 4 * half + 4)
                c = act(lambda e: e.activation(s2[:, u, :], s1[:, u, :], ACT.Sqrt), sqsum[4 * half + 3])
                c = dve(lambda e: e.tensor_scalar(s2[:, u, :], s2[:, u, :], 1e-12, None, ALU.max), c)
                return dve(lambda e: e.reciprocal(s3[:, u, :], s2[:, u, :]), c)

            def normalise(t, w):
                for i in range(2):
                    knt[t] = pool(lambda e, i=i: e.tensor_tensor(kn[t % 2][:, :, i, :], qk[:, t, 16:24, :],
                                                                 s3[:, t, 16:24].unsqueeze(2).broadcast_to([128, 8, 64]), ALU.mult),
                                  w, knr.get(t - 2))
                qn[t] = pool(lambda e: e.tensor_tensor(qk[:, t, 0:16, :], qk[:, t, 0:16, :],
                                                       s3[:, t, 0:16].unsqueeze(2).broadcast_to([128, 16, 64]), ALU.mult), w)

            def turn_q(t):
                b0 = bank(t, 0)
                p = pe(seq(*[tr(place(t, i), qk[:, t, 2 * i:2 * i + 2, :].rearrange("p a c -> p (a c)")) for i in range(8)]),
                       qn[t], free[b0], free[b0 + 1])
                free[b0] = free[b0 + 1] = ev[t, 0] = dve(lambda e: e.tensor_tensor(
                    qTs[t % 2], place(t, 0, 1024).rearrange("p (a c) -> p a c", c=128), qg.unsqueeze(2).broadcast_to([128, 8, 128]), ALU.mult),
                    p, g2, st_.get(t - 2))

            def turn_k(t):
                b0 = bank(t, 0)
                p = pe(seq(*[tr(place(t, 8 + i), kn[t % 2][:, i, :, :].rearrange("p a c -> p (a c)")) for i in range(8)]),
                       knt[t], free[b0 + 2], free[b0 + 3])
                knr[t] = p
                free[b0 + 2] = free[b0 + 3] = ev[t, 1] = act(lambda e: e.copy(
                    kTs[t % 2], place(t, 8, 1024).rearrange("p (a c) -> p a c", c=128)), p, st_.get(t - 2))

            def scores(t):
                b, b0 = t % 2, bank(t, 0)
                for half in range(2):
                    st_[t] = p = pe(seq(*[mms(place(t, at(i)), [(kTs[b][64 * half:64 * half + 64, i // 2, :],
                                                                 qTs[b][64 * half:64 * half + 64, i // 2, :])])
                                          for i in range(half, 16, 2)]), ev[t, 0], ev[t, 1], free[b0 + 2 * half], free[b0 + 2 * half + 1])
                    Eh = E[b][:, 8 * half:8 * half + 8, :]
                    a = act(lambda e, half=half, Eh=Eh: e.activation(Eh, place(t, 8 * half, 1024).rearrange("p (a c) -> p a c", c=128),
                                                                     ACT.Tanh, scale=1.0 / 50.0), p, oread.get(t - 2))
                    free[b0 + 2 * half] = free[b0 + 2 * half + 1] = a
                    a = act(lambda e, Eh=Eh: e.activation(Eh, Eh, ACT.Exp, scale=6.25), a)
                    ms[t, half] = dve(lambda e, Eh=Eh: e.tensor_tensor(Eh, Eh, caus.unsqueeze(1).broadcast_to([128, 8, 128]), ALU.mult), a, t_cm)

            def output(t):
                b, b0 = t % 2, bank(t, 0)
                for half in range(2):
                    p = pe(seq(*[mms(place(t, at(i), 65), [(E[b][:, at(i), :], vx[:, t, i // 2, :])]) for i in range(half, 16, 2)]),
                           ms[t, half], vt[t], pone, free[b0 + 2 * half], free[b0 + 2 * half + 1])
                    oread[t] = p
                    OO = place(t, 8 * half, 1024).rearrange("p (a c) -> p a c", c=128)
                    u = slice(8 * half, 8 * half + 8)
                    r = dve(lambda e, OO=OO, u=u: e.reciprocal(rr[b][:, u], OO[:, :, 64]), p)
                    r = dve(lambda e, OO=OO, u=u: e.tensor_tensor(o1[:, u, :], OO[:, :, 0:64],
                                                                  rr[b][:, u].unsqueeze(2).broadcast_to([128, 8, 64]), ALU.mult), r)
                    free[b0 + 2 * half] = free[b0 + 2 * half + 1] = r
                on[t] = dve(lambda e: e.tensor_tensor(o2, o1[:, 0:8, :], o1[:, 8:16, :], ALU.add), r, last[0])

            def finish(t):
                b0 = bank(t, 0)
                p = pe(seq(*[tr(ps[:, b0 + 3, 128 * i:128 * i + 128], o2[:, 2 * i:2 * i + 2, :].rearrange("p a c -> p (a c)"))
                             for i in range(4)]), on[t], free[b0 + 3])
                last[0] = p
                c = free[b0 + 3] = act(lambda e: e.copy(oT.rearrange("p a c -> p (a c)"), ps[:, b0 + 3, :]), p, last[1])
                last[1] = p = pe(mms(ps[:, b0 + 2, 0:256], [(oT[:, k, :], aWout[:, k, :]) for k in range(4)]), c, free[b0 + 2])
                free[b0 + 2] = dve(lambda e: e.tensor_tensor(x[:, t, :], ps[:, b0 + 2, 0:256], x[:, t, :], ALU.add), p)
                moments(t, free[b0 + 2])

            last = [None, None]
            for t in range(4):
                project(t)
            w = norms(0)
            for t in range(4):
                normalise(t, w) if t < 2 else None
                project(4 + t)
            w2 = norms(1)
            turn_q(0)
            turn_k(0)
            scores(0)
            for t in range(1, NT + 2):
                if t < NT:
                    turn_q(t)
                if t >= 2:
                    finish(t - 2)
                if t < NT:
                    turn_k(t)
                    if t + 1 < NT:
                        normalise(t + 1, w if t + 1 < 4 else w2)
                if t - 1 < NT:
                    output(t - 1)
                if t < NT:
                    scores(t)

        def ffn(arena):
            ends = fresh("ff")
            tw = load_x1(*ends)
            t_b = load_bias(1, "f_b2", *ends)
            ar = Carve(arena)
            gT = ar(128, 8, 1024)
            toks = layernorm()
            xb = pool(lambda e: e.tensor_tensor(x[:, :, :], x[:, :, :],
                                                biasb[:, :].unsqueeze(1).broadcast_to([128, NT, D]), ALU.add), t_b, toks[-1])
            t_h = to_hT(toks)
            g = {}
            n = 0
            for half in range(2):
                for f in range(8):
                    bank = 2 + n % 4
                    p = pe(mms(ps[:, bank, :], [(fw1[:, k, 128 * f:128 * f + 128], hT[:, k, 512 * half:512 * half + 512])
                                                for k in range(2)]), t_h, t_w2, g.get(n - 4))
                    g[n] = act(lambda e, f=f, half=half, bank=bank: e.activation(
                        gT[:, f, 512 * half:512 * half + 512], ps[:, bank, :], ACT.Gelu, bias=b1c[:, f:f + 1]), p)
                    n += 1
            y = {}
            for t in range(NT):
                bank = 6 + t % 2
                p = pe(mms(ps[:, bank, 0:256], [(gT[:, f, 128 * t:128 * t + 128], fw2[:, f, :]) for f in range(8)]),
                       g[7 if t < 4 else 15], y.get(t - 2))
                y[t] = dve(lambda e, t=t, bank=bank: e.tensor_tensor(x[:, t, :], ps[:, bank, 0:256], x[:, t, :], ALU.add), p, xb)
                moments(t, y[t])
            return tw

        def memory():
            ar = Carve(third)
            tk, tv, tq = ar(128, 2, 256), ar(128, 2, 256), ar(128, 2, 256)
            W1T, W2T, W2 = ar(128, 2, 64), ar(64, 256), ar(128, 2, 64)
            for dst, n in ((tk, "t_k"), (tv, "t_v"), (tq, "t_q")):
                t_w = load(dst, d[n], s_w[4], *ends5)
            ends = ends5
            for dst, n in ((W1T, "t_W1T"), (W2T, "t_W2T"), (W2, "t_W2")):
                t_p = load(dst, d[n], s_w[5], *ends)
            load_moe()
            zT, eT, qT = ar(128, 2, 1024), ar(128, 2, 1024), ar(128, 2, 1024)
            z = ar(64, NB, 256)
            wd = ar(128, 2, 256)
            hTs, hs2, us, u, m1, sqv, th, nu, de, ph, gp, daT, da, gq = [ar(64, 64) for _ in range(14)]
            hd = ar(64, 320)
            drT, eb = ar(128, 2, 64), ar(128, 2, 64)
            qb_ = [ar(128, 2, 64) for _ in range(2)]
            gb1, gb2 = ar(64, 1), ar(128, 2)
            hs, dr = hd[:, 0:64], hd[:, 64:320]
            toks = layernorm()
            t_h = to_hT(toks)
            t_d = dve(lambda e: e.tensor_tensor(wd, tk, tv, ALU.subtract), t_w)
            n = 0
            ev = {}

            def evac(n, o, i_, p):
                if n % 2:
                    ev[n] = act(lambda e: e.copy(o, i_), p)
                else:
                    ev[n] = dve(lambda e: e.tensor_copy(o, i_), p)

            for W, T in ((tk, zT), (wd, eT), (tq, qT)):
                for m in range(2):
                    for half in range(2):
                        bank = n % 4
                        p = pe(mms(ps[:, bank, :], [(W[:, k, 128 * m:128 * m + 128], hT[:, k, 512 * half:512 * half + 512])
                                                    for k in range(2)]), t_h, t_w, t_d, ev.get(n - 4))
                        evac(n, T[:, m, 512 * half:512 * half + 512], ps[:, bank, :], p)
                        n += 1
            for b in range(0, NB, 2):
                bank = n % 4
                p = pe(seq(*[tr(ps[0:64, bank, 256 * i + 128 * k:256 * i + 128 * k + 128], zT[:, k, 64 * (b + i):64 * (b + i) + 64])
                             for i in range(2) for k in range(2)]), ev.get(n - 4), ev[2], ev[3])
                evac(n, z[:, b:b + 2, :].rearrange("p a c -> p (a c)"), ps[0:64, bank, :], p)
                n += 1
            t_in = [ev[n - 1], ev[n - 2]]
            C = 0.001 * 2.0 / (NQ * D)
            C0 = 0.3989422804014327

            def update(dst, src, *w):
                return dve(lambda e: e.scalar_tensor_tensor(dst, src, -C, dst, ALU.mult, ALU.add), *w)

            uW1 = uW2 = ub1 = ub2 = t_p
            uW2T = t_p
            ans = None
            eb_ = pool(lambda e: e.tensor_tensor(eb, eT[:, :, 0:64], tb2.unsqueeze(2).broadcast_to([128, 2, 64]), ALU.add), *t_in, t_c)

            def answer_first(t, uW1, ub1):
                tt = slice(64 * t, 64 * t + 64)
                p = pe(mms(ps[0:64, 7, 0:64], [(W1T[:, k, :], qT[:, k, tt]) for k in range(2)]), uW1)
                return act(lambda e: e.activation(gq, ps[0:64, 7, 0:64], ACT.Gelu, bias=tb1), p, ub1)

            def answer_second(t, g, uW2T, qb):
                tt = slice(64 * t, 64 * t + 64)
                p = pe(seq(*[mms(ps[:, 7, 64 + 64 * m:128 + 64 * m], [(W2T[:, 128 * m:128 * m + 128], gq)]) for m in range(2)]), g, uW2T)
                dve(lambda e: e.tensor_tensor(qT[:, :, tt], ps[:, 7, 64:192].rearrange("p (a c) -> p a c", c=64), qb_[t % 2], ALU.add), p, g, qb)
                return p

            qb = None
            for t in range(NB):
                tt = slice(64 * t, 64 * t + 64)
                pa = pe(mms(ps[0:64, 0, 0:64], [(W1T[:, k, :], zT[:, k, tt]) for k in range(2)]), *t_in, uW1)
                ah = act(lambda e: e.activation(hTs, ps[0:64, 0, 0:64], ACT.Gelu, bias=tb1), pa, ub1, t_c)
                a = dve(lambda e: e.tensor_scalar(u, ps[0:64, 0, 0:64], tb1, None, ALU.add), pa, ub1, t_c, ah)
                if t:
                    gq_ = answer_first(t - 1, uW1, ub1)
                sq_ = dve(lambda e: e.tensor_tensor(sqv, u, u, ALU.mult), a)
                m_ = dve(lambda e: e.tensor_scalar(m1, sqv, 1e-24, 2e-12, ALU.is_lt, ALU.mult), sq_)
                us_ = dve(lambda e: e.tensor_tensor(us, u, m1, ALU.add), m_)
                at = act(lambda e: e.activation(th, sqv, ACT.Tanh, scale=-0.25), sq_)
                a2 = act(lambda e: e.activation(hs2, us, ACT.Gelu), us_)
                pb = pe(seq(*[mms(ps[:, 1, 64 * m:64 * m + 64], [(W2T[:, 128 * m:128 * m + 128], hTs)]) for m in range(2)]), ah, uW2T)
                dT = dve(lambda e: e.tensor_tensor(drT, ps[:, 1, 0:128].rearrange("p (a c) -> p a c", c=64), eb, ALU.add), pb, eb_)
                p5 = pe(tr(ps[0:64, 5, 0:64], hTs, 64))
                po = None
                if t:
                    po = answer_second(t - 1, gq_, uW2T, qb)
                pd = pe(mms(ps[0:64, 2, 0:64], [(W2[:, m, :], drT[:, m, :]) for m in range(2)]), dT, uW2)
                p5 = pe(seq(*[tr(ps[0:64, 5, 64 + 128 * m:192 + 128 * m], drT[:, m, :]) for m in range(2)]))
                hd_ = act(lambda e: e.copy(hd, ps[0:64, 5, 0:320]), p5)
                r = dve(lambda e: e.tensor_scalar(nu, th, C0, C0, ALU.mult, ALU.add), at)
                r1 = dve(lambda e: e.tensor_scalar(de, th, -1.0, 1.0, ALU.mult, ALU.add), at)
                r2 = dve(lambda e: e.reciprocal(gp, us), us_)
                r1 = dve(lambda e: e.reciprocal(de, de), r1)
                r = dve(lambda e: e.tensor_tensor(nu, nu, u, ALU.mult), r)
                r2 = dve(lambda e: e.tensor_tensor(gp, gp, hs2, ALU.mult), r2, a2)
                r = dve(lambda e: e.tensor_tensor(ph, nu, de, ALU.mult), r, r1)
                r = dve(lambda e: e.tensor_tensor(gp, gp, ph, ALU.add), r, r2)
                da1 = dve(lambda e: e.tensor_tensor(daT, ps[0:64, 2, 0:64], gp, ALU.mult), pd, r)
                p3 = pe(tr(ps[0:64, 3, 0:64], daT, 64), da1)
                da_ = dve(lambda e: e.tensor_copy(da, ps[0:64, 3, 0:64]), p3)
                p6 = pe(seq(mms(ps[0:64, 6, 0:256], [(hs, dr)])), hd_)
                p1 = pe(seq(*[mms(ps[:, 4, 64 * k:64 * k + 64], [(z[:, t, 128 * k:128 * k + 128], da)]) for k in range(2)]), da_)
                p7 = pe(seq(*[mms(ps[:, 6, 256 + 64 * m:320 + 64 * m], [(dr[:, 128 * m:128 * m + 128], hs)]) for m in range(2)]))
                uW1 = update(W1T.rearrange("p a b -> p (a b)"), ps[:, 4, 0:128], p1, gq_ if t else None)
                g1 = dve(lambda e: e.tensor_reduce(gb1, daT, AX.X, ALU.add), da1)
                ub1 = update(tb1, gb1, g1, gq_ if t else None)
                g2 = dve(lambda e: e.tensor_reduce(gb2, drT, AX.X, ALU.add), dT)
                ub2 = update(tb2, gb2, g2, qb)
                uW2T = update(W2T, ps[0:64, 6, 0:256], p7, po)
                uW2 = update(W2.rearrange("p a b -> p (a b)"), ps[:, 6, 256:384], p7)
                if t + 1 < NB:
                    t2 = slice(64 * t + 64, 64 * t + 128)
                    eb_ = pool(lambda e, t2=t2: e.tensor_tensor(eb, eT[:, :, t2], tb2.unsqueeze(2).broadcast_to([128, 2, 64]), ALU.add), ub2)
                qb = pool(lambda e, t=t, tt=tt: e.tensor_tensor(
                    qb_[t % 2], qT[:, :, tt], tb2.unsqueeze(2).broadcast_to([128, 2, 64]), ALU.add), ub2)
            gq_ = answer_first(NB - 1, uW1, ub1)
            answer_second(NB - 1, gq_, uW2T, qb)
            last = (eng_sems["dve"], eng_sems["dve"].n)
            xt = {}
            for t in range(NT):
                bank = t % 2
                p = pe(seq(*[tr(ps[:, bank, 128 * k:128 * k + 128], qT[:, k, 128 * t:128 * t + 128]) for k in range(2)]), last, xt.get(t - 2))
                xt[t] = dve(lambda e, t=t, bank=bank: e.tensor_tensor(x[:, t, :], ps[:, bank, 0:256], x[:, t, :], ALU.add), p)
                moments(t, xt[t])

        def moe(third_ctx):
            ends = fresh("mo")
            third_ctx.close()
            dn = sb("dn", [128, 8 * 1536])
            rest = sb("rest", [128, 6800])
            irest = sb("irest", [128, 64], mybir.dt.int32)
            for e in range(8):
                t_dn = load(dn[:, 1536 * e:1536 * e + 1536], d["m_dn"][e].rearrange("p a b -> p (a b)"), s_dn, *ends)
            t_gu, t_sh = (s_gu, s_gu.n), (s_w[1], s_w[1].n)
            ar = Carve(rest)
            xs = [ar(128, 256) for _ in range(3)]
            XT = [ar(128, 2, 128) for _ in range(2)]
            ar2 = Carve(rest, ar.off)
            sT, sgs = ar2(128, 2, 512), [ar2(128, 512) for _ in range(2)]
            a_, aT = [ar(128, 768) for _ in range(2)], [ar(128, 6, 128) for _ in range(2)]
            sg = [ar(128, 256) for _ in range(3)]
            yS = [ar(128, 256) for _ in range(2)]
            lg, pr, oh1, oh2, tmp, M, base, slot = [ar(128, NT, 8) for _ in range(8)]
            cnt, nt, start, end = [ar(128, 8) for _ in range(4)]
            pos = ar(128, 16)
            v1, v2, f_, g1, g2 = [ar(128, NT) for _ in range(5)]
            texp = ar(128, NS)
            cmp_ = ar(128, 512)
            ipos, itu, itd = irest[:, 0:16], irest[0:1, 16:16 + NS], irest[0:1, 40:40 + NS]
            mcc = Carve(mc)
            tri, ones, lt, k128, iota = mcc(128, 128), mcc(128, 128), mcc(128, 8, 8), mcc(128, 8), mcc(128, NS)

            toks = layernorm()
            t_h = to_hT(toks, scale=lng, shift=lnb)
            p = pe(seq(*[mms(ps[:, 6, 8 * t:8 * t + 8], [(hT[:, k, 128 * t:128 * t + 128], rw[:, k, :]) for k in range(2)])
                         for t in range(NT)]), t_h, t_sh)

            def b3(v):
                return v.unsqueeze(2).broadcast_to([128, NT, 8])

            sh_free, sh_read, y_free = {}, {}, {}

            def shared_gu(half, f):
                hh = [hT[:, k, 512 * half:512 * half + 512] for k in range(2)]
                return pe(seq(*[mms(ps[:, 2 * f + j, :], [(sgu[:, k, 128 * (f + 2 * j):128 * (f + 2 * j) + 128], hh[k]) for k in range(2)])
                                for j in range(2)]), t_h, t_sh, sh_free.get(f))

            def shared_act(half, f, p):
                s = act(lambda e: e.activation(sgs[f], ps[:, 2 * f, :], ACT.Silu), p, sh_free.get(f))
                sh_free[f] = dve(lambda e: e.tensor_tensor(sT[:, f, :], ps[:, 2 * f + 1, :], sgs[f], ALU.mult), s, sh_read.get(0))

            def shared_down(half):
                for t in range(4):
                    bank, tt = 4 + t % 2, 4 * half + t
                    p = pe(mms(ps[:, bank, 0:256], [(sT[:, f, 128 * t:128 * t + 128], sdn[:, f, :]) for f in range(2)]),
                           sh_free[0], sh_free[1], y_free.get(bank))
                    y_free[bank] = dve(lambda e, tt=tt, bank=bank: e.tensor_tensor(x[:, tt, :], ps[:, bank, 0:256], x[:, tt, :], ALU.add), p)
                sh_read[0] = p

            sh_p = [shared_gu(0, f) for f in range(2)]
            L = ps[:, 6, 0:64].rearrange("p (t e) -> p t e", e=8)
            a = dve(lambda e: e.tensor_reduce(v1, L, AX.X, ALU.max), p)
            a = dve(lambda e: e.tensor_tensor(lg, L, b3(v1), ALU.subtract), a)
            a = act(lambda e: e.activation(pr, lg, ACT.Exp), a)
            a = dve(lambda e: e.tensor_reduce(v1, pr, AX.X, ALU.add), a)
            a = dve(lambda e: e.reciprocal(v1, v1), a)
            a = dve(lambda e: e.tensor_tensor(pr, pr, b3(v1), ALU.mult), a)

            def top(oh, v, a):
                a = dve(lambda e: e.tensor_reduce(v, pr, AX.X, ALU.max), a)
                a = dve(lambda e: e.tensor_tensor(tmp, pr, b3(v), ALU.is_equal), a)
                a = dve(lambda e: e.tensor_tensor(tmp, tmp, eord.unsqueeze(1).broadcast_to([128, NT, 8]), ALU.mult), a, t_c)
                a = dve(lambda e: e.tensor_reduce(f_, tmp, AX.X, ALU.max), a)
                return dve(lambda e: e.tensor_tensor(oh, tmp, b3(f_), ALU.is_equal), a)

            a = top(oh1, v1, a)
            a = dve(lambda e: e.scalar_tensor_tensor(pr, oh1, -2.0, pr, ALU.mult, ALU.add), a)
            a = top(oh2, v2, a)
            tM = dve(lambda e: e.tensor_tensor(M, oh1, oh2, ALU.add), a)

            def flat(v):
                return v.rearrange("p a b -> p (a b)")

            p = pe(seq(mms(ps[:, 7, 0:64], [(tri, flat(M))]), mms(ps[:, 7, 64:128], [(ones, flat(M))])), tM, t_sh)
            R = ps[:, 7, 0:64].rearrange("p (t e) -> p t e", e=8)
            C = ps[:, 7, 64:128].rearrange("p (t e) -> p t e", e=8)
            c4 = cmp_.rearrange("p (t e u) -> p t e u", e=8, u=8)
            c3 = cmp_[:, 0:64].rearrange("p (a b) -> p a b", b=8)
            a = dve(lambda e: e.tensor_tensor(c4, ps[:, 7, 64:128].rearrange("p (u e) -> p e u", e=8).unsqueeze(1).broadcast_to([128, 8, 8, 8]),
                                              lt.unsqueeze(2).broadcast_to([128, 8, 8, 8]), ALU.mult), p)
            a = dve(lambda e: e.tensor_reduce(base, c4, AX.X, ALU.add), a)
            a = dve(lambda e: e.tensor_tensor(cnt, base[:, 7, :], C[:, 7, :], ALU.add), a)
            a = dve(lambda e: e.tensor_tensor(c3, cnt.unsqueeze(2).broadcast_to([128, 8, 8]),
                                              k128.unsqueeze(1).broadcast_to([128, 8, 8]), ALU.is_gt), a)
            a = dve(lambda e: e.tensor_reduce(nt, c3, AX.X, ALU.add), a)
            a = dve(lambda e: e.tensor_tensor(c3, nt.unsqueeze(1).broadcast_to([128, 8, 8]), lt, ALU.mult), a)
            a = dve(lambda e: e.tensor_reduce(start, c3, AX.X, ALU.add), a)
            s_ = dve(lambda e: e.scalar_tensor_tensor(slot, start.unsqueeze(1).broadcast_to([128, NT, 8]), 128.0, base, ALU.mult, ALU.add), a)
            s_ = dve(lambda e: e.tensor_tensor(slot, slot, R, ALU.add), s_)
            for i, oh in ((0, oh1), (8, oh2)):
                b = dve(lambda e, oh=oh: e.tensor_tensor(tmp, oh, slot, ALU.mult), s_)
                s_ = dve(lambda e, i=i: e.tensor_reduce(pos[:, i:i + 8], tmp, AX.X, ALU.add), b)
            t_pos = dve(lambda e: e.tensor_copy(ipos, pos), s_)
            a = dve(lambda e: e.tensor_tensor(end, start, nt, ALU.add), t_pos)
            ce = cmp_[:, 0:NS * 8].rearrange("p (i e) -> p i e", e=8)
            a = dve(lambda e: e.tensor_tensor(ce, iota.unsqueeze(2).broadcast_to([128, NS, 8]),
                                              end.unsqueeze(1).broadcast_to([128, NS, 8]), ALU.is_ge), a)
            a = dve(lambda e: e.tensor_reduce(texp, ce, AX.X, ALU.add), a)
            t_te = dve(lambda e: e.tensor_scalar(itu, texp[0:1, :], 7.0, 3072.0, ALU.min, ALU.mult), a)
            t_te = dve(lambda e: e.tensor_scalar(itd, texp[0:1, :], 7.0, 1536.0, ALU.min, ALU.mult), t_te)
            a = dve(lambda e: e.tensor_tensor(v2, v2, v1, ALU.subtract), t_te)
            a = act(lambda e: e.activation(g2, v2, ACT.Exp), a)
            a = dve(lambda e: e.tensor_scalar(g1, g2, 1.0, None, ALU.add), a)
            a = dve(lambda e: e.reciprocal(g1, g1), a)
            t_g = dve(lambda e: e.tensor_tensor(g2, g2, g1, ALU.mult), a)

            for k in range(2):
                for t in range(NT):
                    i = 8 * k + t
                    t_sc = op("pool", lambda e, i=i, t=t: e.indirect_dma_start(
                        xs_d, bass.IndirectOffsetOnAxis(ap=ipos[:, i:i + 1].bitcast(mybir.dt.uint32), axis=0), h[:, t, :], None),
                        t_pos, toks[-1], t_zero, sem=s_sc, inc=16)

            for f in range(2):
                shared_act(0, f, sh_p[f])
            shared_down(0)
            for f in range(2):
                shared_act(1, f, shared_gu(1, f))
            shared_down(1)

            bfree = {6: t_te, 7: t_te, 0: sh_free[0], 1: sh_free[0], 2: sh_free[1], 3: sh_free[1], 4: y_free[4], 5: y_free[5]}
            xs_t, xs_r, XTt, XTr, at, atr, aTt, yt, yd, dnr = {}, {}, {}, {}, {}, {}, {}, {}, {}, {}

            def load_block(i):
                xs_t[i] = load(xs[i % 3], xs_d[128 * i:128 * i + 128, :], s_xs[i % 3], t_sc, xs_r.get(i - 3))

            def turn_block(i):
                p = pe(seq(*[tr(ps[:, 6, 128 * k:128 * k + 128], xs[i % 3][:, 128 * k:128 * k + 128]) for k in range(2)]),
                       xs_t[i], bfree.get(6))
                xs_r[i] = p
                for k in range(2):
                    bfree[6] = XTt[i] = dve(lambda e, k=k: e.tensor_scalar(
                        XT[i % 2][:, k, :], ps[:, 6, 128 * k:128 * k + 128], lng[:, k:k + 1], lnb[:, k:k + 1], ALU.mult, ALU.add),
                        p, XTr.get(i - 2))

            def gate_up(i, c):
                def f(e):
                    if c == 0:
                        off[i, 0] = e.value_load(itu[:, i:i + 1], min_val=0, max_val=7 * 3072)
                    for k in range(2):
                        m = e.matmul(ps[:, c, :], XT[i % 2][:, k, :], gu[:, bass.ds(off[i, 0] + (1536 * k + 512 * c), 512)],
                                     start=(k == 0), stop=(k == 1))
                    return m
                p = pe(f, XTt[i], t_gu, t_te, bfree.get(c))
                XTr[i] = p
                s = act(lambda e: e.activation(sg[c], ps[:, c, 0:256], ACT.Silu), p, bfree.get(("sg", c)))
                bfree[c] = bfree["sg", c] = at[i, c] = dve(lambda e: e.tensor_tensor(
                    a_[i % 2][:, 256 * c:256 * c + 256], ps[:, c, 256:512], sg[c], ALU.mult), s, atr.get(i - 2, sh_read[0]))

            def turn_a(i):
                for n, c in ((4, 3), (2, 4)):
                    f0 = 0 if c == 3 else 4
                    p = pe(seq(*[tr(ps[:, c, 128 * f:128 * f + 128], a_[i % 2][:, 128 * (f0 + f):128 * (f0 + f) + 128]) for f in range(n)]),
                           at[i, 1 if c == 3 else 2], bfree.get(c))
                    o, s = aT[i % 2][:, f0:f0 + n, :].rearrange("p a b -> p (a b)"), ps[:, c, 0:128 * n]
                    bfree[c] = aTt[i, c] = act(lambda e, o=o, s=s: e.copy(o, s), p, dnr.get(i - 2))
                atr[i] = p

            def down(i):
                bank = (5, 7)[i % 2]

                def f(part):
                    def g(e):
                        if part == 0:
                            off[i, 1] = e.value_load(itd[:, i:i + 1], min_val=0, max_val=7 * 1536)
                        for f in range(4 * part, 4 + 2 * part):
                            m = e.matmul(ps[:, bank, 0:256], aT[i % 2][:, f, :], dn[:, bass.ds(off[i, 1] + 256 * f, 256)],
                                         start=(f == 0), stop=(f == 5))
                        return m
                    return g
                pe(f(0), aTt[i, 3], t_dn, bfree.get(bank))
                p = pe(f(1), aTt[i, 4])
                dnr[i] = p
                bfree[bank] = y = dve(lambda e: e.tensor_copy(yS[i % 2], ps[:, bank, 0:256]), p, yd.get(i - 2))
                yd[i] = load(ys_d[128 * i:128 * i + 128, :], yS[i % 2], s_ys[i % 2], y)

            off = {}
            for i in range(3):
                load_block(i)
            turn_block(0)
            for i in range(NS):
                if i + 1 < NS:
                    turn_block(i + 1)
                    if i + 3 < NS:
                        load_block(i + 3)
                gate_up(i, 0)
                gate_up(i, 1)
                if i:
                    turn_a(i - 1)
                gate_up(i, 2)
                if i:
                    down(i - 1)
            turn_a(NS - 1)
            down(NS - 1)
            yg = [gu[:, 256 * i:256 * i + 256] for i in range(16)]
            yt = {}
            for t in range(NT):
                for k in range(2):
                    i = 8 * k + t
                    yt[i] = op("pool", lambda e, i=i: e.indirect_dma_start(
                        yg[i], None, ys_d, bass.IndirectOffsetOnAxis(ap=ipos[:, i:i + 1].bitcast(mybir.dt.uint32), axis=0)),
                        yd[NS - 1], yd[NS - 2], XTr[NS - 1], sem=s_yg[t], inc=16)
            for t in range(NT):
                a = dve(lambda e, t=t: e.scalar_tensor_tensor(x[:, t, :], yg[t], g1[:, t:t + 1], x[:, t, :], ALU.mult, ALU.add),
                        yt[t], yt[8 + t], t_g, (eng_sems["dve"], eng_sems["dve"].n))
                dve(lambda e, t=t: e.scalar_tensor_tensor(x[:, t, :], yg[8 + t], g2[:, t:t + 1], x[:, t, :], ALU.mult, ALU.add), a)

        if stages > 1 and first <= 2:
            s_cm = sem("cm")
            with ExitStack() as sa_ctx:
                selfattn(sa_ctx.enter_context(nc.sbuf_tensor("sa", [128, 31500], F32)))
        if stages > 2 and first <= 3:
            with ExitStack() as ff_ctx:
                tw1 = ffn(ff_ctx.enter_context(nc.sbuf_tensor("ffa", [128, 8192], F32)))
        arena = second_ctx.enter_context(nc.sbuf_tensor("arena", [128, 2400], F32))
        arenaR = second_ctx.enter_context(nc.sbuf_tensor("arenaR", [128, 27080], F32R))
        if stages > 3 and first <= 4:
            t_b = load_bias(2, "x1_bo", *fresh("x1"))
            xattn("x1", X1, 4, 2, mask1, tw1, t_b)
        if stages > 4:
            ends5 = fresh("tt")
            second_ctx.close()
            gu = sb("gu", [128, 8 * 3072])
            cs = Carve(sb("cs", [128, 1880 + NS]))
            sgu, sdn, rw, mc = cs(128, 2, 512), cs(128, 2, 256), cs(128, 2, 8), cs(128, 328 + NS)
            third_ctx = ExitStack()
            ctx.callback(third_ctx.close)
            third = third_ctx.enter_context(nc.sbuf_tensor("third", [128, 14800], F32))
            s_gu, s_dn, s_sc = sem("gu"), sem("dn"), sem("sc")
            s_xs, s_ys, s_yg = [sem(f"xs{i}") for i in range(3)], [sem(f"ys{i}") for i in range(2)], [sem(f"yg{i}") for i in range(NT)]

            def load_moe():
                for dst, n in ((sgu, "m_sgu"), (sdn, "m_sdn"), (rw, "m_rw"), (mc, "mc")):
                    load(dst, d[n], s_w[1], *ends5)
                for e in range(8):
                    load(gu[:, 3072 * e:3072 * e + 3072], d["m_gu"][e].rearrange("p a b -> p (a b)"), s_gu, *ends5)

            if first <= 5:
                memory()
            else:
                load_moe()
        if stages > 5 and first <= 6:
            moe(third_ctx)
        ends = [(s, s.n) for s in eng_sems.values() if s.n]
        s_out = sem("out")
        t_o = op("sp", lambda e: e.dma_start(out.rearrange("(t b) n c -> (b n) t c", b=2), x[:, :, :]), *ends, sem=s_out, inc=16)
        op("sp", None, t_o)

        block = ctx.enter_context(nc.Block())

        @block.tensor
        def _(e):
            Q.emit("pe", e)

        @block.vector
        def _(e):
            Q.emit("dve", e)

        @block.scalar
        def _(e):
            Q.emit("act", e)

        @block.gpsimd
        def _(e):
            Q.emit("pool", e)

        @block.sync
        def _(e):
            Q.emit("sp", e)


def layout(np, i):
    a = {k: np.asarray(v) for k, v in i.items()}
    C = np.ascontiguousarray
    r = {}
    r["x"] = a["x"]
    r["ctx"] = a["ctx_768"]
    r["ctxT"] = C(a["ctx_768"].transpose(0, 2, 1))
    f = np.float32
    r["ident"] = np.eye(128, dtype=f)
    p = np.arange(128)
    r["mask0"] = ((p[:, None] // 16 == np.arange(8)[None]) * 0.25).astype(f)
    r["mask1"] = ((p[:, None] // 64 == np.arange(2)[None]) * 0.125).astype(f)
    r["eord"] = np.tile(8.0 - np.arange(8), (128, 1)).astype(f)
    r["causal"] = ((p[:, None] // 64 == p[None] // 64) & (p[:, None] <= p[None])).astype(f)

    def col(v, n):
        return C(v.reshape(n, 128).T)

    def rows(w, n):
        return C(w.reshape(n, 128, w.shape[1]).transpose(1, 0, 2))

    r["bq"] = col(a["L0_xattn_bq"], 2)
    r["bvc"] = col(a["L0_xattn_bv"], 2)
    r["normw"] = col(a["L0_attn_norm_w"], 2)
    r["qg"] = col(a["L0_attn_q_gamma"].reshape(-1), 8)
    r["kg"] = C(np.concatenate([a["L0_attn_k_gamma"].T] * 2, 0))
    r["b1c"] = col(a["L0_ffn_b1"], 8)
    r["tb1"] = C(a["L1_attn_b1"].reshape(64, 1))
    r["tb2"] = col(a["L1_attn_b2"], 2)
    r["lng"] = col(a["L1_ffn_ln_gamma"], 2)
    r["lnb"] = col(a["L1_ffn_ln_beta"], 2)
    r["x0_bo"], r["f_b2"], r["x1_bo"] = a["L0_xattn_bo"], a["L0_ffn_b2"], a["L1_xattn_bo"]
    r["x0_wq"] = rows(a["L0_xattn_wq"], 2)
    def twice(w):
        return np.concatenate([w[:, :128], w[:, 128:], w[:, 128:]], 1)

    r["fold"] = (p[:, None] % 64 == np.arange(64)[None]).astype(f)
    r["own"] = (p[:, None] // 64 == np.arange(32)[None] // 16).astype(f)
    r["bkc"] = col(a["L0_xattn_bk"], 2)
    for k in ("wk", "wv"):
        r["x0_" + k] = C(twice(a["L0_xattn_" + k].T).reshape(256, 2, 128).transpose(2, 1, 0))

    def place(wv, H, dh, hpg):
        o = np.zeros((wv.shape[0], H, 128), f)
        for hh in range(H):
            o[:, hh, dh * (hh % hpg):dh * (hh % hpg) + dh] = wv[:, hh * dh:(hh + 1) * dh]
        return o

    r["x0_wo"] = rows(a["L0_xattn_wo"], 2)
    r["a_wq"], r["a_wkv"], r["a_wout"] = rows(a["L0_attn_Wq"], 2), rows(a["L0_attn_Wkv"], 2), rows(a["L0_attn_Wout"], 4)
    r["f_w1"], r["f_w2"] = rows(a["L0_ffn_w1"], 2), rows(a["L0_ffn_w2"], 8)
    r["x1_wq"] = rows(a["L1_xattn_Wq"], 2)
    r["x1_wk"] = rows(twice(a["L1_xattn_Wk"].T), 4)
    wv = place(a["L1_xattn_Wv"], 8, 64, 2)
    r["x1_wv1"], r["x1_wv2"] = C(wv[:128]), C(wv[128:])
    r["x1_wo"] = rows(a["L1_xattn_Wo"], 4)
    for k in "kvq":
        r["t_" + k] = rows(C(a["L1_attn_t_" + k].T), 2)
    r["t_W1T"] = rows(C(a["L1_attn_W1"].T), 2)
    r["t_W2T"] = C(a["L1_attn_W2"].T)
    r["t_W2"] = rows(a["L1_attn_W2"], 2)
    r["m_rw"] = rows(C(a["L1_ffn_router_w"].T), 2)
    g = a["L1_ffn_gate_up_w"].transpose(0, 2, 1).reshape(8, 2, 128, 2, 3, 256)
    r["m_gu"] = C(g.transpose(0, 2, 1, 4, 3, 5).reshape(8, 128, 2, 1536))
    e = np.arange(8)
    lt = (e[None] < e[:, None]).reshape(1, 64)
    rows_ = [p[:, None] < p[None], np.ones((128, 128)), lt.repeat(128, 0), np.tile(128 * e, (128, 1)), np.tile(np.arange(NS), (128, 1))]
    r["mc"] = C(np.concatenate(rows_, 1).astype(f))
    r["m_dn"] = C(a["L1_ffn_down_w"].transpose(0, 2, 1).reshape(8, 6, 128, 256).transpose(0, 2, 1, 3))
    r["m_sgu"] = rows(C(a["L1_ffn_shared_gate_up_w"].T), 2)
    r["m_sdn"] = rows(C(a["L1_ffn_shared_down_w"].T), 2)
    r["tb1"] = np.concatenate([r["tb1"]] * 2, 0)
    names = ("mask0", "mask1", "fold", "own", "bq", "bkc", "bvc", "eord", "normw", "qg", "kg", "b1c", "tb1", "tb2", "lng", "lnb")
    r["small"] = C(np.concatenate([r.pop(n) for n in names], 1))
    return r


def kernel(**inputs):
    import numpy as np
    import concourse.bacc as bacc
    from concourse.bass_utils import run_bass_kernel_spmd

    nc = bacc.Bacc("TRN2", target_bir_lowering=False, num_devices=1)
    arrays = layout(np, inputs)
    d = {n: nc.dram_tensor("in_" + n, v.shape, mybir.dt.from_np(v.dtype), kind="ExternalInput").ap() for n, v in arrays.items()}
    out = nc.dram_tensor("out_x", (16, 64, 256), F32, kind="ExternalOutput").ap()
    program(nc, d, out)
    r = run_bass_kernel_spmd(nc, [{"in_" + n: v for n, v in arrays.items()}], core_ids=[0])
    return r.results[0]["out_x"]
```

```python
from contextlib import ExitStack

import concourse.bass as bass
from concourse import mybir

F32 = mybir.dt.float32
F32R = mybir.dt.float32r
ALU = mybir.AluOpType
ACT = mybir.ActivationFunctionType
AX = mybir.AxisListType

NB, NQ, D, DC, NK = 16, 64, 256, 192, 1601
NT = 8
KT = 13
NS = 23
KL = NK - 12 * 128


class Sem:

    def __init__(self, handle):
        self.h, self.n = handle, 0


class Queues:

    def __init__(self):
        self.q = {k: [] for k in ("pe", "dve", "act", "pool", "sp")}

    def op(self, eng, fn, *waits, sem=None, inc=1):
        self.q[eng].append((waits, fn, sem, inc))
        if sem is not None:
            sem.n += inc
            return (sem, sem.n)
        return None

    def emit(self, eng, e):
        seen = {}
        for waits, fn, sem, inc in self.q[eng]:
            for w in waits:
                if w is None:
                    continue
                s, n = w
                if seen.get(id(s), 0) < n:
                    e.wait_ge(s.h, n)
                    seen[id(s)] = n
            if fn is None:
                continue
            ins = fn(e)
            if sem is not None:
                ins.then_inc(sem.h, inc)


def program(nc, d, out, stages=6, first=1):
    ctx = ExitStack()
    with ctx:
        def sb(name, shape, dt=F32):
            return ctx.enter_context(nc.sbuf_tensor(name, shape, dt))

        sems = [0]

        def sem(name):
            sems[0] += 1
            return Sem(ctx.enter_context(nc.semaphore(f"s_{name}")))

        Q = Queues()
        op = Q.op
        ps = ctx.enter_context(nc.psum_tensor("ps", [128, 8, 512], F32))
        psf = ps[:, :, :].rearrange("p b n -> p (b n)")

        x = sb("x", [128, NT, D])
        h = sb("h", [128, NT, D])
        hT = sb("hT", [128, 2, NT * 128])
        ident = sb("ident", [128, 128])
        small = sb("small", [128, 512])
        biasb, zeros = sb("biasb", [128, 256]), sb("zeros", [128, 256])
        first_ctx = ExitStack()
        ctx.callback(first_ctx.close)
        arenaR0 = first_ctx.enter_context(nc.sbuf_tensor("arenaR0", [128, 36000], F32R))
        arena0 = first_ctx.enter_context(nc.sbuf_tensor("arena0", [128, 9100], F32))

        class Carve:
            def __init__(self, t, off=0):
                self.t, self.off = t, off

            def __call__(self, parts, *shape):
                n = 1
                for s in shape:
                    n *= s
                v = self.t[0:parts, self.off:self.off + n]
                self.off += n
                if len(shape) == 2:
                    v = v.rearrange("p (a b) -> p a b", b=shape[1])
                elif len(shape) == 3:
                    v = v.rearrange("p (a b c) -> p a b c", b=shape[1], c=shape[2])
                assert self.off <= self.t.shape[1], (self.off, self.t.shape)
                return v

        ar0 = Carve(arena0)
        X0 = {k: ar0(128, 2, 256) for k in ("wq", "wk", "wv", "wo")}

        cc = Carve(small)
        mask0, mask1 = cc(128, 8), cc(128, 2)
        fold, own = cc(128, 64), cc(128, 32)
        bq, bkc, bvc = cc(128, 2), cc(128, 2), cc(128, 2)
        eord = cc(128, 8)
        normw, qg, kg, b1c = cc(128, 2), cc(128, 8), cc(128, 8), cc(128, 8)
        tb1, tb2 = cc(128, 1)[0:64], cc(128, 2)
        lng, lnb = cc(128, 2), cc(128, 2)
        n_const = cc.off
        st, mv = cc(128, NT, 6), cc(128, NT, 2)
        ve, sd, rs = cc(128, NT), cc(128, NT), cc(128, NT)
        ss2 = cc(128, NT)

        s_c, s_x = sem("c"), sem("x")
        xs_d = nc.dram_tensor("xs_rows", (128 * NS, D), F32, kind="Internal").ap()
        ys_d = nc.dram_tensor("ys_rows", (128 * NS, D), F32, kind="Internal").ap()
        s_w = [sem(f"w{i}") for i in range(6)]
        s_bias = [sem(f"bias{i}") for i in range(4)]

        def load(dst, src, s, *waits):
            return op("sp", lambda e: e.dma_start(dst, src), *waits, sem=s, inc=16)

        t_x = load(x[:, :, :], d["x"].rearrange("(t b) n c -> (b n) t c", b=2), s_x)
        load(ident[:, :], d["ident"], s_c)
        t_c = load(small[:, 0:n_const], d["small"], s_c)
        for k in ("wk", "wv"):
            t_w0 = load(X0[k], d["x0_" + k], s_w[0])

        eng_sems = {}

        def fresh(tag):
            old = dict(eng_sems)
            for k in ("pe", "dve", "act", "pool"):
                eng_sems[k] = sem(f"{tag}_{k}")
            if old:
                ends = [(s, s.n) for s in old.values() if s.n]
                for k in ("pe", "dve", "act", "pool"):
                    op(k, None, *ends)
                return ends
            return []

        def pe(fn, *w):
            return op("pe", fn, *w, sem=eng_sems["pe"])

        def dve(fn, *w):
            return op("dve", fn, *w, sem=eng_sems["dve"])

        def act(fn, *w):
            return op("act", fn, *w, sem=eng_sems["act"])

        def pool(fn, *w):
            return op("pool", fn, *w, sem=eng_sems["pool"])

        def mms(outap, pairs, first=True, last=True):
            def f(e):
                n = len(pairs)
                for i, (a, b) in enumerate(pairs):
                    m = e.matmul(outap, a, b, start=(first and i == 0), stop=(last and i == n - 1))
                return m
            return f

        def seq(*fns):
            def f(e):
                for g in fns:
                    m = g(e)
                return m
            return f

        def tr(outap, inap, k=128):
            return lambda e: e.transpose(outap, inap, ident[0:k, 0:k])

        def rsqrt_of(v, n_ap, r_ap, *w):
            a = act(lambda e: e.activation(n_ap, v, ACT.Sqrt), *w)
            return dve(lambda e: e.reciprocal(r_ap, n_ap), a)

        known = {}

        def moments(t, *w):
            a = dve(lambda e: e.bn_stats(st[:, t, :], x[:, t, :]), *w)
            known[t] = dve(lambda e: e.bn_aggr(mv[:, t, :], st[:, t, :]), a)

        def layernorm(*w, rms=False):
            for t in range(NT):
                if t not in known:
                    moments(t, *w)
            b = known[NT - 1]
            known.clear()
            c = dve(lambda e: e.tensor_scalar(ve, mv[:, :, 1], 1e-5, None, ALU.add), b)
            r = rsqrt_of(ve, sd, rs, c)
            if rms:
                c = dve(lambda e: e.tensor_tensor(ss2, rs, rs, ALU.mult), r)
                c = dve(lambda e: e.tensor_tensor(ss2, ss2, mv[:, :, 1], ALU.mult), c)
                c = dve(lambda e: e.tensor_scalar(ve, ss2, 1.1920929e-07, None, ALU.add), c)
                c = rsqrt_of(ve, sd, ss2, c)
                r = dve(lambda e: e.tensor_tensor(rs, rs, ss2, ALU.mult), c)
            toks = []
            for t in range(NT):
                toks.append(dve(lambda e, t=t: e.tensor_scalar(h[:, t, :], x[:, t, :], mv[:, t, 0:1], rs[:, t:t + 1],
                                                               ALU.subtract, ALU.mult), r))
            return toks

        def to_hT(toks, scale=None, shift=None, parts=None, after=None):
            res = {}
            n = 0
            for half in range(2):
                for k in range(2):
                    bank = n % 2
                    p = pe(seq(*[tr(ps[:, bank, 128 * i:128 * i + 128], h[:, 4 * half + i, 128 * k:128 * k + 128])
                                 for i in range(4)]), toks[4 * half + 3], t_c, res.get(n - 2))
                    o, i_ = hT[:, k, 512 * half:512 * half + 512], ps[:, bank, :]
                    if parts is not None:
                        hi, lo = [v[:, k, 512 * half:512 * half + 512] for v in parts]
                        a = act(lambda e, hi=hi, i_=i_: e.copy(hi, i_), p)
                        res[n] = dve(lambda e, hi=hi, lo=lo, i_=i_: e.tensor_tensor(lo, i_, hi, ALU.subtract), a)
                    elif scale is None:
                        res[n] = act(lambda e, o=o, i_=i_: e.copy(o, i_), p)
                    elif shift is None:
                        res[n] = dve(lambda e, o=o, i_=i_, k=k: e.tensor_scalar(o, i_, scale[:, k:k + 1], None, ALU.mult), p)
                    else:
                        res[n] = dve(lambda e, o=o, i_=i_, k=k: e.tensor_scalar(
                            o, i_, scale[:, k:k + 1], shift[:, k:k + 1], ALU.mult, ALU.add), p)
                    n += 1
                if after is not None:
                    after(half, res[2 * half], res[2 * half + 1])
            return res[3]

        bias_tok = []

        def load_bias(i, name, *w):
            bias_tok.append(load(biasb[:, :], d[name].partition_broadcast(128), s_bias[i], *w, *bias_tok[-1:]))
            return bias_tok[-1]

        def latents(t_w):
            W = X0
            ar, arr = ar0, Carve(arenaR0)
            raw2, P = ar(128, NK), ar(128, NK)
            c1h, c1l, c2 = [arr(128, KT * 128) for _ in range(3)]
            wh, wl = [{k: arr(128, 2, 256) for k in ("wk", "wv")} for _ in range(2)]
            PTh, PTl = arr(128, KT, 256), arr(128, KT, 256)
            Vh, Vl = [[arr(128, KT, 256) for _ in range(2)] for _ in range(2)]
            vs = [ar(128, 512) for _ in range(4)]
            oS = ar(128, 256)
            O = [ar(128, 8, 32) for _ in range(2)]
            aT = ar(128, 2, 128)
            mx4, mx, sums, rc = [[ar(128, k) for _ in range(2)] for k in (4, 1, 2, 1)]
            Kh, Kl = [[arr(128, NK + 1) for _ in range(2)] for _ in range(2)]
            qh, ql = [[arr(128, 8, 64) for _ in range(2)] for _ in range(2)]
            qTh, qTl = arr(128, 2, 128), arr(128, 2, 128)
            s_raw, s_wq = sem("x0raw"), sem("x0wq")
            for c in (c1h, c1l, c2):
                t_ones = dve(lambda e, c=c: e.memset(c[:, NK:KT * 128].bitcast(F32), 0.0))
            for k in ("wk", "wv"):
                a = act(lambda e, k=k: e.copy(wh[k], W[k]), t_w)
                t_wl = pool(lambda e, k=k: e.tensor_tensor(wl[k], W[k], wh[k], ALU.subtract), a)

            pairs = [(b, j) for b in range(NB) for j in range(8)]
            N = len(pairs)
            raw_tok, split_tok, cread, kt, vt, qt, qTt, bd = {}, {}, {}, {}, {}, {}, {}, {}
            exa, exb, s_tok, tr_done, av, on, turned, aTt, proj, oSt, oSr, rct = {}, {}, {}, {}, {}, {}, {}, {}, {}, {}, {}, {}
            free, vread, ptt = {}, {}, {}

            def raw1(b):
                return P if b == 0 else h[:, :, :].rearrange("p a b -> p (a b)")[:, 0:NK]

            def load_raw(b, *w):
                if b:
                    w += tuple(t for c in range(4) for t in split_tok[b - 1, c])
                load(raw1(b), d["ctxT"][b, 0:128, :], s_raw, *w)
                load(raw2[0:64, :], d["ctxT"][b, 128:192, :], s_raw, *w)
                raw_tok[b] = load(raw2[64:128, :], d["ctxT"][b, 128:192, :], s_raw)

            def split(b, c):
                w = (raw_tok[b], cread.get(b - 1), t_ones)
                k = slice(400 * c, 400 * c + 400 + (c == 3))
                a1 = act(lambda e: e.copy(c1h[:, k], raw1(b)[:, k]), *w)
                a2 = (act if c > 1 else pool)(lambda e: (e.copy if c > 1 else e.tensor_copy)(c2[:, k], raw2[:, k]), *w)
                p1 = pool(lambda e: e.tensor_tensor(c1l[:, k], raw1(b)[:, k], c1h[:, k], ALU.subtract), a1)
                p2 = pool(lambda e: e.tensor_tensor(c2[64:128, k], raw2[64:128, k], c2[64:128, k], ALU.subtract), a2, p1)
                op("pool", None, p2)
                split_tok[b, c] = [a1, p2]

            def keys(b, g, c, bank, early=False):
                k0, n = 400 * c, 400 + 2 * (c == 3)
                k, f = slice(k0, k0 + n), slice(128 * g, 128 * g + 128)
                H, L = wh["wk"], wl["wk"]
                o = ps[:, bank, 0:n]
                p = pe(mms(o, [(H[:, 0, f], c1h[:, k]), (H[:, 0, f], c1l[:, k]), (L[:, 0, f], c1h[:, k]),
                               (H[:, 1, f], c2[:, k]), (L[:, 1, f], c2[:, k])]), *split_tok[b, c], t_wl, free.get(bank))
                cread[b] = p
                w = (p, t_c, s_tok.get(8 * b - 5 + 4 * g))
                if early:
                    a = dve(lambda e: e.tensor_scalar(Kh[g][:, k], o, bkc[:, g:g + 1], None, ALU.add), *w)
                else:
                    a = act(lambda e: e.activation(Kh[g][:, k], o, ACT.Identity, bias=bkc[:, g:g + 1]), *w)
                free[bank] = kt[b, g] = dve(lambda e: e.scalar_tensor_tensor(
                    Kl[g][:, k], o, bkc[:, g:g + 1], Kh[g][:, k], ALU.add, ALU.subtract), a)

            def vals(b, q, bank, early=False):
                H, L = wh["wv"], wl["wv"]
                ts = range(2 * q, min(2 * q + 2, KT))
                fs = []
                for t in ts:
                    k = slice(128 * t, 128 * t + 128)
                    fs.append(mms(ps[:, bank, 256 * (t % 2):256 * (t % 2) + 256],
                                  [(c1h[:, k], H[:, 0, :]), (c1l[:, k], H[:, 0, :]), (c1h[:, k], L[:, 0, :]),
                                   (c2[:, k], H[:, 1, :]), (c2[:, k], L[:, 1, :])]))
                p = pe(seq(*fs), *split_tok[b, min(256 * q // 400, 3)], *split_tok[b, min((256 * q + 255) // 400, 3)], t_wl, free.get(bank))
                cread[b] = p
                r, w, v = (128, 512, vs[q % 4]) if q < 6 else (KL, 256, vs[q % 4])
                o = ps[0:r, bank, 0:w]
                w_ = (p, vread.get(q % 4))
                if early:
                    free[bank] = a = dve(lambda e: e.tensor_copy(v[0:r, 0:w], o), *w_)
                else:
                    free[bank] = a = act(lambda e: e.copy(v[0:r, 0:w], o), *w_)
                H, L = [x_[b % 2][0:r, ts[0]:ts[-1] + 1, :].rearrange("p a c -> p (a c)") for x_ in (Vh, Vl)]
                h_ = pool(lambda e: e.tensor_copy(H, v[0:r, 0:w]), a, av.get(4 * b - 5))
                vt[b] = vread[q % 4] = pool(lambda e: e.tensor_tensor(L, v[0:r, 0:w], H, ALU.subtract), h_)

            def queries(tile, bank=6):
                p = pe(seq(*[mms(ps[:, bank, 128 * g:128 * g + 128],
                                 [(W["wq"][:, k, 128 * g:128 * g + 128], hT[:, k, 128 * tile:128 * tile + 128])
                                  for k in range(2)]) for g in range(2)]), t_h, t_w, free.get(bank))
                w = (p, t_c, bd.get((2 * tile - 1, 1)))
                for g in range(2):
                    o = ps[:, bank, 128 * g:128 * g + 128]
                    a = act(lambda e, g=g, o=o: e.activation(qTh[:, g, :], o, ACT.Identity, bias=bq[:, g:g + 1]), *w)
                for g in range(2):
                    o = ps[:, bank, 128 * g:128 * g + 128]
                    a = dve(lambda e, g=g, o=o: e.scalar_tensor_tensor(qTl[:, g, :], o, bq[:, g:g + 1], qTh[:, g, :],
                                                                       ALU.add, ALU.subtract), a)
                qTt[tile] = free[bank] = a

            def blockdiag(b, g):
                c = slice(64 * (b % 2), 64 * (b % 2) + 64)
                for q, s in ((qh, qTh), (ql, qTl)):
                    bd[b, g] = pool(lambda e, q=q, s=s: e.tensor_tensor(
                        q[g], s[:, g, c].unsqueeze(1).broadcast_to([128, 8, 64]),
                        mask0.unsqueeze(2).broadcast_to([128, 8, 64]), ALU.mult), qTt[b // 2], t_c, s_tok.get(8 * b - 5 + 4 * g))

            def turn_p(n, g):
                bank = 4 + g % 2
                fs = []
                for t in range(4 * g, min(4 * g + 4, KT)):
                    k = 128 if t < 12 else KL
                    fs.append(tr(ps[0:k, bank, 128 * (t % 4):128 * (t % 4) + 128], P[:, 128 * t:128 * t + k]))
                tr_done[n] = p = pe(seq(*fs), exa[n], exb[n], free.get(bank))
                k, c = (128, 512) if g < 3 else (KL, 128)
                H, L = [x_[0:k, 4 * g:4 * g + c // 128, 128 * (n % 2):128 * (n % 2) + 128] for x_ in (PTh, PTl)]
                src = ps[0:k, bank, 0:c].rearrange("p (a c) -> p a c", c=128)
                a = act(lambda e: e.copy(H, src), p, av.get(n // 2 - 1))
                free[bank] = ptt[n, g] = dve(lambda e: e.tensor_tensor(L, src, H, ALU.subtract), a)

            def scores(n, c):
                b, j = pairs[n]
                g = j // 4
                w = 400 + 2 * (c == 3)
                k = slice(400 * c, 400 * c + w)
                m = slice(2 * (j % 4), 2 * (j % 4) + 2)
                H, L = [q[g][:, m, :].rearrange("p a b -> p (a b)") for q in (qh, ql)]
                s_tok[n] = pe(mms(ps[:, c, 0:w], [(H, Kh[g][:, k]), (H, Kl[g][:, k]), (L, Kh[g][:, k])]),
                              (exa if c < 3 else exb).get(n - 1, free.get(c)), bd[b, g], kt[b, g])
                dve(lambda e: e.tensor_reduce(mx4[n % 2][:, c:c + 1], ps[:, c, 0:400 + (c == 3)], AX.X, ALU.max),
                    s_tok[n], exb.get(n - 2))

            def softmax(n):
                m = dve(lambda e: e.tensor_reduce(mx[n % 2], mx4[n % 2], AX.X, ALU.max, negate=True), (eng_sems["dve"], eng_sems["dve"].n))
                exa[n] = act(lambda e: e.activation(P[:, 0:1200].rearrange("p (a b) -> p a b", b=400), ps[:, 0:3, 0:400], ACT.Exp,
                                                    bias=mx[n % 2], accum_out=sums[n % 2][:, 0:1]),
                             m, tr_done.get(n - 1), *(split_tok[0, 3] if n == 0 else ()))
                exb[n] = act(lambda e: e.activation(P[:, 1200:NK], ps[:, 3, 0:401], ACT.Exp, bias=mx[n % 2],
                                                    accum_out=sums[n % 2][:, 1:2]), m)

            def values(m):
                b, g = m // 4, (m // 2) % 2
                o = ps[:, 7, 0:256]
                f = slice(128 * g, 128 * g + 128)
                for t in range(KT):
                    r = 128 if t < 12 else KL
                    H, L = Vh[b % 2][0:r, t, f], Vl[b % 2][0:r, t, f]
                    av[m] = pe(mms(o, [(H, PTh[0:r, t, :]), (H, PTl[0:r, t, :]), (L, PTh[0:r, t, :])], t == 0, t == KT - 1),
                               ptt[2 * m + 1, t // 4], free.get(7), vt[b])
                free[7] = oSt[m] = dve(lambda e: e.tensor_copy(oS, o), av[m], oSr.get(m - 1))

            def normalise(m):
                b = m // 4
                o = ps[:, 7, 0:256]
                oSr[m] = p = pe(seq(*[tr(o[:, 128 * i:128 * i + 128], oS[:, 128 * i:128 * i + 128]) for i in range(2)]), oSt[m], free[7])
                for i in range(2):
                    n = 2 * m + i
                    j = n % 8
                    free[7] = on[n] = dve(lambda e, i=i, j=j: e.scalar_tensor_tensor(
                        O[b % 2][:, j, :], o[:, 128 * i + 32 * (j % 4):128 * i + 32 * (j % 4) + 32], rc[i], own, ALU.mult, ALU.mult),
                        p, rct[n], t_c, turned.get((b - 2, 1)))

            def total(n):
                s_, r = sums[n % 2], rc[n % 2]
                a = dve(lambda e: e.tensor_tensor(r, s_[:, 0:1], s_[:, 1:2], ALU.add), exb[n], on.get(n - 2))
                rct[n] = dve(lambda e: e.reciprocal(r, r), a)

            def turn(b, g):
                o = ps[:, 6, 0:64]
                turned[b, g] = p = pe(mms(o, [(O[b % 2][:, 4 * g:4 * g + 4, :].rearrange("p a c -> p (a c)"), fold)]),
                                      on[8 * b + 4 * g + 3], free[6], t_c)
                free[6] = aTt[b, g] = dve(lambda e: e.tensor_scalar(aT[:, g, 64 * (b % 2):64 * (b % 2) + 64], o, bvc[:, g:g + 1], None, ALU.add),
                                          p, t_c, proj.get(b // 2 - 1))

            def project(tile):
                o = ps[:, 6, 0:256]
                proj[tile] = p = pe(mms(o, [(aT[:, g, :], W["wo"][:, g, :]) for g in range(2)]), free[6])
                free[6] = dve(lambda e: e.tensor_tensor(x[:, tile, :], o, x[:, tile, :], ALU.add), p, xb, toks[-1])
                moments(tile, free[6])

            load_raw(0)
            for k in ("wq", "wo"):
                t_w = load(W[k], d["x0_" + k], s_wq)
            t_b = load_bias(0, "x0_bo")
            t_zero = load(xs_d.rearrange("(i p) c -> p i c", p=128), zeros[:, :].unsqueeze(1).broadcast_to([128, NS, D]), s_zero, t_z)
            for c in range(4):
                split(0, c)
            toks = layernorm(t_x)
            for c in range(4):
                keys(0, 0, c, 2 + c)
            for q in range(2):
                vals(0, q, 6 + q)
            t_h = to_hT(toks)
            queries(0)
            blockdiag(0, 0)
            load_raw(1, t_h)

            xb = pool(lambda e: e.tensor_tensor(x[:, :, :], x[:, :, :],
                                                biasb[:, :].unsqueeze(1).broadcast_to([128, NT, D]), ALU.add), t_b, toks[-1])
            for n in range(N + 1):
                b, j = pairs[n] if n < N else (NB, 0)
                jobs = []
                if b < NB and j == 1:
                    jobs = [lambda c=c: keys(b, 1, c, 4 + c, c < 2) for c in range(4)]
                elif b + 1 < NB and j == 3:
                    jobs = [lambda q=q: vals(b + 1, q, 4 + q, q < 4) for q in range(4)]
                elif b + 1 < NB and j == 5:
                    jobs = [lambda c=c: keys(b + 1, 0, c, 4 + c, c < 2) for c in range(4)]
                elif b + 1 < NB and j == 7:
                    jobs = [lambda q=q: vals(b + 1, q, q, q < 5) for q in range(4, 7)]
                if j == 0 and b < NB:
                    blockdiag(b, 1)
                if j == 4 and b + 1 < NB:
                    blockdiag(b + 1, 0)
                if n >= 1:
                    turn_p(n - 1, 0)
                    turn_p(n - 1, 1)
                if n < N:
                    scores(n, 0)
                    scores(n, 1)
                if n >= 3 and n % 2 == 1:
                    normalise((n - 3) // 2)
                if n >= 4 and n % 4 == 2:
                    b2, j2 = pairs[n - 3]
                    turn(b2, j2 // 4)
                if n >= 1:
                    turn_p(n - 1, 2)
                if n < N:
                    scores(n, 2)
                if j == 3:
                    if b + 2 < NB:
                        load_raw(b + 2)
                if n >= 1:
                    turn_p(n - 1, 3)
                if n < N:
                    scores(n, 3)
                    softmax(n)
                if j == 2 and b + 1 < NB:
                    for c in range(4):
                        split(b + 1, c)
                if n == 0:
                    jobs = [lambda q=q: vals(0, q, 4 + q % 4) for q in range(2, 7)]
                for f in jobs:
                    f()
                if n >= 1:
                    total(n - 1)
                if n >= 3 and b % 2 == 0 and j == 2:
                    project(b // 2 - 1)
                if j == 2 and b % 2 == 1 and b + 1 < NB:
                    queries((b + 1) // 2)
                if n >= 1 and n % 2 == 0:
                    values(n // 2 - 1)
            normalise(N // 2 - 1)
            turn(NB - 1, 1)
            project(NT - 1)
            return t_b, t_zero, [cread[NB - 1]]

        def xattn(tag, W, G, hpg, mask, t_w, t_b, ends):
            H = G * hpg
            NP = H // 2
            PPG = hpg // 2
            NH = hpg * 64
            aw, ar, arr = Carve(wsb), Carve(arena), Carve(arenaR)
            raw2, P, rawn = aw(128, NK), aw(128, NK), aw(128, KT, 192)
            qT = [aw(128, G, 128) for _ in range(2)]
            qbd = [aw(128, H, 64) for _ in range(2)]
            oT1, oT2 = aw(128, H, 128), ar(64, H, 128)
            On = [ar(128, 192) for _ in range(2)]
            Ol = ar(128, 192)
            aT = ar(128, G, 128)
            mx4, mx = [ar(128, 4) for _ in range(2)], [ar(128, 1) for _ in range(2)]
            rc = [ar(128, 1) for _ in range(2)]
            c1h, c1l, c2 = [[arr(128, NK + 1) for _ in range(2)] for _ in range(3)]
            cN = [arr(128, KT, 386) for _ in range(2)]
            PTh, PTl = [arr(128, KT, 128) for _ in range(2)]
            qh, ql = [arr(128, 2, H * 64) for _ in range(2)]
            s_raw = sem(f"{tag}raw")
            s_cn = sem(f"{tag}cn")

            for i in range(2):
                for col, v in ((192, 1.0), (193, 0.0)):
                    dve(lambda e, i=i, col=col, v=v: e.memset(cN[i][:, :, col:col + 1].bitcast(F32), v))
                for c in (c1h, c1l, c2):
                    t_ones = dve(lambda e, i=i, c=c: e.memset(c[i][:, NK:NK + 1].bitcast(F32), 0.0))

            pairs = [(b, j) for b in range(NB) for j in range(NP)]
            N = len(pairs)
            raw_tok, cn_tok, split_tok, part_tok = {}, {}, {}, {}
            exa, exb, s_tok, tr_done, av, on, otr, oTt = {}, {}, {}, {}, {}, {}, {}, {}
            qTt, qd, qq, atile = {}, {}, {}, {}
            qread = {}
            evs = [None, None]
            xfree = [None]
            at_free = [None]

            def raw1(b):
                return h[:, :, :].rearrange("p a b -> p (a b)")[:, 0:NK] if b else P

            def load_raw(b, *w):
                if b:
                    w += tuple(t for c in range(4) for t in split_tok[b - 1, c])
                load(raw1(b), d["ctxT"][b, 0:128, :], s_raw, *w)
                load(raw2[0:64, :], d["ctxT"][b, 128:192, :], s_raw, *w)
                raw_tok[b] = load(raw2[64:128, :], d["ctxT"][b, 128:192, :], s_raw)

            def load_cn(b):
                w = part_tok.get(b - 1, t_ones)
                load(rawn[:, 0:12, :], d["ctx"][b, 0:1536, :].rearrange("(t p) c -> p t c", p=128), s_cn, w)
                cn_tok[b] = load(rawn[0:KL, 12, :], d["ctx"][b, 1536:NK, :], s_cn)

            def split_keys(b, c):
                o = cN[b % 2]
                w = (cn_tok[b], av.get((b - 1) * NP - 1))
                t0, t1 = (0, 4, 7, 10)[c], (4, 7, 10, 12)[c]
                for k, t in [(128, slice(t0, t1))] + ([(KL, slice(12, 13))] if c == 3 else []):
                    p = pool(lambda e, k=k, t=t: e.tensor_copy(o[0:k, t, 0:192], rawn[0:k, t, :]), *w)
                    part_tok[b] = pool(lambda e, k=k, t=t: e.tensor_tensor(o[0:k, t, 194:386], rawn[0:k, t, :],
                                                                           o[0:k, t, 0:192], ALU.subtract), p)

            def split(b, c):
                i = b % 2
                k = slice(400 * c, 400 * c + 400 + (c == 3))
                w = (raw_tok[b], s_tok.get((b - 1) * NP - 1), t_ones)
                a1 = act(lambda e: e.copy(c1h[i][:, k], raw1(b)[:, k]), *w)
                a2 = act(lambda e: e.copy(c2[i][:, k], raw2[:, k]), *w)
                p1 = pool(lambda e: e.tensor_tensor(c1l[i][:, k], raw1(b)[:, k], c1h[i][:, k], ALU.subtract), a1)
                split_tok[b, c] = [a1, p1, a2]

            def split_low(b, c):
                i = b % 2
                k = slice(400 * c, 400 * c + 400 + (c == 3))
                t = split_tok[b, c]
                t[2] = dve(lambda e: e.tensor_tensor(c2[i][64:128, k], raw2[64:128, k], c2[i][64:128, k], ALU.subtract), t[2])

            def queries(tile):
                i = tile % 2
                p = pe(seq(*[mms(ps[:, 7, 128 * g:128 * g + 128],
                                 [(W["wq"][:, k, 128 * g:128 * g + 128], hT[:, k, 128 * tile:128 * tile + 128])
                                  for k in range(2)]) for g in range(G)]), t_h, t_w, xfree[0])
                src = ps[:, 7, 0:128 * G].rearrange("p (g n) -> p g n", n=128)
                w = (p, qd.get(2 * tile - 3))
                t = dve(lambda e: e.tensor_copy(qT[i], src), *w)
                qTt[tile] = xfree[0] = t

            def blockdiag(b):
                i = b % 2
                s = qT[(b // 2) % 2][:, :, 64 * i:64 * i + 64]
                for g in range(G):
                    t = pool(lambda e, g=g: e.tensor_tensor(
                        qbd[i][:, g * hpg:(g + 1) * hpg, :], s[:, g, :].unsqueeze(1).broadcast_to([128, hpg, 64]),
                        mask.unsqueeze(2).broadcast_to([128, hpg, 64]), ALU.mult), qTt[b // 2], qread.get(b - 2), t_c)
                qd[b] = t

            def absorb(b, g):
                i = b % 2
                qs = qbd[i][:, g * hpg:(g + 1) * hpg, :].rearrange("p a b -> p (a b)")
                sl = slice(g * NH, (g + 1) * NH)
                w = s_tok.get((b - 1) * NP + (g + 1) * PPG - 1) if b else None
                p = pe(seq(*[mms(ps[:, 7, NH * part:NH * part + NH], [(W["wk"][:, g, 128 * part:128 * part + 128], qs)])
                             for part in range(2)]), qd[b], xfree[0], t_w)
                o = ps[:, 7, 0:2 * NH].rearrange("p (a c) -> p a c", c=NH)
                a = act(lambda e: e.copy(qh[:, :, sl], o), p, w)
                xfree[0] = dve(lambda e: e.tensor_tensor(ql[:, :, sl], o, qh[:, :, sl], ALU.subtract), a)
                qread[b] = p
                qq[b, g] = xfree[0]

            def turn_p(n, g):
                bank = 4 + g % 2
                fs = []
                for t in range(4 * g, min(4 * g + 4, KT)):
                    k = 128 if t < 12 else KL
                    fs.append(tr(ps[0:k, bank, 128 * (t % 4):128 * (t % 4) + 128], P[:, 128 * t:128 * t + k]))
                p = pe(seq(*fs), exa[n], exb[n], evs[g % 2])
                k, c = (128, 512) if g < 3 else (KL, 128)
                hi, lo = [v[0:k, 4 * g:4 * g + c // 128, :].rearrange("p a b -> p (a b)") for v in (PTh, PTl)]
                src = ps[0:k, bank, 0:c]
                a = act(lambda e: e.copy(hi, src), p, av.get(n - 1))
                evs[g % 2] = dve(lambda e: e.tensor_tensor(lo, src, hi, ALU.subtract), a)
                tr_done[n] = p

            def scores(n, c):
                b, j = pairs[n]
                i = b % 2
                g = j // PPG
                k0, k1 = 400 * c, 400 * c + (400 if c < 3 else 402)
                m = slice(128 * j, 128 * j + 128)
                k = slice(k0, k1)
                s_tok[n] = pe(mms(ps[:, c, 0:k1 - k0], [(qh[:, 0, m], c1h[i][:, k]), (qh[:, 0, m], c1l[i][:, k]), (ql[:, 0, m], c1h[i][:, k]),
                                                        (qh[:, 1, m], c2[i][:, k]), (ql[:, 1, m], c2[i][:, k])]),
                              exa.get(n - 1) if c < 3 else exb.get(n - 1), qq[b, g], *split_tok[b, c], t_ones)
                dve(lambda e: e.tensor_reduce(mx4[n % 2][:, c:c + 1], ps[:, c, 0:400 + (c == 3)], AX.X, ALU.max),
                    s_tok[n], exb.get(n - 2))

            def softmax(n):
                m = dve(lambda e: e.tensor_reduce(mx[n % 2], mx4[n % 2], AX.X, ALU.max, negate=True), (eng_sems["dve"], eng_sems["dve"].n))
                bias = mx[n % 2]
                exa[n] = act(lambda e: e.activation(P[:, 0:1200].rearrange("p (a b) -> p a b", b=400), ps[:, 0:3, 0:400], ACT.Exp, bias=bias),
                             m, tr_done.get(n - 1), *(t for c in range(4) for t in (split_tok[0, c] if n == 0 else ())))
                exb[n] = act(lambda e: e.activation(P[:, 1200:NK], ps[:, 3, 0:401], ACT.Exp, bias=bias), m)

            def values(n):
                b, j = pairs[n]
                o, c = ps[:, 6, 0:386], cN[b % 2]

                def f(e):
                    for t in range(KT):
                        k = 128 if t < 12 else KL
                        two = [(o, PTh, 386), (o[:, 0:256], PTl, 256)]
                        for i, (ot, pt, w) in enumerate(two if t < 12 else two[::-1]):
                            m = e.matmul(ot, pt[0:k, t, :], c[0:k, t, 0:w], start=(t + i == 0), stop=(t + i == 13))
                    return m
                av[n] = pe(f, evs[0], evs[1], on.get(n - 1), part_tok[b], t_ones)
                r = dve(lambda e: e.reciprocal(rc[n % 2], o[:, 192:193]), av[n])
                r = dve(lambda e: e.tensor_scalar(Ol, o[:, 194:386], rc[n % 2], None, ALU.mult), r)
                on[n] = dve(lambda e: e.scalar_tensor_tensor(On[n % 2], o[:, 0:192], rc[n % 2], Ol, ALU.mult, ALU.add), r, otr.get(n - 2))

            def turn(n):
                b, j = pairs[n]
                o1, o2 = ps[:, 7, 0:128], ps[0:64, 7, 128:256]
                p = pe(seq(tr(o1, On[n % 2][:, 0:128]), tr(o2, On[n % 2][:, 128:128 + 64])), on[n], xfree[0])
                otr[n] = p
                c = 64 * (b % 2)
                w = (p, atile.get(b // 2 - 1))
                dve(lambda e: e.tensor_copy(oT1[:, 2 * j:2 * j + 2, c:c + 64], o1.rearrange("p (a q) -> p a q", a=2)), *w)
                xfree[0] = oTt[n] = dve(lambda e: e.tensor_copy(oT2[0:64, 2 * j:2 * j + 2, c:c + 64],
                                                                o2.rearrange("p (a q) -> p a q", a=2)), *w)

            def project(tile):
                last = oTt[(2 * tile + 2) * NP - 1]
                fs = []
                for g in range(G):
                    prs = []
                    for hh in range(g * hpg, (g + 1) * hpg):
                        prs += [(W["wv1"][:, hh, :], oT1[:, hh, :]), (W["wv2"][0:64, hh, :], oT2[0:64, hh, :])]
                    fs.append(mms(ps[:, 7, 128 * g:128 * g + 128], prs))
                p = pe(seq(*fs), last, xfree[0])
                atile[tile] = p
                c = act(lambda e: e.copy(aT.rearrange("p a b -> p (a b)"), ps[:, 7, 0:128 * G]), p, at_free[0])
                o = ps[:, 7, 0:256]
                p = pe(mms(o, [(aT[:, g, :], W["wo"][:, g, :]) for g in range(G)]), c)
                at_free[0] = p
                xfree[0] = dve(lambda e: e.tensor_tensor(x[:, tile, :], o, x[:, tile, :], ALU.add), p, xb, toks[-1])
                moments(tile, xfree[0])

            load_raw(0, *ends)
            load_cn(0)
            toks = layernorm(t_x)
            for c in range(4):
                split(0, c)
            t_h = to_hT(toks)
            for c in range(4):
                split_low(0, c)
            load_raw(1, t_h)
            queries(0)
            blockdiag(0)
            for g in range(G):
                absorb(0, g)
            xb = pool(lambda e: e.tensor_tensor(x[:, :, :], x[:, :, :],
                                                biasb[:, :].unsqueeze(1).broadcast_to([128, NT, D]), ALU.add), t_b, toks[-1])

            for n in range(N + 1):
                if n < N:
                    b, j = pairs[n]
                    if j == 0 and b + 1 < NB:
                        if (b + 1) % 2 == 0:
                            queries((b + 1) // 2)
                        blockdiag(b + 1)
                if n == 0:
                    for c in range(4):
                        split_keys(0, c)
                    load_cn(1)
                if n >= 1:
                    turn_p(n - 1, 0)
                    turn_p(n - 1, 1)
                if n < N:
                    scores(n, 0)
                    scores(n, 1)
                if n >= 1:
                    turn_p(n - 1, 2)
                    turn_p(n - 1, 3)
                if n < N:
                    scores(n, 2)
                    scores(n, 3)
                    softmax(n)
                    if b + 1 < NB:
                        split(b + 1, j)
                if n >= 2:
                    turn(n - 2)
                    b2, j2 = pairs[n - 2]
                    if j2 == NP - 1 and b2 % 2 == 1:
                        project(b2 // 2)
                if n < N and b + 1 < NB:
                    split_low(b + 1, j)
                if n >= 1:
                    values(n - 1)
                if n < N and b + 1 < NB:
                    split_keys(b + 1, j)
                    if j == 3 and b + 2 < NB:
                        load_raw(b + 2)
                        load_cn(b + 2)
                    absorb(b + 1, j)
            turn(N - 1)
            project(NT - 1)

        fresh("x0")
        s_zero = sem("zero")
        t_z = pool(lambda e: e.memset(zeros[:, :], 0.0))
        if first <= 1:
            t_b, t_zero, t_early = latents(t_w0)
        else:
            t_zero = load(xs_d.rearrange("(i p) c -> p i c", p=128), zeros[:, :].unsqueeze(1).broadcast_to([128, NS, D]), s_zero, t_z)
            t_b, t_early = load_bias(0, "x0_bo"), []

        t_end = fresh("x0e")
        first_ctx.close()
        second_ctx = ExitStack()
        ctx.callback(second_ctx.close)
        wsb = second_ctx.enter_context(nc.sbuf_tensor("wsb", [128, 9216], F32))
        wc = Carve(wsb)
        aWq, aWkv, aWout = wc(128, 2, 1024), wc(128, 2, 1024), wc(128, 4, 256)
        fw1, fw2 = wc(128, 2, 1024), wc(128, 8, 256)

        for dst, n in ((aWq, "a_wq"), (aWkv, "a_wkv"), (aWout, "a_wout")):
            t_w1 = load(dst, d[n], s_w[1], *t_early)

        for dst, n in ((fw1, "f_w1"), (fw2, "f_w2")):
            t_w2 = load(dst, d[n], s_w[2], *t_end)

        def load_x1(*w):
            for k in ("wq", "wk", "wv1", "wv2", "wo"):
                t = load(X1[k], d["x1_" + k], s_w[3], *w)
            return t

        if first > 1:
            for k in ("pe", "dve", "act", "pool", "sp"):
                op(k, None, t_x, t_c, t_w0, t_w1, t_w2, t_b)
        def selfattn(sa_ctx):
            ends = fresh("sa")
            arena = sa_ctx.enter_context(nc.sbuf_tensor("sa", [128, 20900], F32))
            pr_ctx = ExitStack()
            parts = Carve(pr_ctx.enter_context(nc.sbuf_tensor("sap", [128, 12288], F32R)))
            aWqh, aWql, aWkvh, aWkvl, hTh, hTl = [parts(128, 2, 1024) for _ in range(6)]
            ar, ah = Carve(arena), Carve(h[:, :, :].rearrange("p a b -> p (a b)"))
            caus = ar(128, 128)
            t_cm = load(caus, d["causal"], s_cm, *ends)
            qk = ar(128, NT, 24, 64)
            vx = ar(128, NT, 8, 65)
            s1, s2, s3 = ar(128, NT, 24), ar(128, NT, 24), ar(128, NT, 24)
            rr = [ar(128, 16) for _ in range(2)]
            sq = [ar(128, 24, 64) for _ in range(2)]
            o1, o2, oT = ah(128, 16, 64), ah(128, 8, 64), ah(128, 4, 128)
            o14 = o1.rearrange("p (a b j) c -> p a b j c", a=2, j=2)
            g1 = dve(lambda e: e.tensor_scalar(qg, qg, 1.0, 8.0, ALU.add, ALU.mult), t_c)
            g2 = dve(lambda e: e.tensor_scalar(kg, kg, 1.0, 8.0, ALU.add, ALU.mult), t_c)
            g2 = dve(lambda e: e.tensor_tensor(qg, qg, kg, ALU.mult), g1, g2)
            wp = {}

            def split_w(i, c):
                w, hi, lo = ((aWq, aWqh, aWql), (aWkv, aWkvh, aWkvl))[i]
                u = slice(512 * c, 512 * c + 512)
                a = act(lambda e: e.copy(hi[:, :, u], w[:, :, u]), t_w1)
                wp[2 * i + c] = pool(lambda e: e.tensor_tensor(lo[:, :, u], w[:, :, u], hi[:, :, u], ALU.subtract), a)

            split_w(0, 0)
            toks = layernorm(rms=True)
            for i, c in ((0, 1), (1, 0), (1, 1)):
                split_w(i, c)
            pone = pool(lambda e: e.memset(vx[:, :, :, 64:65], 1.0))
            t_h = {}

            def split_h(half, *w):
                u = slice(512 * half, 512 * half + 512)
                a = act(lambda e: e.copy(hTh[:, :, u], hT[:, :, u]), *w)
                t_h[half] = dve(lambda e: e.tensor_tensor(hTl[:, :, u], hT[:, :, u], hTh[:, :, u], ALU.subtract), a)

            res = to_hT(toks, scale=normw, after=split_h)
            free = {b: res for b in range(8)}
            sqsum, vt, qn, knt, ev, st_, ms, on, oread = {}, {}, {}, {}, {}, {}, {}, {}, {}

            def bank(t, i):
                return 4 * (t % 2) + i

            def place(t, i, n=128):
                return psf[:, 2048 * (t % 2) + 128 * i:2048 * (t % 2) + 128 * i + n]

            def project(t):
                b0 = bank(t, 0)
                u = slice(128 * t, 128 * t + 128)
                for c in range(4):
                    hi, lo = (aWqh, aWql) if c < 2 else (aWkvh, aWkvl)
                    o = slice(512 * (c % 2), 512 * (c % 2) + 512)
                    p = pe(mms(ps[:, b0 + c, :], [pair for k in range(2) for pair in (
                        (hTh[:, k, u], hi[:, k, o]), (hTl[:, k, u], hi[:, k, o]), (hTh[:, k, u], lo[:, k, o]))]),
                        t_h[t // 4], wp[c], *[free[b0 + i] for i in range(4)])
                src = psf[:, 512 * b0:512 * b0 + 1536].rearrange("p (a c) -> p a c", c=64)
                c = dve(lambda e: e.tensor_copy(qk[:, t, :, :], src), p)
                a = act(lambda e: e.activation(sq[t % 2], src, ACT.Square), p, sqsum.get(t - 2), c)
                vt[t] = act(lambda e: e.copy(vx[:, t, :, 0:64], ps[:, b0 + 3, :].rearrange("p (a c) -> p a c", c=64)), p)
                for i in range(4):
                    free[b0 + i] = vt[t]
                sqsum[t] = dve(lambda e: e.tensor_reduce(s1[:, t, :], sq[t % 2], AX.X, ALU.add), a)

            def norms(half):
                u = slice(4 * half, 4 * half + 4)
                c = act(lambda e: e.activation(s2[:, u, :], s1[:, u, :], ACT.Sqrt), sqsum[4 * half + 3])
                c = dve(lambda e: e.tensor_scalar(s2[:, u, :], s2[:, u, :], 1e-12, None, ALU.max), c)
                return dve(lambda e: e.reciprocal(s3[:, u, :], s2[:, u, :]), c)

            def normalise(t, w):
                knt[t] = pool(lambda e: e.tensor_tensor(qk[:, t, 16:24, :], qk[:, t, 16:24, :],
                                                        s3[:, t, 16:24].unsqueeze(2).broadcast_to([128, 8, 64]), ALU.mult), w)
                qn[t] = pool(lambda e: e.tensor_tensor(qk[:, t, 0:16, :], qk[:, t, 0:16, :],
                                                       s3[:, t, 0:16].unsqueeze(2).broadcast_to([128, 16, 64]), ALU.mult), w)

            def turn_q(t):
                b0 = bank(t, 0)
                p = pe(seq(*[tr(place(t, i), qk[:, t, 2 * i:2 * i + 2, :].rearrange("p a c -> p (a c)")) for i in range(8)]),
                       qn[t], free[b0], free[b0 + 1])
                free[b0] = free[b0 + 1] = ev[t, 0] = dve(lambda e: e.tensor_tensor(
                    qTs[t % 2], place(t, 0, 1024).rearrange("p (a c) -> p a c", c=128), qg.unsqueeze(2).broadcast_to([128, 8, 128]), ALU.mult),
                    p, g2, st_.get(t - 2))

            def turn_k(t):
                b0 = bank(t, 0)
                p = pe(seq(*[tr(place(t, 8 + i), qk[:, t, 16 + 2 * i:18 + 2 * i, :].rearrange("p a c -> p (a c)")) for i in range(4)]),
                       knt[t], free[b0 + 2])
                free[b0 + 2] = ev[t, 1] = act(lambda e: e.copy(
                    kTs[t % 2], place(t, 8, 512).rearrange("p (a c) -> p a c", c=128)), p, st_.get(t - 2))

            def scores(t):
                b, b0 = t % 2, bank(t, 0)
                for half in range(2):
                    u = slice(64 * half, 64 * half + 64)
                    st_[t] = p = pe(seq(*[mms(place(t, 8 * half + 2 * i, 256), [(kTs[b][u, i, :],
                                                                                 qTs[b][u, 2 * i:2 * i + 2, :].rearrange("p a c -> p (a c)"))])
                                          for i in range(4)]), ev[t, 0], ev[t, 1], free[b0 + 2 * half], free[b0 + 2 * half + 1])
                    Eh = E[b][:, 8 * half:8 * half + 8, :]
                    a = act(lambda e, half=half, Eh=Eh: e.activation(Eh, place(t, 8 * half, 1024).rearrange("p (a c) -> p a c", c=128),
                                                                     ACT.Tanh, scale=1.0 / 50.0), p, oread.get(t - 2))
                    free[b0 + 2 * half] = free[b0 + 2 * half + 1] = a
                    a = act(lambda e, Eh=Eh: e.activation(Eh, Eh, ACT.Exp, scale=6.25), a)
                    ms[t, half] = dve(lambda e, Eh=Eh: e.tensor_tensor(Eh, Eh, caus.unsqueeze(1).broadcast_to([128, 8, 128]), ALU.mult), a, t_cm)

            def output(t):
                b, b0 = t % 2, bank(t, 0)
                for half in range(2):
                    p = pe(seq(*[mms(place(t, 8 * half + i, 65), [(E[b][:, 8 * half + i, :], vx[:, t, i // 2 * 2 + half, :])]) for i in range(8)]),
                           ms[t, half], vt[t], pone, free[b0 + 2 * half], free[b0 + 2 * half + 1])
                    oread[t] = p
                    OO = place(t, 8 * half, 1024).rearrange("p (a c) -> p a c", c=128)
                    u = slice(8 * half, 8 * half + 8)
                    r = dve(lambda e, OO=OO, u=u: e.reciprocal(rr[b][:, u], OO[:, :, 64]), p)
                    r = dve(lambda e, OO=OO, u=u: e.tensor_tensor(o1[:, u, :], OO[:, :, 0:64],
                                                                  rr[b][:, u].unsqueeze(2).broadcast_to([128, 8, 64]), ALU.mult), r)
                    free[b0 + 2 * half] = free[b0 + 2 * half + 1] = r
                on[t] = dve(lambda e: e.tensor_tensor(o2.rearrange("p (b a) c -> p a b c", a=2), o14[:, :, :, 0, :], o14[:, :, :, 1, :], ALU.add), r, last[0])

            def finish(t):
                b0 = bank(t, 0)
                p = pe(seq(*[tr(ps[:, b0 + 3, 128 * i:128 * i + 128], o2[:, 2 * i:2 * i + 2, :].rearrange("p a c -> p (a c)"))
                             for i in range(4)]), on[t], free[b0 + 3])
                last[0] = p
                c = free[b0 + 3] = act(lambda e: e.copy(oT.rearrange("p a c -> p (a c)"), ps[:, b0 + 3, :]), p, last[1])
                last[1] = p = pe(mms(ps[:, b0 + 3, 0:256], [(oT[:, k, :], aWout[:, k, :]) for k in range(4)]), c, free[b0 + 3])
                free[b0 + 3] = dve(lambda e: e.tensor_tensor(x[:, t, :], ps[:, b0 + 3, 0:256], x[:, t, :], ALU.add), p)
                moments(t, free[b0 + 3])

            last = [None, None]
            for t in range(4):
                project(t)
            w = norms(0)
            for t in range(4):
                normalise(t, w) if t < 2 else None
                project(4 + t)
            w2 = norms(1)
            pr_ctx.close()
            at = Carve(sa_ctx.enter_context(nc.sbuf_tensor("sat", [128, 7168], F32)))
            qTs, kTs = [at(128, 8, 128) for _ in range(2)], [at(128, 4, 128) for _ in range(2)]
            E = [at(128, 16, 128) for _ in range(2)]
            turn_q(0)
            turn_k(0)
            scores(0)
            for t in range(1, NT + 2):
                if t < NT:
                    turn_q(t)
                if t >= 2:
                    finish(t - 2)
                if t < NT:
                    turn_k(t)
                if t + 1 < NT:
                    normalise(t + 1, w if t + 1 < 4 else w2)
                if t - 1 < NT:
                    output(t - 1)
                if t < NT:
                    scores(t)

        def ffn(arenaR, arena):
            ends = fresh("ff")
            tw = load_x1(*ends)
            t_b = load_bias(1, "f_b2", *ends)
            arr = Carve(arenaR)
            hTh, hTl = [arr(128, 2, 1024) for _ in range(2)]
            w1h, w1l = [arr(128, 2, 1024) for _ in range(2)]
            w2h, w2l = [arr(128, 8, 256) for _ in range(2)]
            gTh, gTl = [arr(128, 8, 1024) for _ in range(2)]
            gs = [arena[:, 512 * i:512 * i + 512] for i in range(2)]
            t_p = []
            for w, hi, lo in ((fw1, w1h, w1l), (fw2, w2h, w2l)):
                a = act(lambda e, w=w, hi=hi: e.copy(hi, w), t_w2)
                t_p.append(pool(lambda e, w=w, hi=hi, lo=lo: e.tensor_tensor(lo, w, hi, ALU.subtract), a))
            toks = layernorm()
            xb = pool(lambda e: e.tensor_tensor(x[:, :, :], x[:, :, :],
                                                biasb[:, :].unsqueeze(1).broadcast_to([128, NT, D]), ALU.add), t_b, toks[-1])
            t_h = to_hT(toks, parts=(hTh, hTl))
            g, hi_ = {}, {}
            n = 0
            for half in range(2):
                u = slice(512 * half, 512 * half + 512)
                for f in range(8):
                    bank = 2 + n % 4
                    o = slice(128 * f, 128 * f + 128)
                    p = pe(mms(ps[:, bank, :], [pair for k in range(2) for pair in (
                        (w1h[:, k, o], hTh[:, k, u]), (w1h[:, k, o], hTl[:, k, u]), (w1l[:, k, o], hTh[:, k, u]))]),
                        t_h, t_p[0], hi_.get(n - 4))
                    a = act(lambda e, f=f, bank=bank, n=n: e.activation(gs[n % 2], ps[:, bank, :], ACT.Gelu, bias=b1c[:, f:f + 1]), p, g.get(n - 2))
                    hi_[n] = act(lambda e, f=f, u=u, n=n: e.copy(gTh[:, f, u], gs[n % 2]), a)
                    g[n] = dve(lambda e, f=f, u=u, n=n: e.tensor_tensor(gTl[:, f, u], gs[n % 2], gTh[:, f, u], ALU.subtract), hi_[n])
                    n += 1
            y = {}
            for t in range(NT):
                bank = 6 + t % 2
                o = slice(128 * t, 128 * t + 128)
                p = pe(mms(ps[:, bank, 0:256], [pair for f in range(8) for pair in (
                    (gTh[:, f, o], w2h[:, f, :]), (gTh[:, f, o], w2l[:, f, :]), (gTl[:, f, o], w2h[:, f, :]))]),
                    g[7 if t < 4 else 15], t_p[1], y.get(t - 2))
                y[t] = dve(lambda e, t=t, bank=bank: e.tensor_tensor(x[:, t, :], ps[:, bank, 0:256], x[:, t, :], ALU.add), p, xb)
                moments(t, y[t])
            return tw

        def memory():
            ar = Carve(third)
            tk, tv, tq = ar(128, 2, 256), ar(128, 2, 256), ar(128, 2, 256)
            W1T, W2T, W2 = ar(128, 2, 64), ar(64, 256), ar(128, 2, 64)
            for dst, n in ((tk, "t_k"), (tv, "t_v"), (tq, "t_q")):
                t_w = load(dst, d[n], s_w[4], *ends5)
            ends = ends5
            for dst, n in ((W1T, "t_W1T"), (W2T, "t_W2T"), (W2, "t_W2")):
                t_p = load(dst, d[n], s_w[5], *ends)
            load_moe()
            zT, eT, qT = ar(128, 2, 1024), ar(128, 2, 1024), ar(128, 2, 1024)
            z = ar(64, NB, 256)
            wd = ar(128, 2, 256)
            hTs, hs2, us, u, m1, sqv, th, nu, de, ph, gp, da, gq, one = [ar(64, 64) for _ in range(14)]
            hs2_, dr = [ar(64, 64) for _ in range(2)], ar(64, 256)
            drT, eb = ar(128, 2, 64), ar(128, 2, 64)
            qb_ = [ar(128, 2, 64) for _ in range(2)]
            gb2 = ar(128, 2)
            b1r = ar(1, 64)
            toks = layernorm()
            t_h = to_hT(toks)
            t_d = dve(lambda e: e.tensor_tensor(wd, tk, tv, ALU.subtract), t_w)
            n = 0
            ev = {}

            def evac(n, o, i_, p):
                if n % 2:
                    ev[n] = act(lambda e: e.copy(o, i_), p)
                else:
                    ev[n] = dve(lambda e: e.tensor_copy(o, i_), p)

            for W, T in ((tk, zT), (wd, eT), (tq, qT)):
                for m in range(2):
                    for half in range(2):
                        bank = n % 4
                        p = pe(mms(ps[:, bank, :], [(W[:, k, 128 * m:128 * m + 128], hT[:, k, 512 * half:512 * half + 512])
                                                    for k in range(2)]), t_h, t_w, t_d, ev.get(n - 4))
                        evac(n, T[:, m, 512 * half:512 * half + 512], ps[:, bank, :], p)
                        n += 1
            for b in range(0, NB, 2):
                bank = n % 4
                p = pe(seq(*[tr(ps[0:64, bank, 256 * i + 128 * k:256 * i + 128 * k + 128], zT[:, k, 64 * (b + i):64 * (b + i) + 64])
                             for i in range(2) for k in range(2)]), ev.get(n - 4), ev[2], ev[3])
                evac(n, z[:, b:b + 2, :].rearrange("p a c -> p (a c)"), ps[0:64, bank, :], p)
                n += 1
            t_in = [ev[n - 1], ev[n - 2]]
            C = 0.001 * 2.0 / (NQ * D)
            C0 = 0.3989422804014327

            def update(dst, src, *w):
                return dve(lambda e: e.scalar_tensor_tensor(dst, src, -C, dst, ALU.mult, ALU.add), *w)

            uW1 = uW2 = ub1 = ub2 = t_p
            uW2T = t_p
            ans = None
            eb_ = pool(lambda e: e.tensor_tensor(eb, eT[:, :, 0:64], tb2.unsqueeze(2).broadcast_to([128, 2, 64]), ALU.add), *t_in, t_c)

            def answer_first(t, uW1, ub1):
                tt = slice(64 * t, 64 * t + 64)
                p = pe(mms(ps[0:64, 7, 0:64], [(W1T[:, k, :], qT[:, k, tt]) for k in range(2)]), uW1)
                return act(lambda e: e.activation(gq, ps[0:64, 7, 0:64], ACT.Gelu, bias=tb1), p, ub1)

            def answer_second(t, g, uW2T):
                return pe(seq(*[mms(ps[:, 7, 64 + 64 * m:128 + 64 * m], [(W2T[:, 128 * m:128 * m + 128], gq)]) for m in range(2)]), g, uW2T)

            def answer_add(t, p, g, qb):
                tt = slice(64 * t, 64 * t + 64)
                dve(lambda e: e.tensor_tensor(qT[:, :, tt], ps[:, 7, 64:192].rearrange("p (a c) -> p a c", c=64), qb_[t % 2], ALU.add), p, g, qb)

            t_one = pool(lambda e: e.memset(one, 1.0))
            p = pe(tr(ps[0:1, 3, 0:64], tb1, 64), t_c, *t_in)
            ub1r = dve(lambda e: e.tensor_copy(b1r, ps[0:1, 3, 0:64]), p)
            qb = None
            for t in range(NB):
                tt = slice(64 * t, 64 * t + 64)
                pu = pe(mms(ps[0:64, 3, 0:64], [(zT[:, k, tt], W1T[:, k, :]) for k in range(2)] + [(one[0:1, :], b1r)]), ub1r, t_one, *t_in, uW1)
                pa = pe(mms(ps[0:64, 0, 0:64], [(W1T[:, k, :], zT[:, k, tt]) for k in range(2)]))
                ah = act(lambda e: e.activation(hTs, ps[0:64, 0, 0:64], ACT.Gelu, bias=tb1), pa, ub1, t_c)
                if t:
                    p7 = pe(seq(*[mms(ps[:, 5, 256 + 64 * m:320 + 64 * m], [(dr[:, 128 * m:128 * m + 128], hs2_[(t - 1) % 2])])
                                  for m in range(2)]))
                a = dve(lambda e: e.tensor_copy(u, ps[0:64, 3, 0:64]), pu)
                hs = hs2_[t % 2]
                hs_ = act(lambda e, hs=hs: e.activation(hs, u, ACT.Gelu), a)
                sq_ = dve(lambda e: e.tensor_tensor(sqv, u, u, ALU.mult), a)
                m_ = dve(lambda e: e.tensor_scalar(m1, sqv, 1e-24, 2e-12, ALU.is_lt, ALU.mult), sq_)
                us_ = dve(lambda e: e.tensor_tensor(us, u, m1, ALU.add), m_)
                at = act(lambda e: e.activation(th, sqv, ACT.Tanh, scale=-0.25), sq_)
                a2 = act(lambda e: e.activation(hs2, us, ACT.Gelu), us_)
                pb = pe(seq(*[mms(ps[:, 1, 64 * m:64 * m + 64], [(W2T[:, 128 * m:128 * m + 128], hTs)]) for m in range(2)]), ah, uW2T)
                if t:
                    gq_ = answer_first(t - 1, uW1, ub1)
                r2 = dve(lambda e: e.reciprocal(gp, us), us_)
                if t:
                    uW2 = update(W2.rearrange("p a b -> p (a b)"), ps[:, 5, 256:384], p7)
                r1 = dve(lambda e: e.tensor_scalar(de, th, -1.0, 1.0, ALU.mult, ALU.add), at)
                dT = dve(lambda e: e.tensor_tensor(drT, ps[:, 1, 0:128].rearrange("p (a c) -> p a c", c=64), eb, ALU.add), pb, eb_)
                r1 = dve(lambda e: e.reciprocal(de, de), r1)
                r = dve(lambda e: e.scalar_tensor_tensor(nu, th, 1.0, u, ALU.add, ALU.mult), at)
                r2 = dve(lambda e: e.tensor_tensor(gp, gp, hs2, ALU.mult), r2, a2)
                r = dve(lambda e: e.scalar_tensor_tensor(ph, nu, C0, de, ALU.mult, ALU.mult), r, r1)
                r = dve(lambda e: e.tensor_tensor(gp, gp, ph, ALU.add), r, r2)
                pd = pe(mms(ps[0:64, 2, 0:64], [(drT[:, m, :], W2[:, m, :]) for m in range(2)]), dT, uW2)
                p5 = pe(seq(*[tr(ps[0:64, 5, 128 * m:128 * m + 128], drT[:, m, :]) for m in range(2)]))
                po = answer_second(t - 1, gq_, uW2T) if t else None
                dr_ = act(lambda e: e.copy(dr, ps[0:64, 5, 0:256]), p5)
                da_ = dve(lambda e: e.tensor_tensor(da, ps[0:64, 2, 0:64], gp, ALU.mult), pd, r)
                p1 = pe(seq(*[mms(ps[:, 4, 64 * k:64 * k + 64], [(z[:, t, 128 * k:128 * k + 128], da)]) for k in range(2)]), da_)
                pg = pe(seq(mms(ps[0:64, 3, 64:65], [(da, one[:, 0:1])]), mms(ps[0:1, 3, 128:192], [(one[:, 0:1], da)])))
                p6 = pe(mms(ps[0:64, 6, 0:256], [(hs, dr)]), hs_, dr_)
                g2 = dve(lambda e: e.tensor_reduce(gb2, drT, AX.X, ALU.add), dT)
                if t:
                    answer_add(t - 1, po, gq_, qb)
                ub2 = update(tb2, gb2, g2, qb)
                uW1 = update(W1T.rearrange("p a b -> p (a b)"), ps[:, 4, 0:128], p1)
                ub1 = update(tb1, ps[0:64, 3, 64:65], pg, gq_ if t else ah)
                ub1r = update(b1r, ps[0:1, 3, 128:192], pg)
                uW2T = update(W2T, ps[0:64, 6, 0:256], p6)
                if t + 1 < NB:
                    t2 = slice(64 * t + 64, 64 * t + 128)
                    eb_ = pool(lambda e, t2=t2: e.tensor_tensor(eb, eT[:, :, t2], tb2.unsqueeze(2).broadcast_to([128, 2, 64]), ALU.add), ub2)
                qb = pool(lambda e, t=t, tt=tt: e.tensor_tensor(
                    qb_[t % 2], qT[:, :, tt], tb2.unsqueeze(2).broadcast_to([128, 2, 64]), ALU.add), ub2)
            gq_ = answer_first(NB - 1, uW1, ub1)
            answer_add(NB - 1, answer_second(NB - 1, gq_, uW2T), gq_, qb)
            last = (eng_sems["dve"], eng_sems["dve"].n)
            xt = {}
            for t in range(NT):
                bank = t % 2
                p = pe(seq(*[tr(ps[:, bank, 128 * k:128 * k + 128], qT[:, k, 128 * t:128 * t + 128]) for k in range(2)]), last, xt.get(t - 2))
                xt[t] = dve(lambda e, t=t, bank=bank: e.tensor_tensor(x[:, t, :], ps[:, bank, 0:256], x[:, t, :], ALU.add), p)
                moments(t, xt[t])

        s_out = sem("out")
        stored = []

        def store_out(t0, t1, *w):
            stored.append(t1)
            return op("sp", lambda e: e.dma_start(out.rearrange("(t b) n c -> (b n) t c", b=2)[:, t0:t1, :], x[:, t0:t1, :]), *w, sem=s_out, inc=16)

        def moe(third_ctx):
            ends = fresh("mo")
            third_ctx.close()
            dn = sb("dn", [128, 8 * 1536])
            rest = sb("rest", [128, 6800])
            irest = sb("irest", [128, 64], mybir.dt.int32)
            for e in range(8):
                t_dn = load(dn[:, 1536 * e:1536 * e + 1536], d["m_dn"][e].rearrange("p a b -> p (a b)"), s_dn, *ends)
            t_gu, t_sh = (s_gu, s_gu.n), (s_w[1], s_w[1].n)
            ar = Carve(rest)
            xs = [ar(128, 256) for _ in range(3)]
            XT = [ar(128, 2, 128) for _ in range(2)]
            ar2 = Carve(rest, ar.off)
            sT, sgs = ar2(128, 2, 512), [ar2(128, 512) for _ in range(2)]
            a_, aT = [ar(128, 768) for _ in range(2)], [ar(128, 6, 128) for _ in range(2)]
            sg = [ar(128, 256) for _ in range(3)]
            yS = [ar(128, 256) for _ in range(2)]
            lg, pr, oh1, oh2, tmp, M, base, slot = [ar(128, NT, 8) for _ in range(8)]
            cnt, nt, start, end = [ar(128, 8) for _ in range(4)]
            pos = ar(128, 16)
            v1, v2, f_, g1, g2 = [ar(128, NT) for _ in range(5)]
            texp = ar(128, NS)
            cmp_ = ar(128, 512)
            ipos, itu, itd = irest[:, 0:16], irest[0:1, 16:16 + NS], irest[0:1, 40:40 + NS]
            mcc = Carve(mc)
            tri, ones, lt, k128, iota = mcc(128, 128), mcc(128, 128), mcc(128, 8, 8), mcc(128, 8), mcc(128, NS)

            toks = layernorm()
            t_h = to_hT(toks, scale=lng, shift=lnb)
            p = pe(seq(*[mms(ps[:, 6, 8 * t:8 * t + 8], [(hT[:, k, 128 * t:128 * t + 128], rw[:, k, :]) for k in range(2)])
                         for t in range(NT)]), t_h, t_sh)

            def b3(v):
                return v.unsqueeze(2).broadcast_to([128, NT, 8])

            sh_free, sh_read, y_free = {}, {}, {}

            def shared_gu(half, f):
                hh = [hT[:, k, 512 * half:512 * half + 512] for k in range(2)]
                return pe(seq(*[mms(ps[:, 2 * f + j, :], [(sgu[:, k, 128 * (f + 2 * j):128 * (f + 2 * j) + 128], hh[k]) for k in range(2)])
                                for j in range(2)]), t_h, t_sh, sh_free.get(f))

            def shared_act(half, f, p):
                s = act(lambda e: e.activation(sgs[f], ps[:, 2 * f, :], ACT.Silu), p, sh_free.get(f))
                sh_free[f] = dve(lambda e: e.tensor_tensor(sT[:, f, :], ps[:, 2 * f + 1, :], sgs[f], ALU.mult), s, sh_read.get(0))

            def shared_down(half):
                for t in range(4):
                    bank, tt = 4 + t % 2, 4 * half + t
                    p = pe(mms(ps[:, bank, 0:256], [(sT[:, f, 128 * t:128 * t + 128], sdn[:, f, :]) for f in range(2)]),
                           sh_free[0], sh_free[1], y_free.get(bank))
                    y_free[bank] = dve(lambda e, tt=tt, bank=bank: e.tensor_tensor(x[:, tt, :], ps[:, bank, 0:256], x[:, tt, :], ALU.add), p)
                sh_read[0] = p

            sh_p = [shared_gu(0, f) for f in range(2)]
            L = ps[:, 6, 0:64].rearrange("p (t e) -> p t e", e=8)
            a = dve(lambda e: e.tensor_reduce(v1, L, AX.X, ALU.max), p)
            a = dve(lambda e: e.tensor_tensor(lg, L, b3(v1), ALU.subtract), a)
            a = act(lambda e: e.activation(pr, lg, ACT.Exp), a)
            a = dve(lambda e: e.tensor_reduce(v1, pr, AX.X, ALU.add), a)
            a = dve(lambda e: e.reciprocal(v1, v1), a)
            a = dve(lambda e: e.tensor_tensor(pr, pr, b3(v1), ALU.mult), a)

            def top(oh, v, a):
                a = dve(lambda e: e.tensor_reduce(v, pr, AX.X, ALU.max), a)
                a = dve(lambda e: e.tensor_tensor(tmp, pr, b3(v), ALU.is_equal), a)
                a = dve(lambda e: e.tensor_tensor(tmp, tmp, eord.unsqueeze(1).broadcast_to([128, NT, 8]), ALU.mult), a, t_c)
                a = dve(lambda e: e.tensor_reduce(f_, tmp, AX.X, ALU.max), a)
                return dve(lambda e: e.tensor_tensor(oh, tmp, b3(f_), ALU.is_equal), a)

            a = top(oh1, v1, a)
            a = dve(lambda e: e.scalar_tensor_tensor(pr, oh1, -2.0, pr, ALU.mult, ALU.add), a)
            a = top(oh2, v2, a)
            tM = dve(lambda e: e.tensor_tensor(M, oh1, oh2, ALU.add), a)

            def flat(v):
                return v.rearrange("p a b -> p (a b)")

            p = pe(seq(mms(ps[:, 7, 0:64], [(tri, flat(M))]), mms(ps[:, 7, 64:128], [(ones, flat(M))])), tM, t_sh)
            R = ps[:, 7, 0:64].rearrange("p (t e) -> p t e", e=8)
            C = ps[:, 7, 64:128].rearrange("p (t e) -> p t e", e=8)
            c4 = cmp_.rearrange("p (t e u) -> p t e u", e=8, u=8)
            c3 = cmp_[:, 0:64].rearrange("p (a b) -> p a b", b=8)
            a = dve(lambda e: e.tensor_tensor(c4, ps[:, 7, 64:128].rearrange("p (u e) -> p e u", e=8).unsqueeze(1).broadcast_to([128, 8, 8, 8]),
                                              lt.unsqueeze(2).broadcast_to([128, 8, 8, 8]), ALU.mult), p)
            a = dve(lambda e: e.tensor_reduce(base, c4, AX.X, ALU.add), a)
            a = dve(lambda e: e.tensor_tensor(cnt, base[:, 7, :], C[:, 7, :], ALU.add), a)
            a = dve(lambda e: e.tensor_tensor(c3, cnt.unsqueeze(2).broadcast_to([128, 8, 8]),
                                              k128.unsqueeze(1).broadcast_to([128, 8, 8]), ALU.is_gt), a)
            a = dve(lambda e: e.tensor_reduce(nt, c3, AX.X, ALU.add), a)
            a = dve(lambda e: e.tensor_tensor(c3, nt.unsqueeze(1).broadcast_to([128, 8, 8]), lt, ALU.mult), a)
            a = dve(lambda e: e.tensor_reduce(start, c3, AX.X, ALU.add), a)
            s_ = dve(lambda e: e.scalar_tensor_tensor(slot, start.unsqueeze(1).broadcast_to([128, NT, 8]), 128.0, base, ALU.mult, ALU.add), a)
            s_ = dve(lambda e: e.tensor_tensor(slot, slot, R, ALU.add), s_)
            for i, oh in ((0, oh1), (8, oh2)):
                b = dve(lambda e, oh=oh: e.tensor_tensor(tmp, oh, slot, ALU.mult), s_)
                s_ = dve(lambda e, i=i: e.tensor_reduce(pos[:, i:i + 8], tmp, AX.X, ALU.add), b)
            t_pos = dve(lambda e: e.tensor_copy(ipos, pos), s_)
            a = dve(lambda e: e.tensor_tensor(end, start, nt, ALU.add), t_pos)
            ce = cmp_[:, 0:NS * 8].rearrange("p (i e) -> p i e", e=8)
            a = dve(lambda e: e.tensor_tensor(ce, iota.unsqueeze(2).broadcast_to([128, NS, 8]),
                                              end.unsqueeze(1).broadcast_to([128, NS, 8]), ALU.is_ge), a)
            a = dve(lambda e: e.tensor_reduce(texp, ce, AX.X, ALU.add), a)
            t_te = dve(lambda e: e.tensor_scalar(itu, texp[0:1, :], 7.0, 3072.0, ALU.min, ALU.mult), a)
            t_te = dve(lambda e: e.tensor_scalar(itd, texp[0:1, :], 7.0, 1536.0, ALU.min, ALU.mult), t_te)
            a = dve(lambda e: e.tensor_tensor(v2, v2, v1, ALU.subtract), t_te)
            a = act(lambda e: e.activation(g2, v2, ACT.Exp), a)
            a = dve(lambda e: e.tensor_scalar(g1, g2, 1.0, None, ALU.add), a)
            a = dve(lambda e: e.reciprocal(g1, g1), a)
            t_g = dve(lambda e: e.tensor_tensor(g2, g2, g1, ALU.mult), a)

            for k in range(2):
                for t in range(NT):
                    i = 8 * k + t
                    t_sc = op("pool", lambda e, i=i, t=t: e.indirect_dma_start(
                        xs_d, bass.IndirectOffsetOnAxis(ap=ipos[:, i:i + 1].bitcast(mybir.dt.uint32), axis=0), h[:, t, :], None),
                        t_pos, toks[-1], t_zero, sem=s_sc, inc=16)

            for f in range(2):
                shared_act(0, f, sh_p[f])
            shared_down(0)
            for f in range(2):
                shared_act(1, f, shared_gu(1, f))
            shared_down(1)

            bfree = {6: t_te, 7: t_te, 0: sh_free[0], 1: sh_free[0], 2: sh_free[1], 3: sh_free[1], 4: y_free[4], 5: y_free[5]}
            xs_t, xs_r, XTt, XTr, at, atr, aTt, yt, yd, dnr = {}, {}, {}, {}, {}, {}, {}, {}, {}, {}

            def load_block(i):
                xs_t[i] = load(xs[i % 3], xs_d[128 * i:128 * i + 128, :], s_xs[i % 3], t_sc, xs_r.get(i - 3))

            def turn_block(i):
                p = pe(seq(*[tr(ps[:, 6, 128 * k:128 * k + 128], xs[i % 3][:, 128 * k:128 * k + 128]) for k in range(2)]),
                       xs_t[i], bfree.get(6))
                xs_r[i] = p
                for k in range(2):
                    bfree[6] = XTt[i] = dve(lambda e, k=k: e.tensor_scalar(
                        XT[i % 2][:, k, :], ps[:, 6, 128 * k:128 * k + 128], lng[:, k:k + 1], lnb[:, k:k + 1], ALU.mult, ALU.add),
                        p, XTr.get(i - 2))

            def gate_up(i, c):
                def f(e):
                    if c == 0:
                        off[i, 0] = e.value_load(itu[:, i:i + 1], min_val=0, max_val=7 * 3072)
                    for k in range(2):
                        m = e.matmul(ps[:, c, :], XT[i % 2][:, k, :], gu[:, bass.ds(off[i, 0] + (1536 * k + 512 * c), 512)],
                                     start=(k == 0), stop=(k == 1))
                    return m
                p = pe(f, XTt[i], t_gu, t_te, bfree.get(c))
                XTr[i] = p
                s = act(lambda e: e.activation(sg[c], ps[:, c, 0:256], ACT.Silu), p, bfree.get(("sg", c)))
                bfree[c] = bfree["sg", c] = at[i, c] = dve(lambda e: e.tensor_tensor(
                    a_[i % 2][:, 256 * c:256 * c + 256], ps[:, c, 256:512], sg[c], ALU.mult), s, atr.get(i - 2, sh_read[0]))

            def turn_a(i):
                for n, c in ((4, 3), (2, 4)):
                    f0 = 0 if c == 3 else 4
                    p = pe(seq(*[tr(ps[:, c, 128 * f:128 * f + 128], a_[i % 2][:, 128 * (f0 + f):128 * (f0 + f) + 128]) for f in range(n)]),
                           at[i, 1 if c == 3 else 2], bfree.get(c))
                    o, s = aT[i % 2][:, f0:f0 + n, :].rearrange("p a b -> p (a b)"), ps[:, c, 0:128 * n]
                    bfree[c] = aTt[i, c] = act(lambda e, o=o, s=s: e.copy(o, s), p, dnr.get(i - 2))
                atr[i] = p

            def down(i):
                bank = (5, 7)[i % 2]

                def f(part):
                    def g(e):
                        if part == 0:
                            off[i, 1] = e.value_load(itd[:, i:i + 1], min_val=0, max_val=7 * 1536)
                        for f in range(4 * part, 4 + 2 * part):
                            m = e.matmul(ps[:, bank, 0:256], aT[i % 2][:, f, :], dn[:, bass.ds(off[i, 1] + 256 * f, 256)],
                                         start=(f == 0), stop=(f == 5))
                        return m
                    return g
                pe(f(0), aTt[i, 3], t_dn, bfree.get(bank))
                p = pe(f(1), aTt[i, 4])
                dnr[i] = p
                bfree[bank] = y = dve(lambda e: e.tensor_copy(yS[i % 2], ps[:, bank, 0:256]), p, yd.get(i - 2))
                yd[i] = load(ys_d[128 * i:128 * i + 128, :], yS[i % 2], s_ys[i % 2], y)

            off = {}
            for i in range(3):
                load_block(i)
            turn_block(0)
            for i in range(NS):
                if i + 1 < NS:
                    turn_block(i + 1)
                    if i + 3 < NS:
                        load_block(i + 3)
                gate_up(i, 0)
                gate_up(i, 1)
                if i:
                    turn_a(i - 1)
                gate_up(i, 2)
                if i:
                    down(i - 1)
            turn_a(NS - 1)
            down(NS - 1)
            yg = [gu[:, 256 * i:256 * i + 256] for i in range(16)]
            yt = {}
            for t in range(NT):
                for k in range(2):
                    i = 8 * k + t
                    yt[i] = op("pool", lambda e, i=i: e.indirect_dma_start(
                        yg[i], None, ys_d, bass.IndirectOffsetOnAxis(ap=ipos[:, i:i + 1].bitcast(mybir.dt.uint32), axis=0)),
                        yd[NS - 1], yd[NS - 2], XTr[NS - 1], sem=s_yg[t], inc=16)
            for t in range(NT):
                a = dve(lambda e, t=t: e.scalar_tensor_tensor(x[:, t, :], yg[t], g1[:, t:t + 1], x[:, t, :], ALU.mult, ALU.add),
                        yt[t], yt[8 + t], t_g, (eng_sems["dve"], eng_sems["dve"].n))
                a = dve(lambda e, t=t: e.scalar_tensor_tensor(x[:, t, :], yg[8 + t], g2[:, t:t + 1], x[:, t, :], ALU.mult, ALU.add), a)
                if t in (4, 6):
                    store_out(0 if t == 4 else 5, t + 1, a)

        if stages > 1 and first <= 2:
            s_cm = sem("cm")
            with ExitStack() as sa_ctx:
                selfattn(sa_ctx)
        wx = Carve(second_ctx.enter_context(nc.sbuf_tensor("wx", [128, 5184], F32)))
        X1 = dict(wq=wx(128, 2, 512), wk=wx(128, 4, 256), wv1=wx(128, 8, 128), wv2=wx(64, 8, 128), wo=wx(128, 4, 256))
        if first == 4:
            tw1 = load_x1()
        if stages > 2 and first <= 3:
            with ExitStack() as ff_ctx:
                tw1 = ffn(ff_ctx.enter_context(nc.sbuf_tensor("ffa", [128, 28672], F32R)),
                          ff_ctx.enter_context(nc.sbuf_tensor("ffg", [128, 1024], F32)))
        arena = second_ctx.enter_context(nc.sbuf_tensor("arena", [128, 2400], F32))
        arenaR = second_ctx.enter_context(nc.sbuf_tensor("arenaR", [128, 27080], F32R))
        if stages > 3 and first <= 4:
            ends = fresh("x1")
            t_b = load_bias(2, "x1_bo", *ends)
            xattn("x1", X1, 4, 2, mask1, tw1, t_b, ends)
        if stages > 4:
            ends5 = fresh("tt")
            second_ctx.close()
            gu = sb("gu", [128, 8 * 3072])
            cs = Carve(sb("cs", [128, 1880 + NS]))
            sgu, sdn, rw, mc = cs(128, 2, 512), cs(128, 2, 256), cs(128, 2, 8), cs(128, 328 + NS)
            third_ctx = ExitStack()
            ctx.callback(third_ctx.close)
            third = third_ctx.enter_context(nc.sbuf_tensor("third", [128, 14800], F32))
            s_gu, s_dn, s_sc = sem("gu"), sem("dn"), sem("sc")
            s_xs, s_ys, s_yg = [sem(f"xs{i}") for i in range(3)], [sem(f"ys{i}") for i in range(2)], [sem(f"yg{i}") for i in range(NT)]

            def load_moe():
                for dst, n in ((sgu, "m_sgu"), (sdn, "m_sdn"), (rw, "m_rw"), (mc, "mc")):
                    load(dst, d[n], s_w[1], *ends5)
                for e in range(8):
                    load(gu[:, 3072 * e:3072 * e + 3072], d["m_gu"][e].rearrange("p a b -> p (a b)"), s_gu, *ends5)

            if first <= 5:
                memory()
            else:
                load_moe()
        if stages > 5 and first <= 6:
            moe(third_ctx)
        ends = [(s, s.n) for s in eng_sems.values() if s.n]
        t_o = store_out(stored[-1] if stored else 0, NT, *ends)
        op("sp", None, t_o)

        block = ctx.enter_context(nc.Block())

        @block.tensor
        def _(e):
            Q.emit("pe", e)

        @block.vector
        def _(e):
            Q.emit("dve", e)

        @block.scalar
        def _(e):
            Q.emit("act", e)

        @block.gpsimd
        def _(e):
            Q.emit("pool", e)

        @block.sync
        def _(e):
            Q.emit("sp", e)


def layout(np, i):
    a = {k: np.asarray(v) for k, v in i.items()}
    C = np.ascontiguousarray
    r = {}
    r["x"] = a["x"]
    r["ctx"] = a["ctx_768"]
    r["ctxT"] = C(a["ctx_768"].transpose(0, 2, 1))
    f = np.float32
    r["ident"] = np.eye(128, dtype=f)
    p = np.arange(128)
    r["mask0"] = ((p[:, None] // 16 == np.arange(8)[None]) * 0.25).astype(f)
    r["mask1"] = ((p[:, None] // 64 == np.arange(2)[None]) * 0.125).astype(f)
    r["eord"] = np.tile(8.0 - np.arange(8), (128, 1)).astype(f)
    r["causal"] = ((p[:, None] // 64 == p[None] // 64) & (p[:, None] <= p[None])).astype(f)

    def col(v, n):
        return C(v.reshape(n, 128).T)

    def rows(w, n):
        return C(w.reshape(n, 128, w.shape[1]).transpose(1, 0, 2))

    r["bq"] = col(a["L0_xattn_bq"], 2)
    r["bvc"] = col(a["L0_xattn_bv"], 2)
    r["normw"] = col(a["L0_attn_norm_w"], 2)
    qheads = [4 * i + 2 * k + j for i in range(4) for j in range(2) for k in range(2)]
    kheads = [q // 2 for q in qheads]
    r["qg"] = col(a["L0_attn_q_gamma"][qheads].reshape(-1), 8)
    r["kg"] = col(a["L0_attn_k_gamma"][kheads].reshape(-1), 8)
    r["b1c"] = col(a["L0_ffn_b1"], 8)
    r["tb1"] = C(a["L1_attn_b1"].reshape(64, 1))
    r["tb2"] = col(a["L1_attn_b2"], 2)
    r["lng"] = col(a["L1_ffn_ln_gamma"], 2)
    r["lnb"] = col(a["L1_ffn_ln_beta"], 2)
    r["x0_bo"], r["f_b2"], r["x1_bo"] = a["L0_xattn_bo"], a["L0_ffn_b2"], a["L1_xattn_bo"]
    r["x0_wq"] = rows(a["L0_xattn_wq"], 2)
    def twice(w):
        return np.concatenate([w[:, :128], w[:, 128:], w[:, 128:]], 1)

    r["fold"] = (p[:, None] % 64 == np.arange(64)[None]).astype(f)
    r["own"] = (p[:, None] // 64 == np.arange(32)[None] // 16).astype(f)
    r["bkc"] = col(a["L0_xattn_bk"], 2)
    for k in ("wk", "wv"):
        r["x0_" + k] = C(twice(a["L0_xattn_" + k].T).reshape(256, 2, 128).transpose(2, 1, 0))

    def place(wv, H, dh, hpg):
        o = np.zeros((wv.shape[0], H, 128), f)
        for hh in range(H):
            o[:, hh, dh * (hh % hpg):dh * (hh % hpg) + dh] = wv[:, hh * dh:(hh + 1) * dh]
        return o

    r["x0_wo"] = rows(a["L0_xattn_wo"], 2)
    r["a_wq"], r["a_wkv"], r["a_wout"] = rows(a["L0_attn_Wq"].reshape(256, 16, 64)[:, qheads].reshape(256, 1024), 2), rows(a["L0_attn_Wkv"], 2), rows(a["L0_attn_Wout"], 4)
    r["f_w1"], r["f_w2"] = rows(a["L0_ffn_w1"], 2), rows(a["L0_ffn_w2"], 8)
    r["x1_wq"] = rows(a["L1_xattn_Wq"], 2)
    r["x1_wk"] = rows(twice(a["L1_xattn_Wk"].T), 4)
    wv = place(a["L1_xattn_Wv"], 8, 64, 2)
    r["x1_wv1"], r["x1_wv2"] = C(wv[:128]), C(wv[128:])
    r["x1_wo"] = rows(a["L1_xattn_Wo"], 4)
    for k in "kvq":
        r["t_" + k] = rows(C(a["L1_attn_t_" + k].T), 2)
    r["t_W1T"] = rows(C(a["L1_attn_W1"].T), 2)
    r["t_W2T"] = C(a["L1_attn_W2"].T)
    r["t_W2"] = rows(a["L1_attn_W2"], 2)
    r["m_rw"] = rows(C(a["L1_ffn_router_w"].T), 2)
    g = a["L1_ffn_gate_up_w"].transpose(0, 2, 1).reshape(8, 2, 128, 2, 3, 256)
    r["m_gu"] = C(g.transpose(0, 2, 1, 4, 3, 5).reshape(8, 128, 2, 1536))
    e = np.arange(8)
    lt = (e[None] < e[:, None]).reshape(1, 64)
    rows_ = [p[:, None] < p[None], np.ones((128, 128)), lt.repeat(128, 0), np.tile(128 * e, (128, 1)), np.tile(np.arange(NS), (128, 1))]
    r["mc"] = C(np.concatenate(rows_, 1).astype(f))
    r["m_dn"] = C(a["L1_ffn_down_w"].transpose(0, 2, 1).reshape(8, 6, 128, 256).transpose(0, 2, 1, 3))
    r["m_sgu"] = rows(C(a["L1_ffn_shared_gate_up_w"].T), 2)
    r["m_sdn"] = rows(C(a["L1_ffn_shared_down_w"].T), 2)
    r["tb1"] = np.concatenate([r["tb1"]] * 2, 0)
    names = ("mask0", "mask1", "fold", "own", "bq", "bkc", "bvc", "eord", "normw", "qg", "kg", "b1c", "tb1", "tb2", "lng", "lnb")
    r["small"] = C(np.concatenate([r.pop(n) for n in names], 1))
    return r


def kernel(**inputs):
    import numpy as np
    import concourse.bacc as bacc
    from concourse.bass_utils import run_bass_kernel_spmd

    nc = bacc.Bacc("TRN2", target_bir_lowering=False, num_devices=1)
    arrays = layout(np, inputs)
    d = {n: nc.dram_tensor("in_" + n, v.shape, mybir.dt.from_np(v.dtype), kind="ExternalInput").ap() for n, v in arrays.items()}
    out = nc.dram_tensor("out_x", (16, 64, 256), F32, kind="ExternalOutput").ap()
    program(nc, d, out)
    r = run_bass_kernel_spmd(nc, [{"in_" + n: v for n, v in arrays.items()}], core_ids=[0])
    return r.results[0]["out_x"]
```
